# Optimizing a Trainium2 kernel written in Bass

```python
import numpy as np
import jax
import jax.numpy as jnp

def _softmax(x, axis=-1):
    return jax.nn.softmax(x, axis=axis)

def _gelu(x):
    return jax.nn.gelu(x, approximate=True)

def _silu(x):
    return jax.nn.silu(x)

def _sigmoid(x):
    return jax.nn.sigmoid(x)

def _layernorm(x, axis=-1, eps=1e-05):
    m = jnp.mean(x, axis=axis, keepdims=True)
    v = jnp.var(x, axis=axis, keepdims=True)
    return (x - m) / jnp.sqrt(v + eps)

def _scatter_add(tgt, idx, src, axis=0):
    return tgt.at[idx].add(src)

def _segment_sum(src, seg, n):
    return jax.ops.segment_sum(src, seg, n)
kernel_name = 'mk_seq_preln_d2_jaxref_r8_64d589'

def setup_inputs(seed: int=0):
    np.random.seed(seed)
    _w = jnp.asarray

    def _L0_attn_setup():
        import jax, jax.numpy as jnp
        import numpy as np
        D_MODEL = 128
        NUM_HEADS = 16
        DK = D_MODEL // NUM_HEADS
        key = jax.random.key(seed)
        kx, kq, kk, kv, ko = jax.random.split(key, 5)
        B, S = (4, 256)
        bound = float(np.sqrt(6.0 / (D_MODEL + D_MODEL)))
        uni = lambda k: jax.random.uniform(k, (D_MODEL, D_MODEL), jnp.float32, -bound, bound)
        return {'x': jax.random.normal(kx, (B, S, D_MODEL), jnp.float32), 'q_heads': uni(kq), 'k_heads': uni(kk), 'v_heads': uni(kv), 'output_proj': uni(ko)}
    _L0_attn_in = _L0_attn_setup()

    def _L0_ffn_setup():
        import jax, jax.numpy as jnp
        import numpy as np
        import math
        N_EMBD = 128
        HIDDEN = 4 * N_EMBD
        N_EXPERTS = 8
        TOP_K = 2
        B, T = (4, 256)

        def new_gelu(x):
            c = math.sqrt(2.0 / math.pi)
            return 0.5 * x * (1.0 + jnp.tanh(c * (x + 0.044715 * x * x * x)))

        def _moe_forward(x, Wfc_s, bfc_s, Wproj_s, bproj_s, Wr, Wfc, bfc, Wproj, bproj):
            Bb, Tt, C = x.shape
            xf = x.reshape(Bb * Tt, C)
            N = Bb * Tt
            shared = new_gelu(xf @ Wfc_s + bfc_s) @ Wproj_s + bproj_s
            logits = xf @ Wr
            probs = jax.nn.softmax(logits, axis=-1)
            topk_p, topk_i = jax.lax.top_k(probs, TOP_K)
            topk_p = topk_p / jnp.sum(topk_p, axis=-1, keepdims=True)
            gate = jnp.zeros((N, N_EXPERTS), dtype=xf.dtype)
            gate = gate.at[jnp.arange(N)[:, None], topk_i].add(topk_p)
            routed = jnp.zeros_like(xf)
            for e in range(N_EXPERTS):
                h = new_gelu(xf @ Wfc[e] + bfc[e]) @ Wproj[e] + bproj[e]
                routed = routed + h * gate[:, e:e + 1]
            return (shared + routed).reshape(Bb, Tt, C)
        key = jax.random.key(seed)
        ks = jax.random.split(key, 10)
        s = 0.02
        return {'x': jax.random.normal(ks[0], (B, T, N_EMBD), dtype=jnp.float32), 'Wfc_s': jax.random.normal(ks[1], (N_EMBD, HIDDEN), dtype=jnp.float32) * s, 'bfc_s': jnp.zeros((HIDDEN,), dtype=jnp.float32), 'Wproj_s': jax.random.normal(ks[2], (HIDDEN, N_EMBD), dtype=jnp.float32) * s, 'bproj_s': jnp.zeros((N_EMBD,), dtype=jnp.float32), 'Wr': jax.random.normal(ks[3], (N_EMBD, N_EXPERTS), dtype=jnp.float32) * s, 'Wfc': jax.random.normal(ks[4], (N_EXPERTS, N_EMBD, HIDDEN), dtype=jnp.float32) * s, 'bfc': jnp.zeros((N_EXPERTS, HIDDEN), dtype=jnp.float32), 'Wproj': jax.random.normal(ks[5], (N_EXPERTS, HIDDEN, N_EMBD), dtype=jnp.float32) * s, 'bproj': jnp.zeros((N_EXPERTS, N_EMBD), dtype=jnp.float32)}
    _L0_ffn_in = _L0_ffn_setup()

    def _L1_attn_setup():
        import jax, jax.numpy as jnp
        import numpy as np
        B, L, D = (2, 256, 128)
        H, HD = (16, 64)
        LD = 32
        key = jax.random.key(seed)
        ks = jax.random.split(key, 6)
        s = lambda fan_in: 1.0 / np.sqrt(fan_in)
        x_bld = jax.random.normal(ks[0], (B, L, D), dtype=jnp.float32)
        Wq = jax.random.normal(ks[1], (D, H, HD), dtype=jnp.float32) * s(D)
        Wkv_down = jax.random.normal(ks[2], (D, LD), dtype=jnp.float32) * s(D)
        Wk_up = jax.random.normal(ks[3], (LD, H, HD), dtype=jnp.float32) * s(LD)
        Wv_up = jax.random.normal(ks[4], (LD, H, HD), dtype=jnp.float32) * s(LD)
        Wout = jax.random.normal(ks[5], (H, HD, D), dtype=jnp.float32) * s(H * HD)
        return {'x_bld': x_bld, 'Wq': Wq, 'Wkv_down': Wkv_down, 'Wk_up': Wk_up, 'Wv_up': Wv_up, 'Wout': Wout}
    _L1_attn_in = _L1_attn_setup()

    def _L1_ffn_setup():
        import jax, jax.numpy as jnp
        import numpy as np
        B, S, D = (2, 64, 128)
        E, K, I = (16, 8, 128)
        I_SH = 128
        ROUTE_SCALE = 2.826
        key = jax.random.key(seed)
        ks = jax.random.split(key, 8)
        s = 0.02
        return {'x': jax.random.normal(ks[0], (B, S, D), dtype=jnp.float32), 'gate_w': jax.random.normal(ks[1], (E, D), dtype=jnp.float32) * s, 'expert_bias': jnp.zeros((E,), dtype=jnp.float32), 'w_gate': jax.random.normal(ks[2], (E, I, D), dtype=jnp.float32) * s, 'w_up': jax.random.normal(ks[3], (E, I, D), dtype=jnp.float32) * s, 'w_down': jax.random.normal(ks[4], (E, D, I), dtype=jnp.float32) * s, 'shared_gate_w': jax.random.normal(ks[5], (I_SH, D), dtype=jnp.float32) * s, 'shared_up_w': jax.random.normal(ks[6], (I_SH, D), dtype=jnp.float32) * s, 'shared_down_w': jax.random.normal(ks[7], (D, I_SH), dtype=jnp.float32) * s}
    _L1_ffn_in = _L1_ffn_setup()
    _d = {'L0_attn_x': _L0_attn_in['x'], 'L0_attn_q_heads': _L0_attn_in['q_heads'], 'L0_attn_k_heads': _L0_attn_in['k_heads'], 'L0_attn_v_heads': _L0_attn_in['v_heads'], 'L0_attn_output_proj': _L0_attn_in['output_proj'], 'L0_ffn_Wfc_s': _L0_ffn_in['Wfc_s'], 'L0_ffn_bfc_s': _L0_ffn_in['bfc_s'], 'L0_ffn_Wproj_s': _L0_ffn_in['Wproj_s'], 'L0_ffn_bproj_s': _L0_ffn_in['bproj_s'], 'L0_ffn_Wr': _L0_ffn_in['Wr'], 'L0_ffn_Wfc': _L0_ffn_in['Wfc'], 'L0_ffn_bfc': _L0_ffn_in['bfc'], 'L0_ffn_Wproj': _L0_ffn_in['Wproj'], 'L0_ffn_bproj': _L0_ffn_in['bproj'], 'L1_attn_Wq': _L1_attn_in['Wq'], 'L1_attn_Wkv_down': _L1_attn_in['Wkv_down'], 'L1_attn_Wk_up': _L1_attn_in['Wk_up'], 'L1_attn_Wv_up': _L1_attn_in['Wv_up'], 'L1_attn_Wout': _L1_attn_in['Wout'], 'L1_ffn_gate_w': _L1_ffn_in['gate_w'], 'L1_ffn_expert_bias': _L1_ffn_in['expert_bias'], 'L1_ffn_w_gate': _L1_ffn_in['w_gate'], 'L1_ffn_w_up': _L1_ffn_in['w_up'], 'L1_ffn_w_down': _L1_ffn_in['w_down'], 'L1_ffn_shared_gate_w': _L1_ffn_in['shared_gate_w'], 'L1_ffn_shared_up_w': _L1_ffn_in['shared_up_w'], 'L1_ffn_shared_down_w': _L1_ffn_in['shared_down_w']}
    _x0 = _d['L0_attn_x']
    _d['L0_attn_x'] = jax.random.normal(jax.random.fold_in(jax.random.key(seed), 1), (4, 1024, 128), dtype=_x0.dtype)
    del _x0
    return _d

def reference(L0_attn_x, L0_attn_q_heads, L0_attn_k_heads, L0_attn_v_heads, L0_attn_output_proj, L0_ffn_Wfc_s, L0_ffn_bfc_s, L0_ffn_Wproj_s, L0_ffn_bproj_s, L0_ffn_Wr, L0_ffn_Wfc, L0_ffn_bfc, L0_ffn_Wproj, L0_ffn_bproj, L1_attn_Wq, L1_attn_Wkv_down, L1_attn_Wk_up, L1_attn_Wv_up, L1_attn_Wout, L1_ffn_gate_w, L1_ffn_expert_bias, L1_ffn_w_gate, L1_ffn_w_up, L1_ffn_w_down, L1_ffn_shared_gate_w, L1_ffn_shared_up_w, L1_ffn_shared_down_w):

    def _L0_attn_ref(x, q_heads, k_heads, v_heads, output_proj):
        import jax, jax.numpy as jnp
        import numpy as np
        D_MODEL = 128
        NUM_HEADS = 16
        DK = D_MODEL // NUM_HEADS
        B, S, _ = x.shape

        def proj(W):
            return (x @ W.T).reshape(B, S, NUM_HEADS, DK).transpose(0, 2, 1, 3)
        q, k, v = (proj(q_heads), proj(k_heads), proj(v_heads))
        scale = 1.0 / jnp.sqrt(jnp.asarray(DK, x.dtype))
        scores = jnp.einsum('bhqd,bhkd->bhqk', q, k) * scale
        causal = jnp.triu(jnp.ones((S, S), bool), k=1)
        scores = jnp.where(causal, jnp.asarray(-jnp.inf, scores.dtype), scores)
        attn = jax.nn.softmax(scores, axis=-1)
        out = jnp.einsum('bhqk,bhkd->bhqd', attn, v)
        out = out.transpose(0, 2, 1, 3).reshape(B, S, D_MODEL)
        return out @ output_proj.T

    def _L0_ffn_ref(x, Wfc_s, bfc_s, Wproj_s, bproj_s, Wr, Wfc, bfc, Wproj, bproj):
        import jax, jax.numpy as jnp
        import numpy as np
        import math
        N_EMBD = 128
        HIDDEN = 4 * N_EMBD
        N_EXPERTS = 8
        TOP_K = 2
        B, T = (4, 256)

        def new_gelu(x):
            c = math.sqrt(2.0 / math.pi)
            return 0.5 * x * (1.0 + jnp.tanh(c * (x + 0.044715 * x * x * x)))

        def _moe_forward(x, Wfc_s, bfc_s, Wproj_s, bproj_s, Wr, Wfc, bfc, Wproj, bproj):
            Bb, Tt, C = x.shape
            xf = x.reshape(Bb * Tt, C)
            N = Bb * Tt
            shared = new_gelu(xf @ Wfc_s + bfc_s) @ Wproj_s + bproj_s
            logits = xf @ Wr
            probs = jax.nn.softmax(logits, axis=-1)
            topk_p, topk_i = jax.lax.top_k(probs, TOP_K)
            topk_p = topk_p / jnp.sum(topk_p, axis=-1, keepdims=True)
            gate = jnp.zeros((N, N_EXPERTS), dtype=xf.dtype)
            gate = gate.at[jnp.arange(N)[:, None], topk_i].add(topk_p)
            routed = jnp.zeros_like(xf)
            for e in range(N_EXPERTS):
                h = new_gelu(xf @ Wfc[e] + bfc[e]) @ Wproj[e] + bproj[e]
                routed = routed + h * gate[:, e:e + 1]
            return (shared + routed).reshape(Bb, Tt, C)
        return _moe_forward(x, Wfc_s, bfc_s, Wproj_s, bproj_s, Wr, Wfc, bfc, Wproj, bproj)

    def _L1_attn_ref(x_bld, Wq, Wkv_down, Wk_up, Wv_up, Wout):
        import jax, jax.numpy as jnp
        import numpy as np
        B, L, D = (2, 256, 128)
        H, HD = (16, 64)
        LD = 32
        q_blhd = jnp.einsum('bld,dhk->blhk', x_bld, Wq)
        latent_bll = jnp.einsum('bld,dc->blc', x_bld, Wkv_down)
        k_blhd = jnp.einsum('blc,chk->blhk', latent_bll, Wk_up)
        v_blhd = jnp.einsum('blc,chk->blhk', latent_bll, Wv_up)
        attn = jnp.einsum('bqhd,bkhd->bhqk', q_blhd, k_blhd) / jnp.sqrt(jnp.asarray(HD, dtype=x_bld.dtype))
        l = x_bld.shape[1]
        mask = (jnp.arange(l)[None, :] <= jnp.arange(l)[:, None])[None, None]
        neg_inf = jnp.finfo(attn.dtype).min
        attn = jax.nn.softmax(jnp.where(mask, attn, neg_inf), axis=-1)
        y_blhd = jnp.einsum('bhqk,bkhd->bqhd', attn, v_blhd)
        return jnp.einsum('bqhd,hdo->bqo', y_blhd, Wout)

    def _L1_ffn_ref(x, gate_w, expert_bias, w_gate, w_up, w_down, shared_gate_w, shared_up_w, shared_down_w):
        import jax, jax.numpy as jnp
        import numpy as np
        B, S, D = (2, 64, 128)
        E, K, I = (16, 8, 128)
        I_SH = 128
        ROUTE_SCALE = 2.826
        gates = jnp.einsum('bsd,ed->bse', x, gate_w)
        scores = jax.nn.sigmoid(gates.astype(jnp.float32))
        sel_scores = scores + expert_bias
        _, inds = jax.lax.top_k(sel_scores, K)
        selected = jnp.take_along_axis(scores, inds, axis=-1)
        selected = selected / selected.sum(axis=-1, keepdims=True)
        selected = selected * ROUTE_SCALE
        onehot = jax.nn.one_hot(inds, E, dtype=selected.dtype)
        combine = jnp.einsum('bske,bsk->bse', onehot, selected)
        hg = jnp.einsum('bsd,eid->bsei', x, w_gate)
        hu = jnp.einsum('bsd,eid->bsei', x, w_up)
        h = jax.nn.silu(hg) * hu
        ye = jnp.einsum('bsei,edi->bsed', h, w_down)
        y = jnp.einsum('bsed,bse->bsd', ye, combine).astype(x.dtype)
        g = jnp.einsum('bsd,id->bsi', x, shared_gate_w)
        u = jnp.einsum('bsd,id->bsi', x, shared_up_w)
        y = y + jnp.einsum('bsi,di->bsd', jax.nn.silu(g) * u, shared_down_w)
        return y
    x = L0_attn_x
    x = x + _L0_attn_ref(_layernorm(x, axis=-1), L0_attn_q_heads, L0_attn_k_heads, L0_attn_v_heads, L0_attn_output_proj)
    x = x + _L0_ffn_ref(_layernorm(x, axis=-1), L0_ffn_Wfc_s, L0_ffn_bfc_s, L0_ffn_Wproj_s, L0_ffn_bproj_s, L0_ffn_Wr, L0_ffn_Wfc, L0_ffn_bfc, L0_ffn_Wproj, L0_ffn_bproj)
    x = x + _L1_attn_ref(_layernorm(x, axis=-1), L1_attn_Wq, L1_attn_Wkv_down, L1_attn_Wk_up, L1_attn_Wv_up, L1_attn_Wout)
    x = x + _L1_ffn_ref(_layernorm(x, axis=-1), L1_ffn_gate_w, L1_ffn_expert_bias, L1_ffn_w_gate, L1_ffn_w_up, L1_ffn_w_down, L1_ffn_shared_gate_w, L1_ffn_shared_up_w, L1_ffn_shared_down_w)
    return x

_drawn_inputs = setup_inputs


def setup_inputs(seed=0):
    import zlib

    import numpy as np

    out = dict(_drawn_inputs(seed))
    spreads = {'L0_ffn_bfc_s': (0.0, 0.1),
     'L0_ffn_bproj_s': (0.0, 0.1),
     'L0_ffn_bfc': (0.0, 0.455),
     'L0_ffn_bproj': (0.0, 0.1),
     'L1_ffn_expert_bias': (0.0, 0.8)}
    factors = {'L1_ffn_gate_w': 8.0,
     'L1_ffn_w_gate': 8.0,
     'L1_ffn_w_up': 8.0,
     'L1_ffn_w_down': 8.0,
     'L1_ffn_shared_gate_w': 8.0,
     'L1_ffn_shared_up_w': 8.0,
     'L1_ffn_shared_down_w': 8.0}
    for name, (base, spread) in spreads.items():
        noise = np.random.default_rng([zlib.crc32(name.encode()), seed]).standard_normal(out[name].shape)
        drawn = base * np.exp(spread * noise) if base else spread * noise
        out[name] = jnp.asarray(drawn.astype(out[name].dtype))
    for name, factor in factors.items():
        out[name] = (out[name] * factor).astype(out[name].dtype)
    return out
```

```python
from contextlib import ExitStack

import concourse.bass as bass
from concourse import mybir

F32 = mybir.dt.float32
F32R = mybir.dt.float32r
BF16 = mybir.dt.bfloat16
ALU = mybir.AluOpType
ACT = mybir.ActivationFunctionType
AXX = mybir.AxisListType.X

P = 128
D = 128
BATCH, SEQ = 4, 1024
TOK = BATCH * SEQ
TILES = TOK // P
ST = 512
NST = TOK // ST
TPS = ST // P
TPB = SEQ // P
HEADS = 16
EPS = 1e-5
MASKED = -1e30

ROUTE_SCALE = 2.826


def lin(g, a, c):
    u, par = g
    return u * (2 * a) + (par * a + c)


def rounds(eng, n):
    yield 0
    with eng.Fori(1, n) as u:
        yield u


def wait_past(eng, sem, value):
    if not isinstance(value, int) or value > 0:
        eng.wait_ge(sem, value)


class Shared:

    def __init__(self, nc, ctx):
        self.nc, self.ctx = nc, ctx
        sb = lambda n, s, d: ctx.enter_context(nc.sbuf_tensor(n, s, d))
        self.ident, self.ident_bf = sb("ident", [P, P], F32), sb("ident_bf", [P, P], BF16)
        self.mask_q, self.mask_k = sb("mask_q", [P, P], BF16), sb("mask_k", [P, P], BF16)
        self.x = sb("x", [P, TILES, D], F32)
        self.stats = sb("stats", [P, TILES, 6], F32)
        self.mean, self.rstd, self.tmp = (sb(n, [P, TILES], F32) for n in ("mean", "rstd", "dev"))

    def sem(self, name):
        return self.ctx.enter_context(self.nc.semaphore(name))


def causal_pieces():
    full, partial = [], []
    for j in range(TPB):
        for half in range(SEQ // ST):
            q0, q1 = max(j * P, half * ST), (half + 1) * ST
            if q0 < q1:
                (full if q1 - q0 == ST else partial).append((j, q0, q1))
    pieces = [[seg] for seg in full]
    while partial:
        seg = partial.pop(0)
        mate = next(s for s in partial if s[2] - s[1] + seg[2] - seg[1] == ST)
        partial.remove(mate)
        pieces.append([seg, mate])
    return pieces


PIECES = causal_pieces()
NP = len(PIECES)


def ln_stats(k, name, load=None):
    nc, sem = k.nc, k.sem
    stats_done, combined, std_ready = sem(name + "_stats"), sem(name + "_comb"), sem(name + "_std")
    x_loaded = sem(name + "_xld")
    st = k.stats
    with nc.Block() as block:
        if load is not None:
            @block.sync
            def _(sp):
                load(sp, x_loaded)

        @block.vector
        def _(dve):
            if load is not None:
                dve.wait_ge(x_loaded, 16 * 2)
            with dve.Fori(0, TILES // 4) as u:
                for t in range(4):
                    last = nc.vector.bn_stats(st[:, bass.ds(u * 4 + t, 1), :].rearrange("p o s -> p (o s)"),
                                              k.x[:, bass.ds(u * 4 + t, 1), :].rearrange("p o d -> p (o d)"))
                    last.then_inc(stats_done, 1)
            dve.wait_ge(stats_done, TILES)
            n = [0]

            def link(ins):
                n[0] += 1
                ins.then_inc(combined, 1)
                dve.wait_ge(combined, n[0])

            mean_e, m2_e, mean_o, m2_o = (st[:, :, i] for i in (1, 2, 4, 5))
            nc.vector.tensor_tensor(k.mean[:, :], mean_e, mean_o, ALU.add).then_inc(combined, 1)
            nc.vector.tensor_tensor(k.tmp[:, :], mean_e, mean_o, ALU.subtract).then_inc(combined, 1)
            nc.vector.tensor_tensor(k.rstd[:, :], m2_e, m2_o, ALU.add).then_inc(combined, 1)
            n[0] = 3
            dve.wait_ge(combined, 3)
            nc.vector.tensor_scalar(k.mean[:, :], k.mean[:, :], 0.5, None, ALU.mult).then_inc(combined, 1)
            n[0] = 4
            link(nc.vector.tensor_tensor(k.tmp[:, :], k.tmp[:, :], k.tmp[:, :], ALU.mult))
            link(nc.vector.scalar_tensor_tensor(k.rstd[:, :], k.tmp[:, :], D / 4.0, k.rstd[:, :], ALU.mult, ALU.add))
            link(nc.vector.tensor_scalar(k.rstd[:, :], k.rstd[:, :], 1.0 / D, EPS, ALU.mult, ALU.add))
            dve.wait_ge(std_ready, 1)
            link(nc.vector.reciprocal(k.rstd[:, :], k.rstd[:, :]))

        @block.scalar
        def _(act):
            act.wait_ge(combined, 7)
            nc.scalar.activation(k.rstd[:, :], k.rstd[:, :], ACT.Sqrt).then_inc(std_ready, 1)


def normalise(k, dve, xn, g, ready):
    for t in range(TPS):
        tile = lin(g, TPS, t)
        last = nc_ts(k, xn[:, t, :], tile)
    last.then_inc(ready, 1)


def nc_ts(k, out, tile):
    one = bass.ds(tile, 1)
    return k.nc.vector.tensor_scalar(out, k.x[:, one, :].rearrange("p o d -> p (o d)"), k.mean[:, one], k.rstd[:, one],
                                     ALU.subtract, ALU.mult)


def project_0(k, w_q, w_k, w_v, scr_q, scr_k, scr_v):
    nc, sem = k.nc, k.sem
    VW = 9
    with ExitStack() as c:
        sb = lambda n, s, d: c.enter_context(nc.sbuf_tensor(n, s, d))
        pb = lambda n: c.enter_context(nc.psum_tensor(n, [P, ST], F32))
        wq, wk, wv = sb("p0_wq", [P, D], F32), sb("p0_wk", [P, D], F32), sb("p0_wv", [P, D], F32)
        xn = [sb(f"p0_xn{i}", [P, TPS, D], F32) for i in range(2)]
        xnT = [sb(f"p0_xnT{i}", [P, ST], F32) for i in range(2)]
        hi = [[sb(f"p0_hi{i}{n}", [P, ST], F32R) for n in "qk"] for i in range(2)]
        lo = [[sb(f"p0_lo{i}{n}", [P, ST], F32R) for n in "qk"] for i in range(2)]
        v1 = [sb(f"p0_v{i}", [P, TPS, HEADS, VW], F32) for i in range(2)]
        xT_ps = [pb(f"p0_xT{i}") for i in range(2)]
        qk_ps = [[pb(f"p0_ps{i}{n}") for n in "qk"] for i in range(2)]
        v_ps = [pb(f"p0_psv{i}") for i in range(2)]
        loaded, ones, xn_ready, xT_done, xnT_ready = (sem("p0_" + n) for n in ("ld", "ones", "xn", "xT", "xnT"))
        q_done, k_done, v_done, hi_ready, lo_ready, v_ready = (sem("p0_" + n) for n in ("q", "k", "v", "hi", "lo", "vr"))
        stored = [sem(f"p0_st{i}") for i in range(2)]
        NSTORE = 8
        with nc.Block() as block:
            @block.sync
            def _(sp):
                for dst, src in ((wq, w_q), (wk, w_k), (wv, w_v)):
                    sp.dma_start(dst[:, :], src).then_inc(loaded, 16)
                for u in rounds(sp, NST // 2):
                    for par in range(2):
                        g = (u, par)
                        cols = slice(par * ST, (par + 1) * ST)
                        for n, scr in enumerate((scr_q, scr_k)):
                            sp.wait_ge(hi_ready, lin(g, 2, n + 1))
                            sp.wait_ge(lo_ready, lin(g, 2, n + 1))
                            for part, tile in ((0, hi[par][n]), (1, lo[par][n])):
                                sp.dma_start(scr[part, bass.ds(u, 1), :, cols].rearrange("b c n -> (b c) n"),
                                             tile[:, :].bitcast(F32)).then_inc(stored[par], 16)
                        sp.wait_ge(v_ready, lin(g, 1, 1))
                        for hg in range(4):
                            sp.dma_start(scr_v[bass.ds(u, 1), hg, :, par * TPS:(par + 1) * TPS, :]
                                         .rearrange("b p t c -> (b p) t c"),
                                         v1[par][:, :, hg * 4:hg * 4 + 4, :].rearrange("p t h c -> p t (h c)"))\
                                .then_inc(stored[par], 16)
                for par in range(2):
                    sp.wait_ge(stored[par], 16 * NSTORE * (NST // 2))

            @block.gpsimd
            def _(pool):
                for i in range(2):
                    nc.gpsimd.memset(v1[i][:, :, :, :], 1.0).then_inc(ones, 1)

            @block.vector
            def _(dve):
                for u in rounds(dve, NST // 2):
                    for par in range(2):
                        g = (u, par)
                        wait_past(dve, xT_done, u * 2)
                        normalise(k, dve, xn[par], g, xn_ready)
                        wait_past(dve, stored[par], 16 * NSTORE * u)
                        for n in range(2):
                            dve.wait_ge(hi_ready, lin(g, 2, n + 1))
                            nc.vector.tensor_tensor(lo[par][n][:, :], qk_ps[par][n][:, :], hi[par][n][:, :].bitcast(F32),
                                                    ALU.subtract).then_inc(lo_ready, 1)

            @block.scalar
            def _(act):
                act.wait_ge(ones, 2)
                for u in rounds(act, NST // 2):
                    for par in range(2):
                        g = (u, par)
                        act.wait_ge(xT_done, lin(g, 1, 1))
                        nc.scalar.copy(xnT[par][:, :], xT_ps[par][:, :]).then_inc(xnT_ready, 1)
                        wait_past(act, stored[par], 16 * NSTORE * u)
                        for n, done in enumerate((q_done, k_done)):
                            act.wait_ge(done, lin(g, 1, 1))
                            nc.scalar.copy(hi[par][n][:, :], qk_ps[par][n][:, :]).then_inc(hi_ready, 1)
                        act.wait_ge(v_done, lin(g, 1, 1))
                        nc.scalar.copy(v1[par][:, :, :, 0:VW - 1],
                                       v_ps[par][:, :].rearrange("p (t h c) -> p t h c", t=TPS, h=HEADS)).then_inc(v_ready, 1)

            @block.tensor
            def _(pe):
                pe.wait_ge(loaded, 48)
                for u in rounds(pe, NST // 2):
                    for par in range(2):
                        g = (u, par)
                        pe.wait_ge(xn_ready, lin(g, 1, 1))
                        for t in range(TPS):
                            last = nc.tensor.transpose(xT_ps[par][:, t * P:(t + 1) * P], xn[par][:, t, :], k.ident[:, :])
                        last.then_inc(xT_done, 1)
                        pe.wait_ge(xnT_ready, lin(g, 1, 1))
                        wait_past(pe, lo_ready, 4 * u)
                        nc.tensor.matmul(qk_ps[par][0][:, :], wq[:, :], xnT[par][:, :], start=True, stop=True).then_inc(q_done, 1)
                        nc.tensor.matmul(qk_ps[par][1][:, :], wk[:, :], xnT[par][:, :], start=True, stop=True).then_inc(k_done, 1)
                        wait_past(pe, v_ready, 2 * u)
                        for t in range(TPS):
                            last = nc.tensor.matmul(v_ps[par][:, t * D:(t + 1) * D], xnT[par][:, t * P:(t + 1) * P], wv[:, :],
                                                    start=True, stop=True)
                        last.then_inc(v_done, 1)


def attention(k, name, HG, R, VD, scale, load_q, load_k, load_v, shared_k, out):
    nc, sem = k.nc, k.sem
    NG = BATCH * HEADS // HG
    CT = P // HG
    VW = VD + 1
    MROW = 96
    KROWS = MROW
    KH = 1 if shared_k else HG
    NSLOT = NP * HG
    NLOAD = 6

    per_head = [[("S", h, i) for i in reversed(range(TPB))] for h in range(HG)]
    base_units = []
    for h in range(HG):
        base_units += per_head[h][:1]
        if h:
            base_units.append(("m", h - 1, 0))
        base_units += per_head[h][1:]
    base_units.append(("m", HG - 1, 0))
    with_out = base_units[:4] + [("o", 0, 0)] + base_units[4:]

    with ExitStack() as c:
        sb = lambda n, s, d: c.enter_context(nc.sbuf_tensor(name + n, s, d))
        qS = [sb(f"qS{i}", [P, HG, SEQ], F32R) for i in range(2)]
        kS = [sb(f"kS{i}", [P, KH, SEQ], F32R) for i in range(2)]
        qT = [sb(f"qT{i}", [P, HG, SEQ], F32R) for i in range(2)]
        kT = [sb(f"kT{i}", [P, KH, SEQ], F32R) for i in range(2)]
        vst = [sb(f"v{i}", [P, TPB, HG if not shared_k else 1, VW], F32) for i in range(2)]
        prob = [sb(f"p{i}", [P, HG, ST], F32) for i in range(2)]
        mneg = [sb(f"m{i}", [P, HG, TPB], F32) for i in range(2)]
        osb = [sb(f"o{i}", [P, SEQ], F32) for i in range(2)]
        rec = [sb(f"rec{i}", [P, TPB, HG], F32) for i in range(2)]
        zero = sb("zero", [P, ST], BF16)
        one = sb("one", [1, SEQ], F32)
        s_ps = [c.enter_context(nc.psum_tensor(name + f"S{i}", [P, SEQ], F32)) for i in range(2)]
        t_ps = [c.enter_context(nc.psum_tensor(name + f"T{i}", [P, ST], F32)) for i in range(2)]
        o_ps = c.enter_context(nc.psum_tensor(name + "O", [P, SEQ], F32))
        init, one_set, zeroed, unit_ready, red_done, mcopy_done, out_done = (
            sem(name + n) for n in ("init", "one", "zd", "unit", "red", "mc", "out"))
        st_ready, exp_done, pv_done, o_copied, rec_done = (sem(name + n) for n in ("st", "exp", "pv", "oc", "rec"))
        ldS = [sem(name + f"ldS{i}") for i in range(2)]
        ldT = [sem(name + f"ldT{i}") for i in range(2)]

        def unit_base(g):
            if isinstance(g[0], int) and lin(g, 1, 0) == 0:
                return NP * HG
            return lin(g, NP * HG + 1, NP * HG - 1)

        def unit_slot(g):
            n = g[1] if isinstance(g[0], int) and lin(g, 1, 0) == 0 else g[1] + 1
            return n % 2

        def after(g, n):
            u, par = g
            return (u + (par + n) // 2, (par + n) % 2)

        def first(g):
            return isinstance(g[0], int) and lin(g, 1, 0) == 0

        def final(g):
            return isinstance(g[0], int) and lin(g, 1, 0) == NG - 1

        def units_of(g):
            if final(g):
                return [("o", 0, 0)]
            return base_units if first(g) else with_out

        def main_steps(eng, step):
            step((0, 0))
            step((0, 1))
            with eng.Fori(1, NG // 2 - 1) as u:
                step((u, 0))
                step((u, 1))
            step((NG // 2 - 1, 0))
            step((NG // 2 - 1, 1))

        with nc.Block() as block:
            @block.sync
            def _(sp):
                sp.wait_ge(init, 8)

                def load_S(g):
                    load_q(sp, qS[g[1]], g, ldS[g[1]])
                    load_k(sp, kS[g[1]], g, ldS[g[1]])

                def load_T(g):
                    load_q(sp, qT[g[1]], g, ldT[g[1]])
                    load_k(sp, kT[g[1]], g, ldT[g[1]])
                    load_v(sp, vst[g[1]], g, ldT[g[1]])

                load_S((0, 0))
                load_T((0, 0))
                load_S((0, 1))
                load_T((0, 1))

                def next_loads(g):
                    sp.wait_ge(red_done, lin(g, TPB * HG, TPB * HG))
                    load_S(after(g, 2))
                    sp.wait_ge(pv_done, lin(g, NP, NP))
                    load_T(after(g, 2))

                with sp.Fori(0, NG // 2 - 1) as u:
                    next_loads((u, 0))
                    next_loads((u, 1))

            @block.gpsimd
            def _(pool):
                for t in (*qS, *kS, *qT, *kT):
                    nc.gpsimd.memset(t[:, :, :].bitcast(F32), 0.0).then_inc(init, 1)

            @block.vector
            def _(dve):
                nc.vector.memset(one[:, :], 1.0).then_inc(one_set, 1)
                nc.vector.memset(zero[:, :], 0.0).then_inc(one_set, 1)
                dve.wait_ge(one_set, 2)
                dve.wait_ge(init, 8)
                for t in kT:
                    for h in range(KH):
                        nc.vector.tensor_copy(t[MROW:MROW + 1, h, :], one[0:1, :]).then_inc(one_set, 1)

                def consume(units, base, slot, gS, gO):
                    n_red = 0
                    for n, (kind, h, i) in enumerate(units):
                        if kind == "m":
                            continue
                        dve.wait_ge(unit_ready, base + (n + 1))
                        buf = s_ps[(slot + n) % 2]
                        if kind == "S":
                            nc.vector.tensor_reduce(mneg[gS[1]][:, h, i:i + 1], buf[:, 0:(i + 1) * P], AXX, ALU.max,
                                                    negate=True).then_inc(red_done, 1)
                        else:
                            o = buf[:, :].rearrange("p (i h c) -> p i h c", i=TPB, h=HG)
                            nc.vector.reciprocal(rec[gO[1]][:, :, :], o[:, :, :, VD]).then_inc(rec_done, 1)
                            dve.wait_ge(rec_done, lin(gO, 1, 1))
                            nc.vector.tensor_tensor(
                                out[:, bass.ds(lin(gO, 1, 0), 1), :, :].rearrange("p o i (h c) -> p (o i) h c", h=HG),
                                o[:, :, :, 0:VD], rec[gO[1]][:, :, :].unsqueeze(3).broadcast_to([P, TPB, HG, VD]),
                                ALU.mult).then_inc(out_done, 1)

                consume(base_units, 0, 0, (0, 0), None)

                def step(g):
                    consume(units_of(g), unit_base(g), unit_slot(g), after(g, 1), after(g, -1) if not first(g) else None)

                main_steps(dve, step)
                consume([("o", 0, 0)], unit_base((NG // 2 - 1, 1)) + 1, unit_slot((NG // 2 - 1, 1)) + 1, None, (NG // 2 - 1, 1))

            @block.scalar
            def _(act):
                def copy_max(base, slot, n, h, gS):
                    act.wait_ge(unit_ready, base + (n + 1))
                    nc.scalar.copy(qT[gS[1]][MROW:MROW + 1, h, :], s_ps[(slot + n) % 2][0:1, :]).then_inc(mcopy_done, 1)

                act.wait_ge(init, 8)
                for n, (kind, h, i) in enumerate(base_units):
                    if kind == "m":
                        copy_max(0, 0, n, h, (0, 0))

                def step(g):
                    units = units_of(g)
                    for p in range(NP):
                        for h in range(HG):
                            slot = p * HG + h
                            act.wait_ge(st_ready, lin(g, NSLOT, slot + 1))
                            if h == 0 and not (first(g) and p < 2):
                                act.wait_ge(pv_done, lin(g, NP, p - 1))
                            nc.scalar.activation(prob[(g[1] + p) % 2][:, h, :], t_ps[slot % 2][:, :], ACT.Exp, scale=scale)\
                                .then_inc(exp_done, 1)
                            todo = units[slot:slot + 1] if slot < NSLOT - 1 else units[slot:]
                            for n, (kind, hm, _) in enumerate(todo):
                                if kind == "m":
                                    copy_max(unit_base(g), unit_slot(g), slot + n, hm, after(g, 1))
                    act.wait_ge(pv_done, lin(g, NP, NP))
                    nc.scalar.copy(osb[g[1]][:, :], o_ps[:, :]).then_inc(o_copied, 1)

                main_steps(act, step)

            @block.tensor
            def _(pe):
                pe.wait_ge(one_set, 2 + 2 * KH)
                for b in range(SEQ // ST):
                    nc.tensor.matmul(o_ps[:, b * ST:(b + 1) * ST], zero[:, 0:P], zero[:, :], start=True, stop=True)

                def unit(units, base, slot, n, gS, gO, before):
                    kind, h, i = units[n]
                    prev = units[n - 2] if n >= 2 else before[n] if before else None
                    if prev is not None:
                        back = 0 if n >= 2 else 1
                        if prev[0] == "S":
                            order = [x for x in base_units if x[0] == "S"].index(prev)
                            pe.wait_ge(red_done, lin(gS, TPB * HG, order + 1 - back * TPB * HG))
                        elif prev[0] == "m":
                            pe.wait_ge(mcopy_done, lin(gS, HG, prev[1] + 1 - back * HG))
                        else:
                            pe.wait_ge(out_done, lin(gO, 1, 1))
                    buf = s_ps[(slot + n) % 2]
                    if kind == "S":
                        if n == 0:
                            pe.wait_ge(ldS[gS[1]], 16 * NLOAD + gS[0] * (16 * NLOAD))
                        w = (i + 1) * P
                        q = qS[gS[1]][0:KROWS, h, i * P:(i + 1) * P]
                        for c0 in range(0, w, ST):
                            c1 = min(c0 + ST, w)
                            nc.tensor.matmul(buf[:, c0:c1], q, kS[gS[1]][0:KROWS, 0 if shared_k else h, c0:c1],
                                             start=True, stop=c1 < w)
                        last = nc.tensor.matmul(buf[:, i * P:w], k.ident_bf[:, :], k.mask_q[:, :], start=False, stop=True)
                    elif kind == "m":
                        done = [x for x in base_units if x[0] == "S"].index(("S", h, 0)) + 1
                        pe.wait_ge(red_done, lin(gS, TPB * HG, done))
                        for b in range(TPB):
                            last = nc.tensor.transpose(buf[0:1, b * P:(b + 1) * P], mneg[gS[1]][:, h, b:b + 1], k.ident[:, :])
                    else:
                        pe.wait_ge(o_copied, lin(gO, 1, 1))
                        for b in range(TPB):
                            last = nc.tensor.transpose(buf[:, b * P:(b + 1) * P], osb[gO[1]][:, b * P:(b + 1) * P], k.ident[:, :])
                    last.then_inc(unit_ready, 1)

                for n in range(len(base_units)):
                    unit(base_units, 0, 0, n, (0, 0), None, None)

                order = [seg for piece in PIECES for seg in piece]
                opens = {b: next(s for s in order if s[1] // ST == b) for b in range(SEQ // ST)}
                closes = {b: [s for s in order if s[1] // ST == b][-1] for b in range(SEQ // ST)}

                def values(g, p):
                    pe.wait_ge(exp_done, lin(g, NSLOT, (p + 1) * HG))
                    if p == 0 and not first(g):
                        wait_past(pe, o_copied, lin(g, 1, 0))
                    off = 0
                    for seg in PIECES[p]:
                        j, q0, q1 = seg
                        for h in range(HG):
                            last = nc.tensor.matmul(
                                o_ps[h * CT:h * CT + VW, q0:q1], vst[g[1]][:, j, 0 if shared_k else h, :],
                                prob[(g[1] + p) % 2][:, h, off:off + q1 - q0],
                                start=opens[q0 // ST] == seg, stop=closes[q0 // ST] == seg)
                        off += q1 - q0
                    last.then_inc(pv_done, 1)

                def step(g):
                    units = units_of(g)
                    gS, gO = after(g, 1), after(g, -1) if not first(g) else None
                    pe.wait_ge(ldT[g[1]], 16 * (NLOAD + 1) + g[0] * (16 * (NLOAD + 1)))
                    for p in range(NP):
                        for h in range(HG):
                            slot = p * HG + h
                            if p == 0:
                                pe.wait_ge(mcopy_done, lin(g, HG, h + 1))
                            if not (first(g) and slot < 2):
                                pe.wait_ge(exp_done, lin(g, NSLOT, slot - 1))
                            buf, off = t_ps[slot % 2], 0
                            for j, q0, q1 in PIECES[p]:
                                diagonal = q0 == j * P
                                last = nc.tensor.matmul(buf[:, off:off + q1 - q0],
                                                        kT[g[1]][0:MROW + 1, 0 if shared_k else h, j * P:(j + 1) * P],
                                                        qT[g[1]][0:MROW + 1, h, q0:q1], start=True, stop=not diagonal)
                                if diagonal:
                                    last = nc.tensor.matmul(buf[:, off:off + P], k.ident_bf[:, :], k.mask_k[:, :],
                                                            start=False, stop=True)
                                off += q1 - q0
                            last.then_inc(st_ready, 1)
                            todo = range(slot, slot + 1) if slot < NSLOT - 1 else range(slot, len(units))
                            for n in todo:
                                if n < len(units):
                                    unit(units, unit_base(g), unit_slot(g), n, gS, gO, base_units[-2:])
                        if p:
                            values(g, p - 1)
                    values(g, NP - 1)

                main_steps(pe, step)
                g = (NG // 2 - 1, 1)
                unit([("m", 0, 0), ("m", 0, 0), ("o", 0, 0)][2:], 0, unit_slot(g) + 1, 0, None, g, None)


def project_out(k, name, attn, w_out, NHG):
    nc, sem = k.nc, k.sem
    GW = attn.shape[3]
    NC = NHG * GW // P
    with ExitStack() as c:
        sb = lambda n, s, d: c.enter_context(nc.sbuf_tensor(name + n, s, d))
        w = w_out
        stage = [sb(f"st{i}", [P, TPS, NHG * GW], F32) for i in range(2)]
        aT = [sb(f"aT{i}", [P, NC, ST], F32) for i in range(2)]
        aT_ps = [c.enter_context(nc.psum_tensor(name + f"aps{i}", [P, ST], F32)) for i in range(4)]
        y_ps = [c.enter_context(nc.psum_tensor(name + f"y{i}", [P, ST], F32)) for i in range(2)]
        staged, turned, aT_ready, y_ready, added = (sem(name + n) for n in ("sg", "tr", "aT", "y", "add"))
        with nc.Block() as block:
            @block.gpsimd
            def _(pool):
                for u in rounds(pool, NST // 2):
                    for par in range(2):
                        wait_past(pool, turned, u * (2 * NC))
                        for t in range(TPS):
                            last = nc.gpsimd.tensor_copy(
                                stage[par][:, t, :].rearrange("p (g c) -> p g c", g=NHG),
                                attn[:, bass.ds(u * NHG, NHG), par * TPS + t, :])
                            last.then_inc(staged, 1)

            @block.tensor
            def _(pe):
                for u in rounds(pe, NST // 2):
                    for par in range(2):
                        g = (u, par)
                        pe.wait_ge(staged, lin(g, TPS, TPS))
                        for n in range(NC):
                            m = (par * NC + n) % 4
                            if NC == 1:
                                wait_past(pe, aT_ready, u * 2)
                            else:
                                wait_past(pe, aT_ready, lin(g, NC, 0))
                            for t in range(TPS):
                                last = nc.tensor.transpose(aT_ps[m][:, t * P:(t + 1) * P], stage[par][:, t, n * P:(n + 1) * P],
                                                           k.ident[:, :])
                            last.then_inc(turned, 1)
                        pe.wait_ge(aT_ready, lin(g, NC, NC))
                        wait_past(pe, added, u * 2)
                        for t in range(TPS):
                            for n in range(NC):
                                last = nc.tensor.matmul(y_ps[par][:, t * D:(t + 1) * D], aT[par][:, n, t * P:(t + 1) * P],
                                                        w[:, n, :], start=n == 0, stop=n == NC - 1)
                        last.then_inc(y_ready, 1)

            @block.scalar
            def _(act):
                for u in rounds(act, NST // 2):
                    for par in range(2):
                        g = (u, par)
                        wait_past(act, y_ready, u * 2)
                        for n in range(NC):
                            act.wait_ge(turned, lin(g, NC, n + 1))
                            nc.scalar.copy(aT[par][:, n, :], aT_ps[(par * NC + n) % 4][:, :]).then_inc(aT_ready, 1)

            @block.vector
            def _(dve):
                for u in rounds(dve, NST // 2):
                    for par in range(2):
                        g = (u, par)
                        dve.wait_ge(y_ready, lin(g, 1, 1))
                        rows = k.x[:, bass.ds(lin(g, TPS, 0), TPS), :]
                        nc.vector.tensor_tensor(rows, y_ps[par][:, :].rearrange("p (t d) -> p t d", t=TPS), rows,
                                                ALU.add).then_inc(added, 1)


def route(k, name, E, K, w_router, bias_row, xnT, gateT):
    nc, sem = k.nc, k.sem
    PAD = 6 if K == 2 else 0
    LOADED = 16 if bias_row is None else 32
    TAKEN, FILL = (-1.0, 3.0) if K == 2 else (-3e38, 0.0)
    with ExitStack() as c:
        sb = lambda n, s, d: c.enter_context(nc.sbuf_tensor(name + n, s, d))
        pb = lambda n: c.enter_context(nc.psum_tensor(name + n, [P, ST], F32))
        wr = sb("wr", [P, E], F32)
        bias = sb("bias", [P, E], F32)
        held = sb("held", [P, 1], F32)
        xn = [sb(f"xn{i}", [P, TPS, D], F32) for i in range(2)]
        xs = [sb(f"xs{i}", [P, ST], F32) for i in range(2)]
        lg = [sb(f"lg{i}", [P, TPS, E], F32) for i in range(2)]
        pr = [sb(f"pr{i}", [P, TPS, E + PAD], F32) for i in range(2)]
        sel = [sb(f"sel{i}", [P, TPS, E], F32) for i in range(2)]
        top = [sb(f"top{i}", [P, TPS, 8], F32) for i in range(2)]
        srt = [sb(f"srt{i}", [P, TPS, 8], F32) for i in range(2)]
        rep = [sb(f"rep{i}", [P, TPS, E + PAD], F32) for i in range(2)]
        sm = [sb(f"sm{i}", [P, TPS], F32) for i in range(2)]
        gt = [sb(f"gt{i}", [P, TPS, 2, E], F32) for i in range(2)]
        hi = [sb(f"hi{i}", [P, TPS, E], F32R) for i in range(2)]
        xT_ps = [pb(f"xT{i}") for i in range(2)]
        l_ps = [pb(f"l{i}") for i in range(2)]
        g_ps = [pb(f"g{i}") for i in range(2)]
        loaded, filled, xn_ready, xT_done, xs_ready, x_kept = (sem(name + n) for n in ("ld", "fl", "xn", "xT", "xs", "xk"))
        l_done, lg_ready, pr_ready, chain, g_done, g_kept, gt_ready = (
            sem(name + n) for n in ("l", "lg", "pr", "ch", "gd", "gk", "gt"))
        with nc.Block() as block:
            @block.sync
            def _(sp):
                sp.dma_start(wr[:, :], w_router).then_inc(loaded, 16)
                if bias_row is not None:
                    sp.dma_start(bias[:, :], bias_row.partition_broadcast(P)).then_inc(loaded, 16)

            @block.tensor
            def _(pe):
                pe.wait_ge(loaded, LOADED)

                def gates(g):
                    pe.wait_ge(gt_ready, lin(g, 1, 1))
                    for t in range(TPS):
                        last = nc.tensor.transpose(g_ps[g[1]][0:2 * E, t * P:(t + 1) * P],
                                                   gt[g[1]][:, t, :, :].rearrange("p a e -> p (a e)"), k.ident[:, :])
                    last.then_inc(g_done, 1)

                for u in rounds(pe, NST // 2):
                    for par in range(2):
                        g = (u, par)
                        pe.wait_ge(xn_ready, lin(g, 1, 1))
                        for t in range(TPS):
                            last = nc.tensor.transpose(xT_ps[par][:, t * P:(t + 1) * P], xn[par][:, t, :], k.ident[:, :])
                        last.then_inc(xT_done, 1)
                        pe.wait_ge(xs_ready, lin(g, 1, 1))
                        for t in range(TPS):
                            last = nc.tensor.matmul(l_ps[par][:, t * E:(t + 1) * E], xs[par][:, t * P:(t + 1) * P], wr[:, :],
                                                    start=True, stop=True)
                        last.then_inc(l_done, 1)
                        gates(g)

            @block.scalar
            def _(act):
                for u in rounds(act, NST // 2):
                    for par in range(2):
                        g = (u, par)
                        act.wait_ge(xT_done, lin(g, 1, 1))
                        wait_past(act, x_kept, u * 2)
                        nc.scalar.copy(xs[par][:, :], xT_ps[par][:, :]).then_inc(xs_ready, 1)
                        act.wait_ge(lg_ready, lin(g, 1, 1))
                        if K == 2:
                            act.wait_ge(filled, 6)
                        nc.scalar.activation(pr[par][:, :, 0:E], lg[par][:, :, :], ACT.Exp, scale=1.0 if K == 2 else -1.0)\
                            .then_inc(pr_ready, 1)
                        act.wait_ge(g_done, lin(g, 1, 1))
                        nc.scalar.copy(gateT[:, bass.ds(lin(g, ST, 0), ST)], g_ps[par][0:2 * E, :]).then_inc(g_kept, 1)

            @block.gpsimd
            def _(pool):
                if K == 2:
                    for t in (*pr, *top, *rep):
                        nc.gpsimd.memset(t[:, :, :], FILL).then_inc(filled, 1)
                for u in rounds(pool, NST // 2):
                    for par in range(2):
                        g = (u, par)
                        pool.wait_ge(xs_ready, lin(g, 1, 1))
                        nc.gpsimd.tensor_copy(xnT[:, bass.ds(lin(g, ST, 0), ST)], xs[par][:, :]).then_inc(x_kept, 1)

            @block.vector
            def _(dve):
                dve.wait_ge(loaded, LOADED)
                if K == 2:
                    dve.wait_ge(filled, 6)
                count = [0]

                def steps(u, par, per):
                    g = (u, par)

                    def link(ins):
                        count[0] += 1
                        ins.then_inc(chain, 1)
                        dve.wait_ge(chain, u * per + count[0])

                    def hold():
                        nc.vector.memset(held[:, :], 0.0)

                    normalise(k, dve, xn[par], g, xn_ready)
                    logits = l_ps[par][:, 0:TPS * E].rearrange("p (t e) -> p t e", t=TPS)
                    wide = lambda a: a.unsqueeze(2).broadcast_to([P, TPS, E])
                    dve.wait_ge(l_done, lin(g, 1, 1))
                    s = sm[par][:, :]
                    p = pr[par][:, :, 0:E]
                    if K == 2:
                        link(nc.vector.tensor_reduce(s, logits, AXX, ALU.max))
                        nc.vector.tensor_tensor(lg[par][:, :, :], logits, wide(s), ALU.subtract).then_inc(lg_ready, 1)
                        dve.wait_ge(pr_ready, lin(g, 1, 1))
                        hold()
                        for t in range(TPS):
                            n = nc.vector.max(srt[par][:, t, :], pr[par][:, t, 0:E])
                            n.then_inc(chain, 1)
                        count[0] += TPS
                        dve.wait_ge(chain, u * per + count[0])
                        link(nc.vector.tensor_copy(top[par][:, :, 0:K], srt[par][:, :, 0:K]))
                        values, chosen = pr[par], p
                    else:
                        nc.vector.tensor_copy(lg[par][:, :, :], logits).then_inc(lg_ready, 1)
                        dve.wait_ge(pr_ready, lin(g, 1, 1))
                        link(nc.vector.tensor_scalar(p, p, 1.0, None, ALU.add))
                        link(nc.vector.reciprocal(p, p))
                        link(nc.vector.tensor_tensor(sel[par][:, :, :], p, bias[:, :].unsqueeze(1).broadcast_to([P, TPS, E]), ALU.add))
                        hold()
                        for t in range(TPS):
                            nc.vector.max(top[par][:, t, :], sel[par][:, t, :]).then_inc(chain, 1)
                        count[0] += TPS
                        dve.wait_ge(chain, u * per + count[0])
                        values, chosen = sel[par], sel[par][:, :, :]
                    hold()
                    for t in range(TPS):
                        nc.vector.match_replace(rep[par][:, t, :], top[par][:, t, :], values[:, t, :], TAKEN).then_inc(chain, 1)
                    count[0] += TPS
                    dve.wait_ge(chain, u * per + count[0])
                    r = rep[par][:, :, 0:E]
                    link(nc.vector.tensor_tensor(r, r, chosen, ALU.not_equal))
                    link(nc.vector.tensor_tensor(r, r, p, ALU.mult))
                    link(nc.vector.tensor_reduce(s, r, AXX, ALU.add))
                    link(nc.vector.reciprocal(s, s))
                    if K != 2:
                        link(nc.vector.tensor_scalar(s, s, ROUTE_SCALE, None, ALU.mult))
                    link(nc.vector.tensor_tensor(r, r, wide(s), ALU.mult))
                    link(nc.vector.tensor_copy(hi[par][:, :, :], r))
                    link(nc.vector.tensor_copy(gt[par][:, :, 0, :], hi[par][:, :, :].bitcast(F32)))
                    nc.vector.tensor_tensor(gt[par][:, :, 1, :], r, hi[par][:, :, :].bitcast(F32), ALU.subtract).then_inc(gt_ready, 1)

                per = 2 * ((2 + TPS + TPS + 7) if K == 2 else (3 + TPS + TPS + 8))
                for u in rounds(dve, NST // 2):
                    count[0] = 0
                    for par in range(2):
                        wait_past(dve, g_done, u * 2)
                        steps(u, par, per)
                assert count[0] == per, (count[0], per)


def moe_0(k, w_fc, b_fc, w_proj, b_proj, b_proj_s, xnT, gateT, sel):
    nc, sem = k.nc, k.sem
    E, NCH = 8, 4
    NE = E + 1
    NH = NE * NCH
    with ExitStack() as c:
        sb = lambda n, s, d: c.enter_context(nc.sbuf_tensor("m0_" + n, s, d))
        pb = lambda n: c.enter_context(nc.psum_tensor("m0_" + n, [P, ST], F32))
        wfc, wpr = sb("wfc", [P, NE, NCH * P], F32), sb("wpr", [P, NE, NCH, D], F32)
        bfc, bps = sb("bfc", [P, NH], F32), sb("bps", [P, 1], F32)
        bp = sb("bp", [2 * E, D], F32)
        bph, bpl = sb("bph", [2 * E, D], F32R), sb("bpl", [2 * E, D], F32R)
        h = [sb(f"h{i}", [P, ST], F32) for i in range(3)]
        gb = [sb(f"gb{i}", [P, ST], F32) for i in range(2)]
        prod = [sb(f"pr{i}", [P, ST], F32) for i in range(2)]
        acc = [sb(f"acc{i}", [P, ST], F32) for i in range(2)]
        f_ps = [pb(f"f{i}") for i in range(3)]
        y_ps = [pb(f"y{i}") for i in range(3)]
        b_ps, t_ps = pb("b"), pb("t")
        loaded, split, fc_done, h_ready, y_done = (sem("m0_" + n) for n in ("ld", "sp", "fc", "h", "y"))
        gb_done, gb_ready, summed, turned, added = (sem("m0_" + n) for n in ("gd", "gb", "sum", "tr", "add"))
        NDVE = 1 + 2 * E
        with nc.Block() as block:
            @block.sync
            def _(sp):
                for dst, src in ((bfc[:, :], b_fc), (bps[:, :], b_proj_s), (bp[0:E, :], b_proj), (bp[E:2 * E, :], b_proj)):
                    sp.dma_start(dst, src).then_inc(loaded, 16)
                for e in range(NE):
                    sp.dma_start(wfc[:, e, :], w_fc[:, e, :]).then_inc(loaded, 16)
                    sp.dma_start(wpr[:, e, :, :], w_proj[:, e, :, :]).then_inc(loaded, 16)

            @block.tensor
            def _(pe):
                pe.wait_ge(loaded, 16 * (4 + 2 * NE))
                pe.wait_ge(split, 2)

                def supertile(g, u, par):
                    cols = bass.ds(lin(g, ST, 0), ST)

                    def project(n):
                        e, ch = divmod(n, NCH)
                        if ch == 0:
                            wait_past(pe, summed, lin(g, NDVE, max(2 * (e - 3), 1) if e >= 3 else 0))
                        pe.wait_ge(h_ready, lin(g, NH, n + 1))
                        last = nc.tensor.matmul(y_ps[e % 3][:, :], wpr[:, e, ch, :], h[n % 3][:, :], start=ch == 0,
                                                stop=ch == NCH - 1 and e > 0)
                        if ch == NCH - 1:
                            if e == 0:
                                nc.tensor.matmul(y_ps[0][:, :], bph[:, :], gateT[:, cols], start=False, stop=False)
                                last = nc.tensor.matmul(y_ps[0][:, :], bpl[:, :], gateT[:, cols], start=False, stop=True)
                            last.then_inc(y_done, 1)

                    for n in range(NH):
                        e, ch = divmod(n, NCH)
                        wait_past(pe, h_ready, lin(g, NH, max(n - 2, 0)))
                        if ch == 0 and e:
                            wait_past(pe, gb_ready, lin(g, E, e - 1))
                        nc.tensor.matmul(f_ps[n % 3][:, :], wfc[:, e, ch * P:(ch + 1) * P], xnT[:, cols], start=True,
                                         stop=True).then_inc(fc_done, 1)
                        if ch == 0 and e:
                            nc.tensor.matmul(b_ps[:, :], sel[:, e - 1, :], gateT[:, cols], start=True, stop=True).then_inc(gb_done, 1)
                        if n >= 2:
                            project(n - 2)
                    project(NH - 2)
                    project(NH - 1)
                    pe.wait_ge(summed, lin(g, NDVE, NDVE))
                    wait_past(pe, added, lin(g, 1, 0))
                    for t in range(TPS):
                        last = nc.tensor.transpose(t_ps[:, t * P:(t + 1) * P], acc[par][:, t * P:(t + 1) * P], k.ident[:, :])
                    last.then_inc(turned, 1)

                for u in rounds(pe, NST // 2):
                    for par in range(2):
                        supertile((u, par), u, par)

            @block.scalar
            def _(act):
                act.wait_ge(loaded, 16 * (4 + 2 * NE))
                for u in rounds(act, NST // 2):
                    for par in range(2):
                        g = (u, par)
                        for n in range(NH):
                            e, ch = divmod(n, NCH)
                            act.wait_ge(fc_done, lin(g, NH, n + 1))
                            nc.scalar.activation(h[n % 3][:, :], f_ps[n % 3][:, :], ACT.Gelu_apprx_tanh, bias=bfc[:, n:n + 1])\
                                .then_inc(h_ready, 1)
                            if ch == 0 and e:
                                wait_past(act, gb_done, lin(g, E, e))
                                wait_past(act, summed, lin(g, NDVE, 2 * (e - 2) if e >= 3 else 0))
                                nc.scalar.copy(gb[e % 2][:, :], b_ps[:, :]).then_inc(gb_ready, 1)

            @block.vector
            def _(dve):
                dve.wait_ge(loaded, 16 * (4 + 2 * NE))
                nc.vector.tensor_copy(bph[:, :], bp[:, :]).then_inc(split, 1)
                dve.wait_ge(split, 1)
                nc.vector.tensor_tensor(bpl[:, :], bp[:, :], bph[:, :].bitcast(F32), ALU.subtract).then_inc(split, 1)

                def supertile(g, par):
                    n = 0

                    def step():
                        nonlocal n
                        n += 1
                        return lin(g, NDVE, n)

                    dve.wait_ge(y_done, lin(g, NE, 1))
                    wait_past(dve, turned, g[0] * 2)
                    nc.vector.tensor_scalar(acc[par][:, :], y_ps[0][:, :], bps[:, 0:1], None, ALU.add)\
                        .then_inc(summed, 1)
                    n = 1
                    dve.wait_ge(summed, lin(g, NDVE, 1))
                    for e in range(1, NE):
                        dve.wait_ge(y_done, lin(g, NE, e + 1))
                        wait_past(dve, gb_ready, lin(g, E, e))
                        nc.vector.tensor_tensor(prod[e % 2][:, :], y_ps[e % 3][:, :], gb[e % 2][:, :], ALU.mult).then_inc(summed, 1)
                        dve.wait_ge(summed, step())
                        nc.vector.tensor_tensor(acc[par][:, :], acc[par][:, :], prod[e % 2][:, :], ALU.add).then_inc(summed, 1)
                        dve.wait_ge(summed, step())
                    dve.wait_ge(turned, lin(g, 1, 1))
                    rows = k.x[:, bass.ds(lin(g, TPS, 0), TPS), :]
                    nc.vector.tensor_tensor(rows, t_ps[:, :].rearrange("p (t d) -> p t d", t=TPS), rows, ALU.add)\
                        .then_inc(added, 1)

                for u in rounds(dve, NST // 2):
                    for par in range(2):
                        supertile((u, par), par)


def absorb(k, w_qT, w_kT, w_vT, w_out, a_q, a_v):
    nc, sem = k.nc, k.sem
    HD, LD = 64, 32
    HPC = P // LD
    with ExitStack() as c:
        sb = lambda n, s: c.enter_context(nc.sbuf_tensor("ab_" + n, s, F32))
        wq, wk = sb("wq", [HD, HEADS, D]), sb("wk", [HD, HEADS, LD])
        wv, wo = sb("wv", [HD, HEADS, LD]), sb("wo", [HD, HEADS, D])
        q_ps = c.enter_context(nc.psum_tensor("ab_q", [P, ST], F32))
        v_ps = c.enter_context(nc.psum_tensor("ab_v", [P, ST], F32))
        loaded, q_done, v_done, kept = (sem("ab_" + n) for n in ("ld", "q", "v", "kept"))
        with nc.Block() as block:
            @block.sync
            def _(sp):
                for dst, src in ((wq, w_qT), (wk, w_kT), (wv, w_vT), (wo, w_out)):
                    sp.dma_start(dst[:, :, :], src).then_inc(loaded, 16)

            @block.tensor
            def _(pe):
                pe.wait_ge(loaded, 64)
                for h in range(HEADS):
                    last = nc.tensor.matmul(q_ps[:, h * LD:(h + 1) * LD], wq[:, h, :], wk[:, h, :], start=True, stop=True)
                last.then_inc(q_done, 1)
                for h in range(HEADS):
                    n, r = divmod(h, HPC)
                    last = nc.tensor.matmul(v_ps[r * LD:(r + 1) * LD, n * D:(n + 1) * D], wv[:, h, :], wo[:, h, :],
                                            start=True, stop=True)
                last.then_inc(v_done, 1)

            @block.vector
            def _(dve):
                dve.wait_ge(q_done, 1)
                nc.vector.tensor_copy(a_q[:, :], q_ps[:, :]).then_inc(kept, 1)
                dve.wait_ge(v_done, 1)
                nc.vector.tensor_copy(a_v[:, :, :], v_ps[:, :].rearrange("p (n o) -> p n o", o=D)).then_inc(kept, 1)


def project_1(k, a_q, w_kv, scr_q, scr_k, scr_v):
    nc, sem = k.nc, k.sem
    LD = 32
    NC = HEADS * LD // P
    NT = NC + 1
    with ExitStack() as c:
        sb = lambda n, s, d: c.enter_context(nc.sbuf_tensor("p1_" + n, s, d))
        pb = lambda n: c.enter_context(nc.psum_tensor("p1_" + n, [P, ST], F32))
        wkv = sb("wkv", [P, LD], F32)
        xn = [sb(f"xn{i}", [P, TPS, D], F32) for i in range(2)]
        xnT = [sb(f"xnT{i}", [P, ST], F32) for i in range(2)]
        hi = [sb(f"hi{i}", [P, NT, ST], F32R) for i in range(2)]
        lo = [sb(f"lo{i}", [P, NT, ST], F32R) for i in range(2)]
        v1 = [sb(f"v{i}", [P, TPS, LD + 1], F32) for i in range(2)]
        xT_ps = [pb(f"xT{i}") for i in range(2)]
        t_ps = [pb(f"t{i}") for i in range(NT)]
        v_ps = pb("v")
        loaded, ones, xn_ready, xT_done, xnT_ready, t_done, v_done, hi_ready, lo_ready, v_ready = (
            sem("p1_" + n) for n in ("ld", "ones", "xn", "xT", "xnT", "t", "v", "hi", "lo", "vr"))
        stored = [sem(f"p1_st{i}") for i in range(2)]
        NSTORE = 2 * NT + 1
        rows = [P] * NC + [LD]
        with nc.Block() as block:
            @block.sync
            def _(sp):
                sp.dma_start(wkv[:, :], w_kv).then_inc(loaded, 16)
                for u in rounds(sp, NST // 2):
                    for par in range(2):
                        g = (u, par)
                        cols = slice(par * ST, (par + 1) * ST)
                        for n in range(NT):
                            dst = scr_q[:, :, n * P:(n + 1) * P, :] if n < NC else scr_k
                            sp.wait_ge(lo_ready, lin(g, NT, n + 1))
                            for part, tile in ((0, hi[par]), (1, lo[par])):
                                sp.dma_start(dst[part, bass.ds(u, 1), :, cols].rearrange("b c n -> (b c) n"),
                                             tile[0:rows[n], n, :].bitcast(F32)).then_inc(stored[par], 16)
                        sp.wait_ge(v_ready, lin(g, 1, 1))
                        sp.dma_start(scr_v[bass.ds(u, 1), :, par * TPS:(par + 1) * TPS, :].rearrange("b p t c -> (b p) t c"),
                                     v1[par][:, :, :]).then_inc(stored[par], 16)
                for par in range(2):
                    sp.wait_ge(stored[par], 16 * NSTORE * (NST // 2))

            @block.gpsimd
            def _(pool):
                for i in range(2):
                    nc.gpsimd.memset(v1[i][:, :, :], 1.0).then_inc(ones, 1)

            @block.vector
            def _(dve):
                for u in rounds(dve, NST // 2):
                    for par in range(2):
                        g = (u, par)
                        wait_past(dve, xT_done, u * 2)
                        normalise(k, dve, xn[par], g, xn_ready)
                        wait_past(dve, stored[par], u * (16 * NSTORE))
                        for n in range(NT):
                            dve.wait_ge(hi_ready, lin(g, NT, n + 1))
                            nc.vector.tensor_tensor(lo[par][0:rows[n], n, :], t_ps[n][0:rows[n], :],
                                                    hi[par][0:rows[n], n, :].bitcast(F32), ALU.subtract).then_inc(lo_ready, 1)

            @block.scalar
            def _(act):
                act.wait_ge(ones, 2)
                for u in rounds(act, NST // 2):
                    for par in range(2):
                        g = (u, par)
                        act.wait_ge(xT_done, lin(g, 1, 1))
                        nc.scalar.copy(xnT[par][:, :], xT_ps[par][:, :]).then_inc(xnT_ready, 1)
                        wait_past(act, stored[par], u * (16 * NSTORE))
                        for n in range(NT):
                            act.wait_ge(t_done, lin(g, NT, n + 1))
                            nc.scalar.copy(hi[par][0:rows[n], n, :], t_ps[n][0:rows[n], :]).then_inc(hi_ready, 1)
                        act.wait_ge(v_done, lin(g, 1, 1))
                        nc.scalar.copy(v1[par][:, :, 0:LD], v_ps[:, 0:TPS * LD].rearrange("p (t c) -> p t c", t=TPS))\
                            .then_inc(v_ready, 1)

            @block.tensor
            def _(pe):
                pe.wait_ge(loaded, 16)
                for u in rounds(pe, NST // 2):
                    for par in range(2):
                        g = (u, par)
                        pe.wait_ge(xn_ready, lin(g, 1, 1))
                        for t in range(TPS):
                            last = nc.tensor.transpose(xT_ps[par][:, t * P:(t + 1) * P], xn[par][:, t, :], k.ident[:, :])
                        last.then_inc(xT_done, 1)
                        pe.wait_ge(xnT_ready, lin(g, 1, 1))
                        for n in range(NT):
                            wait_past(pe, lo_ready, lin(g, NT, 0) if n == NT - 1 else lin(g, NT, 0))
                            w = a_q[:, n * P:(n + 1) * P] if n < NC else wkv[:, :]
                            nc.tensor.matmul(t_ps[n][0:rows[n], :], w, xnT[par][:, :], start=True, stop=True).then_inc(t_done, 1)
                        wait_past(pe, v_ready, lin(g, 1, 0))
                        for t in range(TPS):
                            last = nc.tensor.matmul(v_ps[:, t * LD:(t + 1) * LD], xnT[par][:, t * P:(t + 1) * P], wkv[:, :],
                                                    start=True, stop=True)
                        last.then_inc(v_done, 1)


def moe_1(k, w_g, w_u, w_d, xnT, gateT, sel, out):
    nc, sem = k.nc, k.sem
    E = 16
    NE = E + 1
    with ExitStack() as c:
        sb = lambda n, s, d: c.enter_context(nc.sbuf_tensor("m1_" + n, s, d))
        pb = lambda n: c.enter_context(nc.psum_tensor("m1_" + n, [P, ST], F32))
        wg, wu, wd = (sb(n, [P, NE, P], F32) for n in ("wg", "wu", "wd"))
        act_g = [sb(f"s{i}", [P, ST], F32) for i in range(2)]
        gb = [sb(f"gb{i}", [P, ST], F32) for i in range(2)]
        prod = [sb(f"pr{i}", [P, ST], F32) for i in range(2)]
        h = [sb(f"h{i}", [P, ST], F32) for i in range(2)]
        y = [sb(f"y{i}", [P, ST], F32) for i in range(2)]
        g_ps = [pb(f"g{i}") for i in range(2)]
        u_ps = [pb(f"u{i}") for i in range(2)]
        b_ps, y_ps, t_ps = pb("b"), pb("y"), pb("t")
        loaded, g_done, u_done, gb_done, gb_ready, silu_ready, prod_ready, h_ready = (
            sem("m1_" + n) for n in ("ld", "g", "u", "gd", "gb", "si", "pr", "h"))
        y_done, y_kept, turned, added, stored = (sem("m1_" + n) for n in ("yd", "yk", "tr", "add", "st"))
        with nc.Block() as block:
            @block.sync
            def _(sp):
                for dst, src in ((wg, w_g), (wu, w_u), (wd, w_d)):
                    sp.dma_start(dst[:, :, :], src).then_inc(loaded, 16)
                out_t = out.rearrange("(t p) d -> p t d", p=P)
                with sp.Fori(0, NST) as s:
                    sp.wait_ge(added, s + 1)
                    rows = bass.ds(s * TPS, TPS)
                    sp.dma_start(out_t[:, rows, :], k.x[:, rows, :]).then_inc(stored, 16)
                sp.wait_ge(stored, 16 * NST)

            @block.tensor
            def _(pe):
                pe.wait_ge(loaded, 48)

                def supertile(g, par):
                    cols = bass.ds(lin(g, ST, 0), ST)

                    def down(e):
                        pe.wait_ge(h_ready, lin(g, NE, e + 1))
                        if e == 0:
                            wait_past(pe, y_kept, lin(g, 1, 0))
                        last = nc.tensor.matmul(y_ps[:, :], wd[:, e, :], h[e % 2][:, :], start=e == 0, stop=e == NE - 1)
                        if e == NE - 1:
                            last.then_inc(y_done, 1)

                    for e in range(NE):
                        wait_past(pe, silu_ready, lin(g, NE, max(e - 1, 0)))
                        nc.tensor.matmul(g_ps[e % 2][:, :], wg[:, e, :], xnT[:, cols], start=True, stop=True).then_inc(g_done, 1)
                        wait_past(pe, h_ready, lin(g, NE, max(e - 1, 0)))
                        if e < E:
                            wait_past(pe, gb_ready, lin(g, E, e))
                        nc.tensor.matmul(u_ps[e % 2][:, :], wu[:, e, :], xnT[:, cols], start=True, stop=True).then_inc(u_done, 1)
                        if e < E:
                            nc.tensor.matmul(b_ps[:, :], sel[:, e, :], gateT[:, cols], start=True, stop=True).then_inc(gb_done, 1)
                        if e:
                            down(e - 1)
                    down(NE - 1)
                    pe.wait_ge(y_kept, lin(g, 1, 1))
                    wait_past(pe, added, lin(g, 1, 0))
                    for t in range(TPS):
                        last = nc.tensor.transpose(t_ps[:, t * P:(t + 1) * P], y[par][:, t * P:(t + 1) * P], k.ident[:, :])
                    last.then_inc(turned, 1)

                for u in rounds(pe, NST // 2):
                    for par in range(2):
                        supertile((u, par), par)

            @block.scalar
            def _(act):
                for u in rounds(act, NST // 2):
                    for par in range(2):
                        g = (u, par)
                        for e in range(NE):
                            act.wait_ge(g_done, lin(g, NE, e + 1))
                            wait_past(act, prod_ready, lin(g, NE, max(e - 1, 0)))
                            nc.scalar.activation(act_g[e % 2][:, :], g_ps[e % 2][:, :], ACT.Silu).then_inc(silu_ready, 1)
                            if e < E:
                                act.wait_ge(gb_done, lin(g, E, e + 1))
                                wait_past(act, h_ready, lin(g, NE, max(e - 1, 0)))
                                nc.scalar.copy(gb[e % 2][:, :], b_ps[:, :]).then_inc(gb_ready, 1)
                        act.wait_ge(y_done, lin(g, 1, 1))
                        wait_past(act, turned, u * 2)
                        nc.scalar.copy(y[par][:, :], y_ps[:, :]).then_inc(y_kept, 1)

            @block.vector
            def _(dve):
                for u in rounds(dve, NST // 2):
                    for par in range(2):
                        g = (u, par)
                        for e in range(NE):
                            gated = e < E
                            dve.wait_ge(silu_ready, lin(g, NE, e + 1))
                            dve.wait_ge(u_done, lin(g, NE, e + 1))
                            dst = prod[e % 2] if gated else h[e % 2]
                            ins = nc.vector.tensor_tensor(dst[:, :], u_ps[e % 2][:, :], act_g[e % 2][:, :], ALU.mult)
                            ins.then_inc(prod_ready, 1)
                            dve.wait_ge(prod_ready, lin(g, NE, e + 1))
                            if gated:
                                dve.wait_ge(gb_ready, lin(g, E, e + 1))
                                nc.vector.tensor_tensor(h[e % 2][:, :], prod[e % 2][:, :], gb[e % 2][:, :], ALU.mult)\
                                    .then_inc(h_ready, 1)
                            else:
                                nc.vector.sem_inc(h_ready, 1)
                        dve.wait_ge(turned, lin(g, 1, 1))
                        rows = k.x[:, bass.ds(lin(g, TPS, 0), TPS), :]
                        nc.vector.tensor_tensor(rows, t_ps[:, :].rearrange("p (t d) -> p t d", t=TPS), rows, ALU.add)\
                            .then_inc(added, 1)


def constants(k, sel0, sel1):
    nc, sem = k.nc, k.sem
    made, cast = sem("c_made"), sem("c_cast")
    with ExitStack() as c:
        raw = [c.enter_context(nc.sbuf_tensor(f"c_sel{n}", [s.shape[0], s.shape[1], P], F32)) for n, s in enumerate((sel0, sel1))]
        with nc.Block() as block:
            @block.gpsimd
            def _(pool):
                n = 0
                for t in (k.ident, k.ident_bf, k.mask_q, k.mask_k):
                    nc.gpsimd.memset(t[:, :], 0.0).then_inc(made, 1)
                for t in raw:
                    nc.gpsimd.memset(t[:, :, :], 0.0).then_inc(made, 1)
                n = 6
                pool.wait_ge(made, n)
                for t in (k.ident, k.ident_bf):
                    nc.gpsimd.affine_select(out=t[:, :], in_=t[:, :], compare_op=ALU.not_equal, fill=1.0, base=0,
                                            pattern=[[-1, P]], channel_multiplier=1).then_inc(made, 1)
                nc.gpsimd.affine_select(out=k.mask_q[:, :], in_=k.mask_q[:, :], compare_op=ALU.is_ge, fill=MASKED, base=0,
                                        pattern=[[-1, P]], channel_multiplier=1).then_inc(made, 1)
                nc.gpsimd.affine_select(out=k.mask_k[:, :], in_=k.mask_k[:, :], compare_op=ALU.is_ge, fill=MASKED, base=0,
                                        pattern=[[1, P]], channel_multiplier=-1).then_inc(made, 1)
                n += 4
                for t in raw:
                    E = t.shape[1]
                    for part in range(2):
                        pool.wait_ge(made, n)
                        nc.gpsimd.affine_select(out=t[:, :, :], in_=t[:, :, :], compare_op=ALU.not_equal, fill=1.0, base=-part * E,
                                                pattern=[[-1, E], [0, P]], channel_multiplier=1).then_inc(made, 1)
                        n += 1

            @block.vector
            def _(dve):
                dve.wait_ge(made, 14)
                for t, s in zip(raw, (sel0, sel1)):
                    nc.vector.tensor_copy(s[:, :, :], t[:, :, :]).then_inc(cast, 1)


def transformer(nc, a, out):
    scr = lambda n, s: nc.dram_tensor(n, s, F32, kind="Internal").ap()
    q0, k0 = (scr(n, [2, BATCH, P, SEQ]) for n in ("scr_q0", "scr_k0"))
    v0 = scr("scr_v0", [BATCH, 4, P, TPB, 36])
    q1, k1 = scr("scr_q1", [2, BATCH, 512, SEQ]), scr("scr_k1", [2, BATCH, 32, SEQ])
    v1 = scr("scr_v1", [BATCH, P, TPB, 33])

    def split_rows(scr, HG, R, parts):
        def load(sp, tile, g, s):
            for n, part in enumerate(parts):
                src = scr[part].rearrange("b c n -> (b c) n")[bass.ds(lin(g, HG * R, 0), HG * R), :]
                sp.dma_start(tile[n * R:(n + 1) * R, :, :].bitcast(F32), src.rearrange("(h r) n -> r h n", h=HG)).then_inc(s, 16)
        return load

    def load_v0(sp, tile, g, s):
        src = v0.rearrange("b g p t c -> (b g) p t c")[bass.ds(lin(g, 1, 0), 1), :, :, :]
        sp.dma_start(tile[:, :, :, :].rearrange("p t h c -> p t (h c)"), src.rearrange("g p t c -> (g p) t c")).then_inc(s, 16)

    def batch_of(g):
        return g[0] // 4

    def load_k1(sp, tile, g, s):
        for n, part in enumerate((0, 1, 0)):
            src = k1[part, bass.ds(batch_of(g), 1), :, :].rearrange("b c n -> (b c) n")
            sp.dma_start(tile[n * 32:(n + 1) * 32, 0, :].bitcast(F32), src).then_inc(s, 16)

    def load_v1(sp, tile, g, s):
        src = v1[bass.ds(batch_of(g), 1), :, :, :].rearrange("b p t c -> (b p) t c")
        sp.dma_start(tile[:, :, 0, :], src).then_inc(s, 16)

    def load_x(sp, loaded):
        xt = a["L0_attn_x"].rearrange("(t p) d -> p t d", p=P)
        for half in range(2):
            rows = slice(half * TILES // 2, (half + 1) * TILES // 2)
            sp.dma_start(k.x[:, rows, :], xt[:, rows, :]).then_inc(loaded, 16)

    with ExitStack() as ctx:
        k = Shared(nc, ctx)
        sb = lambda c, n, s, d=F32: c.enter_context(nc.sbuf_tensor(n, s, d))
        sel0, sel1 = sb(ctx, "sel0", [16, 8, P], F32R), sb(ctx, "sel1", [32, 16, P], F32R)
        constants(k, sel0, sel1)

        ln_stats(k, "ln0", load_x)
        project_0(k, a["L0_attn_q_heads"], a["L0_attn_k_heads"], a["L0_attn_v_heads"], q0, k0, v0)
        with ExitStack() as c:
            attn = sb(c, "attn0", [P, 16, TPB, 32])
            attention(k, "a0", 4, 8, 8, 8.0 ** -0.5, split_rows(q0, 4, 8, (0, 0, 1)), split_rows(k0, 4, 8, (0, 1, 0)),
                      load_v0, False, attn)
            w_o = sb(c, "w_o", [P, 1, D])
            load_weights(k, "wo_ld", w_o[:, 0, :], a["L0_attn_output_proj"])
            project_out(k, "o0", attn, w_o, 4)
        ln_stats(k, "ln1")
        with ExitStack() as c:
            xnT, gateT = sb(c, "xnT0", [P, TOK]), sb(c, "gateT0", [16, TOK], F32R)
            route(k, "r0", 8, 2, a["L0_ffn_Wr"], None, xnT, gateT)
            moe_0(k, a["Wfc"], a["bfc"], a["Wproj"], a["L0_ffn_bproj"], a["L0_ffn_bproj_s"], xnT, gateT, sel0)
        ln_stats(k, "ln2")
        with ExitStack() as c:
            a_v = sb(c, "a_v", [P, 4, D])
            with ExitStack() as c1:
                a_q = sb(c1, "a_q", [P, 512])
                absorb(k, a["L1_attn_Wq"], a["L1_attn_Wk_up"], a["L1_attn_Wv_up"], a["L1_attn_Wout"], a_q, a_v)
                project_1(k, a_q, a["L1_attn_Wkv_down"], q1, k1, v1)
            attn = sb(c, "attn1", [P, 32, TPB, 64])
            attention(k, "a1", 2, 32, 32, 64.0 ** -0.5, split_rows(q1, 2, 32, (0, 0, 1)), load_k1, load_v1, True, attn)
            project_out(k, "o1", attn, a_v, 8)
        ln_stats(k, "ln3")
        with ExitStack() as c:
            xnT, gateT = sb(c, "xnT1", [P, TOK]), sb(c, "gateT1", [32, TOK], F32R)
            route(k, "r1", 16, 8, a["L1_ffn_gate_w"], a["L1_ffn_expert_bias"], xnT, gateT)
            moe_1(k, a["w_gate"], a["w_up"], a["w_down"], xnT, gateT, sel1, out)


def load_weights(k, name, dst, src):
    loaded = k.sem(name)
    with k.nc.Block() as block:
        @block.sync
        def _(sp):
            sp.dma_start(dst, src).then_inc(loaded, 16)
            sp.wait_ge(loaded, 16)


def kernel(**inputs):
    import numpy as np
    import concourse.bacc as bacc
    from concourse.bass_utils import run_bass_kernel_spmd

    t = {n: np.asarray(v) for n, v in inputs.items()}
    arrays = {
        "L0_attn_x": t["L0_attn_x"].reshape(TOK, D),
        "L0_attn_q_heads": t["L0_attn_q_heads"].T, "L0_attn_k_heads": t["L0_attn_k_heads"].T,
        "L0_attn_v_heads": t["L0_attn_v_heads"].T, "L0_attn_output_proj": t["L0_attn_output_proj"].T,
        "L0_ffn_Wr": t["L0_ffn_Wr"],
        "Wfc": np.concatenate([t["L0_ffn_Wfc_s"][None], t["L0_ffn_Wfc"]]).transpose(1, 0, 2),
        "bfc": np.concatenate([t["L0_ffn_bfc_s"][None], t["L0_ffn_bfc"]]).reshape(36, P).T,
        "Wproj": np.concatenate([t["L0_ffn_Wproj_s"][None], t["L0_ffn_Wproj"]]).reshape(9, 4, P, D).transpose(2, 0, 1, 3),
        "L0_ffn_bproj": t["L0_ffn_bproj"], "L0_ffn_bproj_s": t["L0_ffn_bproj_s"].reshape(D, 1),
        "L1_attn_Wq": t["L1_attn_Wq"].transpose(2, 1, 0), "L1_attn_Wkv_down": t["L1_attn_Wkv_down"],
        "L1_attn_Wk_up": t["L1_attn_Wk_up"].transpose(2, 1, 0), "L1_attn_Wv_up": t["L1_attn_Wv_up"].transpose(2, 1, 0),
        "L1_attn_Wout": t["L1_attn_Wout"].transpose(1, 0, 2),
        "L1_ffn_gate_w": t["L1_ffn_gate_w"].T, "L1_ffn_expert_bias": t["L1_ffn_expert_bias"],
        "w_gate": np.concatenate([t["L1_ffn_w_gate"], t["L1_ffn_shared_gate_w"][None]]).transpose(2, 0, 1),
        "w_up": np.concatenate([t["L1_ffn_w_up"], t["L1_ffn_shared_up_w"][None]]).transpose(2, 0, 1),
        "w_down": np.concatenate([t["L1_ffn_w_down"], t["L1_ffn_shared_down_w"][None]]).transpose(2, 0, 1),
    }
    arrays = {n: np.ascontiguousarray(v) for n, v in arrays.items()}
    nc = bacc.Bacc("TRN2", target_bir_lowering=False, num_devices=1)
    aps = {n: nc.dram_tensor(n, v.shape, mybir.dt.from_np(v.dtype), kind="ExternalInput").ap() for n, v in arrays.items()}
    out = nc.dram_tensor("out", [TOK, D], F32, kind="ExternalOutput").ap()
    transformer(nc, aps, out)
    r = run_bass_kernel_spmd(nc, [arrays], core_ids=[0])
    return r.results[0]["out"].reshape(BATCH, SEQ, D)
```

```python
from contextlib import ExitStack

import concourse.bass as bass
from concourse import mybir

F32 = mybir.dt.float32
F32R = mybir.dt.float32r
BF16 = mybir.dt.bfloat16
ALU = mybir.AluOpType
ACT = mybir.ActivationFunctionType
AXX = mybir.AxisListType.X

P = 128
D = 128
BATCH, SEQ = 4, 1024
TOK = BATCH * SEQ
TILES = TOK // P
ST = 512
NST = TOK // ST
TPS = ST // P
TPB = SEQ // P
HEADS = 16
EPS = 1e-5
MASKED = -1e30

ROUTE_SCALE = 2.826


def lin(g, a, c):
    u, par = g
    return u * (2 * a) + (par * a + c)


def rounds(eng, n):
    yield 0
    with eng.Fori(1, n) as u:
        yield u


def wait_past(eng, sem, value):
    if not isinstance(value, int) or value > 0:
        eng.wait_ge(sem, value)


def pipelined(eng, n, front, back):
    def round_(u, more):
        front((u, 1))
        back((u, 0))
        if more:
            front((u + 1, 0))
        back((u, 1))

    front((0, 0))
    round_(0, True)
    with eng.Fori(1, n - 1) as u:
        round_(u, True)
    round_(n - 1, False)


class Shared:

    def __init__(self, nc, ctx):
        self.nc, self.ctx = nc, ctx
        sb = lambda n, s, d: ctx.enter_context(nc.sbuf_tensor(n, s, d))
        self.ident, self.ident_bf = sb("ident", [P, P], F32), sb("ident_bf", [P, P], BF16)
        self.mask_q = sb("mask_q", [P, P], BF16)
        self.x = sb("x", [P, TILES, D], F32)
        self.stats = sb("stats", [P, TILES, 6], F32)
        self.mean, self.rstd, self.tmp = (sb(n, [P, TILES], F32) for n in ("mean", "rstd", "dev"))

    def sem(self, name):
        return self.ctx.enter_context(self.nc.semaphore(name))


def causal_pieces():
    full, partial = [], []
    for j in range(TPB):
        for half in range(SEQ // ST):
            q0, q1 = max(j * P, half * ST), (half + 1) * ST
            if q0 < q1:
                (full if q1 - q0 == ST else partial).append((j, q0, q1))
    pairs = []
    while partial:
        seg = partial.pop(0)
        mate = next(s for s in partial if s[2] - s[1] + seg[2] - seg[1] == ST)
        partial.remove(mate)
        pairs.append([seg, mate])
    plain = [[seg] for seg in full if seg[0] * P != seg[1]]
    first, last = [[seg] for seg in full if seg[0] * P == seg[1]]
    pieces = [first]
    for pair in pairs:
        pieces += [plain.pop(0), pair]
    return pieces + [last] + plain


PIECES = causal_pieces()
NP = len(PIECES)


def ln_stats(k, name, load=None):
    nc, sem = k.nc, k.sem
    combined, std_ready = sem(name + "_comb"), sem(name + "_std")
    x_loaded = sem(name + "_xld") if load is not None else None
    st = k.stats
    with nc.Block() as block:
        if load is not None:
            @block.sync
            def _(sp):
                load(sp, x_loaded)

        @block.vector
        def _(dve):
            if load is not None:
                dve.wait_ge(x_loaded, 16 * 2)
            with dve.Fori(0, TILES // 4) as u:
                for t in range(4):
                    last = nc.vector.bn_stats(st[:, bass.ds(u * 4 + t, 1), :].rearrange("p o s -> p (o s)"),
                                              k.x[:, bass.ds(u * 4 + t, 1), :].rearrange("p o d -> p (o d)"))
                    last.then_inc(combined, 1)
            dve.wait_ge(combined, TILES)
            n = [TILES]

            def link(ins):
                n[0] += 1
                ins.then_inc(combined, 1)
                dve.wait_ge(combined, n[0])

            mean_e, m2_e, mean_o, m2_o = (st[:, :, i] for i in (1, 2, 4, 5))
            nc.vector.tensor_tensor(k.mean[:, :], mean_e, mean_o, ALU.add).then_inc(combined, 1)
            nc.vector.tensor_tensor(k.tmp[:, :], mean_e, mean_o, ALU.subtract).then_inc(combined, 1)
            nc.vector.tensor_tensor(k.rstd[:, :], m2_e, m2_o, ALU.add).then_inc(combined, 1)
            n[0] += 3
            dve.wait_ge(combined, n[0])
            nc.vector.tensor_scalar(k.mean[:, :], k.mean[:, :], 0.5, None, ALU.mult).then_inc(combined, 1)
            n[0] += 1
            link(nc.vector.tensor_tensor(k.tmp[:, :], k.tmp[:, :], k.tmp[:, :], ALU.mult))
            link(nc.vector.scalar_tensor_tensor(k.rstd[:, :], k.tmp[:, :], D / 4.0, k.rstd[:, :], ALU.mult, ALU.add))
            link(nc.vector.tensor_scalar(k.rstd[:, :], k.rstd[:, :], 1.0 / D, EPS, ALU.mult, ALU.add))
            dve.wait_ge(std_ready, 1)
            link(nc.vector.reciprocal(k.rstd[:, :], k.rstd[:, :]))

        @block.scalar
        def _(act):
            act.wait_ge(combined, TILES + 7)
            nc.scalar.activation(k.rstd[:, :], k.rstd[:, :], ACT.Sqrt).then_inc(std_ready, 1)


def normalise(k, dve, xn, g, ready):
    for t in range(TPS):
        tile = lin(g, TPS, t)
        last = nc_ts(k, xn[:, t, :], tile)
    last.then_inc(ready, 1)


def nc_ts(k, out, tile):
    one = bass.ds(tile, 1)
    return k.nc.vector.tensor_scalar(out, k.x[:, one, :].rearrange("p o d -> p (o d)"), k.mean[:, one], k.rstd[:, one],
                                     ALU.subtract, ALU.mult)


def project_0(k, w_q, w_k, w_v, scr_q, scr_k, scr_v):
    nc, sem = k.nc, k.sem
    VW = 9
    with ExitStack() as c:
        sb = lambda n, s, d: c.enter_context(nc.sbuf_tensor(n, s, d))
        pb = lambda n: c.enter_context(nc.psum_tensor(n, [P, ST], F32))
        wq, wk, wv = sb("p0_wq", [P, D], F32), sb("p0_wk", [P, D], F32), sb("p0_wv", [P, D], F32)
        xn = [sb(f"p0_xn{i}", [P, TPS, D], F32) for i in range(2)]
        xnT = [sb(f"p0_xnT{i}", [P, ST], F32) for i in range(2)]
        hi = [[sb(f"p0_hi{i}{n}", [P, ST], F32R) for n in "qk"] for i in range(2)]
        lo = [[sb(f"p0_lo{i}{n}", [P, ST], F32R) for n in "qk"] for i in range(2)]
        v1 = [sb(f"p0_v{i}", [P, TPS, HEADS, VW], F32) for i in range(2)]
        xT_ps = [pb(f"p0_xT{i}") for i in range(2)]
        qk_ps = [[pb(f"p0_ps{i}{n}") for n in "qk"] for i in range(2)]
        v_ps = [pb(f"p0_psv{i}") for i in range(2)]
        loaded, ones, xn_ready, xT_done, xnT_ready = (sem("p0_" + n) for n in ("ld", "ones", "xn", "xT", "xnT"))
        q_done, k_done, v_done, hi_ready, lo_ready, v_ready = (sem("p0_" + n) for n in ("q", "k", "v", "hi", "lo", "vr"))
        stored = [sem(f"p0_st{i}") for i in range(2)]
        NSTORE = 8
        with nc.Block() as block:
            @block.sync
            def _(sp):
                for dst, src in ((wq, w_q), (wk, w_k), (wv, w_v)):
                    sp.dma_start(dst[:, :], src).then_inc(loaded, 16)
                for u in rounds(sp, NST // 2):
                    for par in range(2):
                        g = (u, par)
                        cols = slice(par * ST, (par + 1) * ST)
                        for n, scr in enumerate((scr_q, scr_k)):
                            sp.wait_ge(hi_ready, lin(g, 2, n + 1))
                            sp.wait_ge(lo_ready, lin(g, 2, n + 1))
                            for part, tile in ((0, hi[par][n]), (1, lo[par][n])):
                                sp.dma_start(scr[part, bass.ds(u, 1), :, cols].rearrange("b c n -> (b c) n"),
                                             tile[:, :].bitcast(F32)).then_inc(stored[par], 16)
                        sp.wait_ge(v_ready, lin(g, 1, 1))
                        for hg in range(4):
                            sp.dma_start(scr_v[bass.ds(u, 1), hg, :, par * TPS:(par + 1) * TPS, :]
                                         .rearrange("b p t c -> (b p) t c"),
                                         v1[par][:, :, hg * 4:hg * 4 + 4, :].rearrange("p t h c -> p t (h c)"))\
                                .then_inc(stored[par], 16)
                for par in range(2):
                    sp.wait_ge(stored[par], 16 * NSTORE * (NST // 2))

            @block.gpsimd
            def _(pool):
                for i in range(2):
                    nc.gpsimd.memset(v1[i][:, :, :, :], 1.0).then_inc(ones, 1)

            @block.vector
            def _(dve):
                for u in rounds(dve, NST // 2):
                    for par in range(2):
                        g = (u, par)
                        wait_past(dve, xT_done, u * 2)
                        normalise(k, dve, xn[par], g, xn_ready)
                        wait_past(dve, stored[par], 16 * NSTORE * u)
                        for n in range(2):
                            dve.wait_ge(hi_ready, lin(g, 2, n + 1))
                            nc.vector.tensor_tensor(lo[par][n][:, :], qk_ps[par][n][:, :], hi[par][n][:, :].bitcast(F32),
                                                    ALU.subtract).then_inc(lo_ready, 1)

            @block.scalar
            def _(act):
                act.wait_ge(ones, 2)
                for u in rounds(act, NST // 2):
                    for par in range(2):
                        g = (u, par)
                        act.wait_ge(xT_done, lin(g, 1, 1))
                        nc.scalar.copy(xnT[par][:, :], xT_ps[par][:, :]).then_inc(xnT_ready, 1)
                        wait_past(act, stored[par], 16 * NSTORE * u)
                        for n, done in enumerate((q_done, k_done)):
                            act.wait_ge(done, lin(g, 1, 1))
                            nc.scalar.copy(hi[par][n][:, :], qk_ps[par][n][:, :]).then_inc(hi_ready, 1)
                        act.wait_ge(v_done, lin(g, 1, 1))
                        nc.scalar.copy(v1[par][:, :, :, 0:VW - 1],
                                       v_ps[par][:, :].rearrange("p (t h c) -> p t h c", t=TPS, h=HEADS)).then_inc(v_ready, 1)

            @block.tensor
            def _(pe):
                pe.wait_ge(loaded, 48)
                for u in rounds(pe, NST // 2):
                    for par in range(2):
                        g = (u, par)
                        pe.wait_ge(xn_ready, lin(g, 1, 1))
                        for t in range(TPS):
                            last = nc.tensor.transpose(xT_ps[par][:, t * P:(t + 1) * P], xn[par][:, t, :], k.ident[:, :])
                        last.then_inc(xT_done, 1)
                        pe.wait_ge(xnT_ready, lin(g, 1, 1))
                        wait_past(pe, lo_ready, 4 * u)
                        nc.tensor.matmul(qk_ps[par][0][:, :], wq[:, :], xnT[par][:, :], start=True, stop=True).then_inc(q_done, 1)
                        nc.tensor.matmul(qk_ps[par][1][:, :], wk[:, :], xnT[par][:, :], start=True, stop=True).then_inc(k_done, 1)
                        wait_past(pe, v_ready, 2 * u)
                        for t in range(TPS):
                            last = nc.tensor.matmul(v_ps[par][:, t * D:(t + 1) * D], xnT[par][:, t * P:(t + 1) * P], wv[:, :],
                                                    start=True, stop=True)
                        last.then_inc(v_done, 1)


def attention(k, name, HG, R, VD, scale, load_q, load_k, load_v, shared_k, out):
    nc, sem = k.nc, k.sem
    NG = BATCH * HEADS // HG
    CT = P // HG
    VW = VD + 1
    MROW = 96
    KH = 1 if shared_k else HG
    KI = (lambda h: 0) if shared_k else (lambda h: h)
    NSLOT = NP * HG
    NLOAD = 6
    LEAD = 6
    BLOCKS = [b for pair in zip(reversed(range(TPB // 2, TPB)), range(TPB // 2)) for b in pair]
    PBUF = 3
    assert NP % PBUF == 0
    DIAGONALS = [[(off, seg) for off, seg in zip((0, p[0][2] - p[0][1]), p) if seg[1] == seg[0] * P] for p in PIECES]
    NDIAG = [sum(1 + len(d) for d in DIAGONALS[:p + 1] if d) for p in range(NP)]
    PER_MASK = NDIAG[-1]

    chain = []
    for h in range(HG):
        blocks = [("S", h, i) for i in BLOCKS]
        chain += blocks[:2] + ([("m", h - 1, 0)] if h else []) + blocks[2:]
    chain.append(("m", HG - 1, 0))
    S_ORDER = {u: n for n, u in enumerate(x for x in chain if x[0] == "S")}
    NU = len(chain)
    start_units = [(*x, 0) for x in chain] + [(*x, 1) for x in chain[:LEAD]]
    own = [(*x, 1) for x in chain[LEAD:]]
    base_units = own + [(*x, 2) for x in chain[:LEAD]]

    DELAY, PARTS = 2, HG // 2
    VALUES, CARRIED = ({s: [] for s in range(NSLOT)} for _ in range(2))
    for p in range(NP):
        for part in range(PARTS):
            s = p * HG + HG - 1 + DELAY + part * (HG // PARTS)
            (VALUES[s] if s < NSLOT else CARRIED[s - NSLOT]).append((p, part))
    parts = {}
    for p, piece in enumerate(PIECES):
        off = 0
        for seg in piece:
            for part in range(PARTS):
                c0, c1 = max(off, part * (ST // PARTS)), min(off + seg[2] - seg[1], (part + 1) * (ST // PARTS))
                if c0 < c1:
                    parts.setdefault((p, part), []).append((seg, c0, seg[1] + c0 - off, seg[1] + c1 - off))
            off += seg[2] - seg[1]
    LAST_OF_BANK = [max(p for p, piece in enumerate(PIECES) if any(s[1] // ST == b for s in piece)) for b in range(2)]
    COPY_0 = next(s for s in VALUES if (LAST_OF_BANK[0], PARTS - 1) in VALUES[s]) + 1
    COPY_1 = max(s for s in CARRIED if CARRIED[s]) + 1
    OUT_AT = COPY_1 + 2
    with_out = base_units[:OUT_AT] + [("o", 0, 0, -1)] + base_units[OUT_AT:]

    with ExitStack() as c:
        sb = lambda n, s, d: c.enter_context(nc.sbuf_tensor(name + n, s, d))
        qS = [sb(f"qS{i}", [P, HG, SEQ], F32R) for i in range(2)]
        kS = [sb(f"kS{i}", [P, KH, SEQ], F32R) for i in range(2)]
        qT = [sb(f"qT{i}", [P, HG, SEQ], F32R) for i in range(2)]
        kT = [sb(f"kT{i}", [P, KH, SEQ], F32R) for i in range(2)]
        vst = [sb(f"v{i}", [P, TPB, KH, VW], F32) for i in range(2)]
        prob = [sb(f"p{i}", [P, HG, ST], F32) for i in range(PBUF)]
        mneg = [sb(f"m{i}", [P, HG, TPB], F32) for i in range(2)]
        mrow = [sb(f"mr{i}", [TPB, HG, P], F32R) for i in range(2)]
        osb = sb("o", [P, SEQ], F32)
        rec = [sb(f"rec{i}", [P, TPB, HG], F32) for i in range(2)]
        zero = sb("zero", [P, ST], BF16)
        held = sb("held", [P, NP], F32)
        one = osb
        s_ps = [c.enter_context(nc.psum_tensor(name + f"S{i}", [P, SEQ], F32)) for i in range(2)]
        t_ps = [c.enter_context(nc.psum_tensor(name + f"T{i}", [P, ST], F32)) for i in range(2)]
        o_ps = c.enter_context(nc.psum_tensor(name + "O", [P, SEQ], F32))
        init, one_set, unit_ready, red_done, mcopy_done, out_done = (
            sem(name + n) for n in ("init", "one", "unit", "red", "mc", "out"))
        st_ready, exp_done, masked, pv_done, o_copied, rec_done = (
            sem(name + n) for n in ("st", "exp", "mask", "pv", "oc", "rec"))
        ldS = [sem(name + f"ldS{i}") for i in range(2)]
        ldT = [sem(name + f"ldT{i}") for i in range(2)]
        row_set = [[sem(name + f"row{i}{h}") for h in range(HG)] for i in range(2)]

        def after(g, n):
            u, par = g
            return (u + (par + n) // 2, (par + n) % 2)

        def at(g, step):
            return isinstance(g[0], int) and lin(g, 1, 0) == step

        def unit_base(g):
            return NU + LEAD if at(g, 0) else lin(g, NU + 1, NU - 1 + (0 if at(g, NG - 1) else LEAD))

        def unit_slot(g):
            return (LEAD + (g[1] if at(g, 0) else g[1] + 1)) % 2

        def units_of(g):
            if at(g, NG - 1):
                return [("o", 0, 0, -1)]
            if at(g, NG - 2):
                return own[:OUT_AT] + [("o", 0, 0, -1)] + own[OUT_AT:]
            return base_units if at(g, 0) else with_out

        def before(g):
            units = start_units if at(g, 0) else own if at(g, NG - 1) else base_units
            shift = 0 if at(g, 0) else -1
            return [(x[0], x[1], x[2], x[3] + shift) for x in units[-2:]]

        def beside(units, slot):
            if len(units) == 1:
                return range(slot == OUT_AT)
            return range(min(slot, len(units)), min(slot + 1, len(units)) if slot < NSLOT - 1 else len(units))

        def main_steps(eng, step):
            step((0, 0))
            step((0, 1))
            with eng.Fori(1, NG // 2 - 1) as u:
                step((u, 0))
                step((u, 1))
            step((NG // 2 - 1, 0))
            step((NG // 2 - 1, 1))

        END = (NG // 2 - 1, 1)

        with nc.Block() as block:
            @block.sync
            def _(sp):
                sp.wait_ge(init, 2 * 4)

                def load_S(g):
                    load_q(sp, qS[g[1]], g, ldS[g[1]])
                    load_k(sp, kS[g[1]], g, ldS[g[1]])

                def load_T(g):
                    load_q(sp, qT[g[1]], g, ldT[g[1]])
                    load_k(sp, kT[g[1]], g, ldT[g[1]])
                    load_v(sp, vst[g[1]], g, ldT[g[1]])

                def set_row(g, h):
                    sp.wait_ge(mcopy_done, lin(g, HG, h + 1))
                    sp.dma_start(qT[g[1]][MROW:MROW + 1, h, :].bitcast(F32),
                                 mrow[g[1]][:, h, :].bitcast(F32)).then_inc(row_set[g[1]][h], 16)

                def step(g):
                    if not at(g, 0) and not at(g, NG - 1):
                        sp.wait_ge(pv_done, lin(g, NP, 0))
                        load_T(after(g, 1))
                    if not at(g, NG - 2) and not at(g, NG - 1):
                        sp.wait_ge(red_done, lin(g, TPB * HG, TPB * HG))
                        load_S(after(g, 2))
                    if not at(g, NG - 1):
                        for h in range(HG):
                            set_row(after(g, 1), h)

                load_S((0, 0))
                load_S((0, 1))
                load_T((0, 0))
                load_T((0, 1))
                for h in range(HG):
                    set_row((0, 0), h)
                main_steps(sp, step)

            @block.gpsimd
            def _(pool):
                for t in (*qS, *kS, *qT, *kT):
                    nc.gpsimd.memset(t[:, :, :].bitcast(F32), 0.0).then_inc(init, 1)

                def step(g):
                    for p in range(NP):
                        if not DIAGONALS[p]:
                            continue
                        pool.wait_ge(exp_done, lin(g, NSLOT, (p + 1) * HG))
                        nc.gpsimd.tensor_tensor(held[:, p:p + 1], k.ident[:, 0:1], k.ident[:, 0:1], ALU.add).then_inc(masked, 1)
                        for off, _ in DIAGONALS[p]:
                            block_ = prob[p % PBUF][:, :, off:off + P]
                            nc.gpsimd.affine_select(out=block_, in_=block_, compare_op=ALU.is_ge, fill=0.0, base=0,
                                                    pattern=[[0, HG], [1, P]], channel_multiplier=-1).then_inc(masked, 1)

                main_steps(pool, step)

            @block.vector
            def _(dve):
                nc.vector.memset(one[0:1, :], 1.0).then_inc(one_set, 1)
                nc.vector.memset(zero[:, :], 0.0).then_inc(one_set, 1)
                dve.wait_ge(one_set, 2)
                dve.wait_ge(init, 2 * 4)
                for t in kT:
                    for h in range(KH):
                        nc.vector.tensor_copy(t[MROW:MROW + 1, h, :], one[0:1, :]).then_inc(one_set, 1)

                def consume(units, base, slot, g):
                    for n, (kind, h, i, ahead) in enumerate(units):
                        if kind == "m":
                            continue
                        _, par = after(g, ahead)
                        dve.wait_ge(unit_ready, base + (n + 1))
                        buf = s_ps[(slot + n) % 2]
                        if kind == "S":
                            nc.vector.tensor_reduce(mneg[par][:, h, i:i + 1], buf[:, 0:(i + 1) * P], AXX, ALU.max,
                                                    negate=True).then_inc(red_done, 1)
                        else:
                            gO = after(g, ahead)
                            o = buf[:, :].rearrange("p (i h c) -> p i h c", i=TPB, h=HG)
                            nc.vector.reciprocal(rec[par][:, :, :], o[:, :, :, VD]).then_inc(rec_done, 1)
                            dve.wait_ge(rec_done, lin(gO, 1, 1))
                            nc.vector.tensor_tensor(
                                out[:, bass.ds(lin(gO, 1, 0), 1), :, :].rearrange("p o i (h c) -> p (o i) h c", h=HG),
                                o[:, :, :, 0:VD], rec[par][:, :, :].unsqueeze(3).broadcast_to([P, TPB, HG, VD]),
                                ALU.mult).then_inc(out_done, 1)

                consume(start_units, 0, 0, (0, 0))
                main_steps(dve, lambda g: consume(units_of(g), unit_base(g), unit_slot(g), g))
                consume([("o", 0, 0, 0)], unit_base(END) + 1, unit_slot(END) + 1, END)

            @block.scalar
            def _(act):
                def copy_out(g, bank):
                    act.wait_ge(pv_done, lin(g, NP, LAST_OF_BANK[bank] + 1))
                    if bank == 0 and not at(g, 0):
                        act.wait_ge(out_done, lin(g, 1, 0))
                    cols = slice(bank * ST, (bank + 1) * ST)
                    nc.scalar.copy(osb[:, cols], o_ps[:, cols]).then_inc(o_copied, 1)

                def copy_max(base, slot, n, g, h):
                    act.wait_ge(unit_ready, base + (n + 1))
                    nc.scalar.copy(mrow[g[1]][:, h, :], s_ps[(slot + n) % 2][0:TPB, 0:P]).then_inc(mcopy_done, 1)

                for n, (kind, h, _, ahead) in enumerate(start_units):
                    if kind == "m":
                        copy_max(0, 0, n, (0, 0), h)

                def step(g):
                    units = units_of(g)
                    for p in range(NP):
                        for h in range(HG):
                            slot = p * HG + h
                            act.wait_ge(st_ready, lin(g, NSLOT, slot + 1))
                            if h == 0 and not (at(g, 0) and p < PBUF):
                                act.wait_ge(pv_done, lin(g, NP, p - PBUF + 1))
                            nc.scalar.activation(prob[p % PBUF][:, h, :], t_ps[slot % 2][:, :], ACT.Exp, scale=scale)\
                                .then_inc(exp_done, 1)
                            for n in beside(units, slot):
                                kind, hm, _, ahead = units[n]
                                if kind == "m":
                                    gm = after(g, ahead)
                                    if not at(gm, 1):
                                        act.wait_ge(row_set[gm[1]][hm], gm[0] * 16)
                                    copy_max(unit_base(g), unit_slot(g), n, gm, hm)
                            if slot == COPY_0:
                                copy_out(g, 0)
                            if slot == COPY_1 and not at(g, 0):
                                copy_out(after(g, -1), 1)

                main_steps(act, step)
                copy_out(END, 1)

            @block.tensor
            def _(pe):
                pe.wait_ge(one_set, 2 + 2 * KH)
                for b in range(SEQ // ST):
                    nc.tensor.matmul(o_ps[:, b * ST:(b + 1) * ST], zero[:, 0:P], zero[:, :], start=True, stop=True)

                def unit(units, last_units, base, slot, n, g):
                    kind, h, i, ahead = units[n]
                    gU = after(g, ahead)
                    prev = units[n - 2] if n >= 2 else last_units[n] if last_units else None
                    if prev is not None:
                        gP = after(g, prev[3])
                        if prev[0] == "S":
                            pe.wait_ge(red_done, lin(gP, TPB * HG, S_ORDER[prev[:3]] + 1))
                        elif prev[0] == "m":
                            pe.wait_ge(mcopy_done, lin(gP, HG, prev[1] + 1))
                        else:
                            pe.wait_ge(out_done, lin(gP, 1, 1))
                    buf = s_ps[(slot + n) % 2]
                    if kind == "S":
                        if (h, i) == (0, BLOCKS[0]):
                            pe.wait_ge(ldS[gU[1]], gU[0] * (16 * NLOAD) + 16 * NLOAD)
                        w = (i + 1) * P
                        q = qS[gU[1]][0:MROW, h, i * P:(i + 1) * P]
                        for c0 in range(0, w, ST):
                            c1 = min(c0 + ST, w)
                            nc.tensor.matmul(buf[:, c0:c1], q, kS[gU[1]][0:MROW, KI(h), c0:c1], start=True, stop=c1 < w)
                        last = nc.tensor.matmul(buf[:, i * P:w], k.ident_bf[:, :], k.mask_q[:, :], start=False, stop=True)
                    elif kind == "m":
                        pe.wait_ge(red_done, lin(gU, TPB * HG, S_ORDER[("S", h, BLOCKS[-1])] + 1))
                        last = nc.tensor.transpose(buf[0:TPB, 0:P], mneg[gU[1]][:, h, :], k.ident[:, :])
                    else:
                        pe.wait_ge(o_copied, lin(gU, 2, 2))
                        for b in range(TPB):
                            last = nc.tensor.transpose(buf[:, b * P:(b + 1) * P], osb[:, b * P:(b + 1) * P], k.ident[:, :])
                    last.then_inc(unit_ready, 1)

                for n in range(len(start_units)):
                    unit(start_units, None, 0, 0, n, (0, 0))

                order = [(p, part, *x) for p in range(NP) for part in range(PARTS) for x in parts[p, part]]
                opens = {b: next(x for x in order if x[2][1] // ST == b) for b in range(SEQ // ST)}
                closes = {b: [x for x in order if x[2][1] // ST == b][-1] for b in range(SEQ // ST)}

                def values(g, p, part):
                    if part == 0 and DIAGONALS[p]:
                        pe.wait_ge(masked, lin(g, PER_MASK, NDIAG[p]))
                    elif part == 0:
                        pe.wait_ge(exp_done, lin(g, NSLOT, (p + 1) * HG))
                    if part == 0 and p < SEQ // ST and not at(g, 0):
                        pe.wait_ge(o_copied, lin(g, 2, p - 1))
                    for x in parts[p, part]:
                        seg, off, q0, q1 = x
                        bank = q0 // ST
                        for h in range(HG):
                            last = nc.tensor.matmul(o_ps[h * CT:h * CT + VW, q0:q1], vst[g[1]][:, seg[0], KI(h), :],
                                                    prob[p % PBUF][:, h, off:off + q1 - q0],
                                                    start=opens[bank] == (p, part, *x), stop=closes[bank] == (p, part, *x))
                    if part == PARTS - 1:
                        last.then_inc(pv_done, 1)

                def step(g):
                    units = units_of(g)
                    pe.wait_ge(ldT[g[1]], g[0] * (16 * (NLOAD + 1)) + 16 * (NLOAD + 1))
                    for p in range(NP):
                        for h in range(HG):
                            slot = p * HG + h
                            if p == 0:
                                pe.wait_ge(row_set[g[1]][h], g[0] * 16 + 16)
                            if not (at(g, 0) and slot < 2):
                                pe.wait_ge(exp_done, lin(g, NSLOT, slot - 1))
                            off = 0
                            for j, q0, q1 in PIECES[p]:
                                last = nc.tensor.matmul(t_ps[slot % 2][:, off:off + q1 - q0],
                                                        kT[g[1]][0:MROW + 1, KI(h), j * P:(j + 1) * P],
                                                        qT[g[1]][0:MROW + 1, h, q0:q1], start=True, stop=True)
                                off += q1 - q0
                            last.then_inc(st_ready, 1)
                            for n in beside(units, slot):
                                unit(units, before(g), unit_base(g), unit_slot(g), n, g)
                            if not at(g, 0):
                                for pv, part in CARRIED[slot]:
                                    values(after(g, -1), pv, part)
                            for pv, part in VALUES[slot]:
                                values(g, pv, part)

                main_steps(pe, step)
                for slot in CARRIED:
                    for pv, part in CARRIED[slot]:
                        values(END, pv, part)
                unit([("o", 0, 0, 0)], None, 0, unit_slot(END) + 1, 0, END)


def project_out(k, name, attn, w_out, NHG):
    nc, sem = k.nc, k.sem
    GW = attn.shape[3]
    NC = NHG * GW // P
    with ExitStack() as c:
        sb = lambda n, s, d: c.enter_context(nc.sbuf_tensor(name + n, s, d))
        w = w_out
        stage = [sb(f"st{i}", [P, TPS, NHG * GW], F32) for i in range(2)]
        aT = [sb(f"aT{i}", [P, NC, ST], F32) for i in range(2)]
        aT_ps = [c.enter_context(nc.psum_tensor(name + f"aps{i}", [P, ST], F32)) for i in range(4)]
        y_ps = [c.enter_context(nc.psum_tensor(name + f"y{i}", [P, ST], F32)) for i in range(2)]
        staged, turned, aT_ready, y_ready, added = (sem(name + n) for n in ("sg", "tr", "aT", "y", "add"))
        with nc.Block() as block:
            @block.gpsimd
            def _(pool):
                for u in rounds(pool, NST // 2):
                    for par in range(2):
                        wait_past(pool, turned, u * (2 * NC))
                        for t in range(TPS):
                            last = nc.gpsimd.tensor_copy(
                                stage[par][:, t, :].rearrange("p (g c) -> p g c", g=NHG),
                                attn[:, bass.ds(u * NHG, NHG), par * TPS + t, :])
                            last.then_inc(staged, 1)

            @block.tensor
            def _(pe):
                for u in rounds(pe, NST // 2):
                    for par in range(2):
                        g = (u, par)
                        pe.wait_ge(staged, lin(g, TPS, TPS))
                        for n in range(NC):
                            m = (par * NC + n) % 4
                            if NC == 1:
                                wait_past(pe, aT_ready, u * 2)
                            else:
                                wait_past(pe, aT_ready, lin(g, NC, 0))
                            for t in range(TPS):
                                last = nc.tensor.transpose(aT_ps[m][:, t * P:(t + 1) * P], stage[par][:, t, n * P:(n + 1) * P],
                                                           k.ident[:, :])
                            last.then_inc(turned, 1)
                        pe.wait_ge(aT_ready, lin(g, NC, NC))
                        wait_past(pe, added, u * 2)
                        for t in range(TPS):
                            for n in range(NC):
                                last = nc.tensor.matmul(y_ps[par][:, t * D:(t + 1) * D], aT[par][:, n, t * P:(t + 1) * P],
                                                        w[:, n, :], start=n == 0, stop=n == NC - 1)
                        last.then_inc(y_ready, 1)

            @block.scalar
            def _(act):
                for u in rounds(act, NST // 2):
                    for par in range(2):
                        g = (u, par)
                        wait_past(act, y_ready, u * 2)
                        for n in range(NC):
                            act.wait_ge(turned, lin(g, NC, n + 1))
                            nc.scalar.copy(aT[par][:, n, :], aT_ps[(par * NC + n) % 4][:, :]).then_inc(aT_ready, 1)

            @block.vector
            def _(dve):
                for u in rounds(dve, NST // 2):
                    for par in range(2):
                        g = (u, par)
                        dve.wait_ge(y_ready, lin(g, 1, 1))
                        rows = k.x[:, bass.ds(lin(g, TPS, 0), TPS), :]
                        nc.vector.tensor_tensor(rows, y_ps[par][:, :].rearrange("p (t d) -> p t d", t=TPS), rows,
                                                ALU.add).then_inc(added, 1)


def route(k, name, E, K, w_router, bias_row, xh, xl, gateT, weights, weights_loaded):
    nc, sem = k.nc, k.sem
    PAD = 6 if K == 2 else 0
    LOADED = 16 if bias_row is None else 32
    TAKEN, FILL = (-1.0, 3.0) if K == 2 else (-3e38, 0.0)
    with ExitStack() as c:
        sb = lambda n, s, d: c.enter_context(nc.sbuf_tensor(name + n, s, d))
        pb = lambda n: c.enter_context(nc.psum_tensor(name + n, [P, ST], F32))
        wr = sb("wr", [P, E], F32)
        bias = sb("bias", [P, E], F32)
        xn = [sb(f"xn{i}", [P, TPS, D], F32) for i in range(2)]
        xs = [sb(f"xs{i}", [P, ST], F32) for i in range(2)]
        lg = sb("lg", [P, TILES, E], F32)
        pr = sb("pr", [P, TILES, E + PAD], F32)
        sel = sb("sel", [P, TILES, E], F32)
        top = sb("top", [P, TILES, 8], F32)
        srt = sb("srt", [P, TILES, 8], F32)
        rep = sb("rep", [P, TILES, E + PAD], F32)
        sm = sb("sm", [P, TILES], F32)
        gt = sb("gt", [P, TILES, 2, E], F32)
        hi = sb("hi", [P, TILES, E], F32R)
        xT_ps = [pb(f"xT{i}") for i in range(2)]
        l_ps = [pb(f"l{i}") for i in range(2)]
        g_ps = [pb(f"g{i}") for i in range(2)]
        loaded, filled, xn_ready, xT_done, xs_ready, xh_ready, xl_ready = (
            sem(name + n) for n in ("ld", "fl", "xn", "xT", "xs", "xh", "xl"))
        l_done, lg_ready, shifted, pr_ready, chain, g_done, g_kept, gt_ready, w_split = (
            sem(name + n) for n in ("l", "lg", "sh", "pr", "ch", "gd", "gk", "gt", "ws"))
        with nc.Block() as block:
            @block.sync
            def _(sp):
                sp.dma_start(wr[:, :], w_router).then_inc(loaded, 16)
                if bias_row is not None:
                    sp.dma_start(bias[:, :], bias_row.partition_broadcast(P)).then_inc(loaded, 16)

            @block.tensor
            def _(pe):
                pe.wait_ge(loaded, LOADED)

                def turn(g):
                    pe.wait_ge(xn_ready, lin(g, 1, 1))
                    wait_past(pe, xh_ready, lin(g, 1, -1))
                    for t in range(TPS):
                        last = nc.tensor.transpose(xT_ps[g[1]][:, t * P:(t + 1) * P], xn[g[1]][:, t, :], k.ident[:, :])
                    last.then_inc(xT_done, 1)

                def logits(g):
                    pe.wait_ge(xs_ready, lin(g, 1, 1))
                    wait_past(pe, lg_ready, lin(g, 1, -1))
                    for t in range(TPS):
                        last = nc.tensor.matmul(l_ps[g[1]][:, t * E:(t + 1) * E], xs[g[1]][:, t * P:(t + 1) * P], wr[:, :],
                                                start=True, stop=True)
                    last.then_inc(l_done, 1)

                pipelined(pe, NST // 2, turn, logits)
                pe.wait_ge(gt_ready, 1)
                for s in range(NST):
                    if s >= 2:
                        pe.wait_ge(g_kept, s - 1)
                    for t in range(TPS):
                        last = nc.tensor.transpose(g_ps[s % 2][0:2 * E, t * P:(t + 1) * P],
                                                   gt[:, s * TPS + t, :, :].rearrange("p a e -> p (a e)"), k.ident[:, :])
                    last.then_inc(g_done, 1)

            @block.scalar
            def _(act):
                def keep(g):
                    act.wait_ge(xT_done, lin(g, 1, 1))
                    wait_past(act, l_done, lin(g, 1, -1))
                    wait_past(act, xl_ready, lin(g, 1, -1))
                    nc.scalar.copy(xs[g[1]][:, :], xT_ps[g[1]][:, :]).then_inc(xs_ready, 1)
                    nc.scalar.copy(xh[:, bass.ds(lin(g, ST, 0), ST)], xT_ps[g[1]][:, :]).then_inc(xh_ready, 1)

                def keep_logits(g):
                    act.wait_ge(l_done, lin(g, 1, 1))
                    nc.scalar.copy(lg[:, bass.ds(lin(g, TPS, 0), TPS), :],
                                   l_ps[g[1]][:, 0:TPS * E].rearrange("p (t e) -> p t e", t=TPS)).then_inc(lg_ready, 1)

                pipelined(act, NST // 2, keep, keep_logits)
                if K == 2:
                    act.wait_ge(filled, 3)
                    act.wait_ge(shifted, 1)
                else:
                    act.wait_ge(lg_ready, NST)
                nc.scalar.activation(pr[:, :, 0:E], lg[:, :, :], ACT.Exp, scale=1.0 if K == 2 else -1.0).then_inc(pr_ready, 1)
                for s in range(NST):
                    act.wait_ge(g_done, s + 1)
                    nc.scalar.copy(gateT[:, s * ST:(s + 1) * ST], g_ps[s % 2][0:2 * E, :]).then_inc(g_kept, 1)

            @block.gpsimd
            def _(pool):
                if K == 2:
                    for t in (pr, top, rep):
                        nc.gpsimd.memset(t[:, :, :], FILL).then_inc(filled, 1)
                for u in rounds(pool, NST // 2):
                    for par in range(2):
                        pool.wait_ge(xh_ready, lin((u, par), 1, 1))
                        cols = bass.ds(lin((u, par), ST, 0), ST)
                        nc.gpsimd.tensor_tensor(xl[:, cols], xs[par][:, :], xh[:, cols].bitcast(F32), ALU.subtract)\
                            .then_inc(xl_ready, 1)
                pool.wait_ge(weights_loaded, 16 * len(weights))
                for raw, w_hi, _ in weights:
                    nc.gpsimd.tensor_copy(w_hi, raw).then_inc(w_split, 1)
                pool.wait_ge(w_split, len(weights))
                for raw, w_hi, w_lo in weights:
                    nc.gpsimd.tensor_tensor(w_lo, raw, w_hi.bitcast(F32), ALU.subtract)

            @block.vector
            def _(dve):
                for u in rounds(dve, NST // 2):
                    for par in range(2):
                        wait_past(dve, xT_done, lin((u, par), 1, -1))
                        normalise(k, dve, xn[par], (u, par), xn_ready)
                dve.wait_ge(loaded, LOADED)
                if K == 2:
                    dve.wait_ge(filled, 3)
                dve.wait_ge(lg_ready, NST)
                count = [0]

                def link(*instructions):
                    for ins in instructions:
                        ins.then_inc(chain, 1)
                    count[0] += len(instructions)
                    dve.wait_ge(chain, count[0])

                wide = lambda a: a.unsqueeze(2).broadcast_to([P, TILES, E])
                s = sm[:, :]
                p = pr[:, :, 0:E]
                if K == 2:
                    link(nc.vector.tensor_reduce(s, lg[:, :, :], AXX, ALU.max))
                    nc.vector.tensor_tensor(lg[:, :, :], lg[:, :, :], wide(s), ALU.subtract).then_inc(shifted, 1)
                    dve.wait_ge(pr_ready, 1)
                    link(*[nc.vector.max(srt[:, t, :], pr[:, t, 0:E]) for t in range(TILES)])
                    link(nc.vector.tensor_copy(top[:, :, 0:K], srt[:, :, 0:K]))
                    values, chosen = pr, p
                else:
                    dve.wait_ge(pr_ready, 1)
                    link(nc.vector.tensor_scalar(p, p, 1.0, None, ALU.add))
                    link(nc.vector.reciprocal(p, p))
                    link(nc.vector.tensor_tensor(sel[:, :, :], p, bias[:, :].unsqueeze(1).broadcast_to([P, TILES, E]), ALU.add))
                    link(*[nc.vector.max(top[:, t, :], sel[:, t, :]) for t in range(TILES)])
                    values, chosen = sel, sel[:, :, :]
                link(*[nc.vector.match_replace(rep[:, t, :], top[:, t, :], values[:, t, :], TAKEN) for t in range(TILES)])
                r = rep[:, :, 0:E]
                link(nc.vector.tensor_tensor(r, r, chosen, ALU.not_equal))
                link(nc.vector.tensor_tensor(r, r, p, ALU.mult))
                link(nc.vector.tensor_reduce(s, r, AXX, ALU.add))
                link(nc.vector.reciprocal(s, s))
                if K != 2:
                    link(nc.vector.tensor_scalar(s, s, ROUTE_SCALE, None, ALU.mult))
                link(nc.vector.tensor_tensor(r, r, wide(s), ALU.mult))
                link(nc.vector.tensor_copy(hi[:, :, :], r))
                link(nc.vector.tensor_copy(gt[:, :, 0, :], hi[:, :, :].bitcast(F32)))
                nc.vector.tensor_tensor(gt[:, :, 1, :], r, hi[:, :, :].bitcast(F32), ALU.subtract).then_inc(gt_ready, 1)


def moe_0(k, b_fc, b_proj, b_proj_s, wf, wp, xh, xl, gateT, sel):
    nc, sem = k.nc, k.sem
    E, NCH = 8, 4
    NE = E + 1
    NH = NE * NCH
    LAG, HBUF = 3, 4
    with ExitStack() as c:
        sb = lambda n, s, d: c.enter_context(nc.sbuf_tensor("m0_" + n, s, d))
        pb = lambda n: c.enter_context(nc.psum_tensor("m0_" + n, [P, ST], F32))
        bfc, bps = sb("bfc", [P, NH], F32), sb("bps", [P, 1], F32)
        bp = sb("bp", [2 * E, D], F32)
        bph, bpl = sb("bph", [2 * E, D], F32R), sb("bpl", [2 * E, D], F32R)
        h = [sb(f"h{i}", [P, ST], F32) for i in range(2)]
        hh = [sb(f"hh{i}", [P, ST], F32R) for i in range(HBUF)]
        hl = [sb(f"hl{i}", [P, ST], F32R) for i in range(HBUF)]
        gb = [sb(f"gb{i}", [P, ST], F32) for i in range(2)]
        prod = [sb(f"pr{i}", [P, ST], F32) for i in range(2)]
        acc = [sb(f"acc{i}", [P, ST], F32) for i in range(2)]
        f_ps = [pb(f"f{i}") for i in range(3)]
        y_ps = [pb(f"y{i}") for i in range(3)]
        b_ps, t_ps = pb("b"), pb("t")
        loaded, split, fc_done, h_ready, hl_ready, y_done = (sem("m0_" + n) for n in ("ld", "sp", "fc", "h", "hl", "y"))
        gb_done, gb_ready, summed, turned, added = (sem("m0_" + n) for n in ("gd", "gb", "sum", "tr", "add"))
        NSUM = 1 + 2 * E
        READ = lambda e: max(2 * e, 1)
        SUM_AT = lambda e: e * NCH + NCH + LAG
        TURN_AT, ADD_AT = LAG + 3, LAG + 5

        def before(g):
            return (g[0] + (g[1] - 1) // 2, (g[1] - 1) % 2)

        def first(g):
            return isinstance(g[0], int) and g == (0, 0)

        def steps(eng, supertile, tail):
            for u in rounds(eng, NST // 2):
                for par in range(2):
                    supertile((u, par))
            tail((NST // 2 - 1, 1))

        with nc.Block() as block:
            @block.sync
            def _(sp):
                for dst, src in ((bfc[:, :], b_fc), (bps[:, :], b_proj_s), (bp[0:E, :], b_proj), (bp[E:2 * E, :], b_proj)):
                    sp.dma_start(dst, src).then_inc(loaded, 16)

            @block.tensor
            def _(pe):
                def fc(g, n):
                    e, ch = divmod(n, NCH)
                    cols = bass.ds(lin(g, ST, 0), ST)
                    wait_past(pe, h_ready, lin(g, 2 * NH, 2 * (n - 2)))
                    if ch == 2 and e:
                        wait_past(pe, gb_ready, lin(g, E, e - 1))
                    part = slice(ch * P, (ch + 1) * P)
                    nc.tensor.matmul(f_ps[n % 3][:, :], wf[0][:, e, part], xh[:, cols], start=True, stop=False)
                    nc.tensor.matmul(f_ps[n % 3][:, :], wf[0][:, e, part], xl[:, cols], start=False, stop=False)
                    nc.tensor.matmul(f_ps[n % 3][:, :], wf[1][:, e, part], xh[:, cols], start=False, stop=True)\
                        .then_inc(fc_done, 1)
                    if ch == 2 and e:
                        nc.tensor.matmul(b_ps[:, :], sel[:, e - 1:e].broadcast_to([2 * E, P]), gateT[:, cols],
                                         start=True, stop=True).then_inc(gb_done, 1)

                def project(g, n):
                    e, ch = divmod(n, NCH)
                    cols = bass.ds(lin(g, ST, 0), ST)
                    if ch == 0:
                        if e >= 3:
                            pe.wait_ge(summed, lin(g, NSUM, READ(e - 3)))
                        elif not first(g):
                            pe.wait_ge(summed, lin(before(g), NSUM, READ(e - 3 + NE)))
                    pe.wait_ge(hl_ready, lin(g, NH, n + 1))
                    y = y_ps[e % 3][:, :]
                    nc.tensor.matmul(y, wp[0][:, e, ch, :], hh[n % HBUF][:, :], start=ch == 0, stop=False)
                    nc.tensor.matmul(y, wp[0][:, e, ch, :], hl[n % HBUF][:, :], start=False, stop=False)
                    last = nc.tensor.matmul(y, wp[1][:, e, ch, :], hh[n % HBUF][:, :], start=False,
                                            stop=ch == NCH - 1 and e > 0)
                    if ch == NCH - 1:
                        if e == 0:
                            nc.tensor.matmul(y, bph[:, :], gateT[:, cols], start=False, stop=False)
                            last = nc.tensor.matmul(y, bpl[:, :], gateT[:, cols], start=False, stop=True)
                        last.then_inc(y_done, 1)

                def turn(g):
                    pe.wait_ge(summed, lin(g, NSUM, NSUM))
                    wait_past(pe, added, lin(g, 1, 0))
                    for t in range(TPS):
                        last = nc.tensor.transpose(t_ps[:, t * P:(t + 1) * P], acc[g[1]][:, t * P:(t + 1) * P], k.ident[:, :])
                    last.then_inc(turned, 1)

                def supertile(g):
                    for n in range(NH):
                        fc(g, n)
                        if n >= LAG:
                            project(g, n - LAG)
                        elif not first(g):
                            project(before(g), NH - LAG + n)
                        if n == TURN_AT and not first(g):
                            turn(before(g))

                def tail(g):
                    for n in range(NH - LAG, NH):
                        project(g, n)
                    turn(g)

                pe.wait_ge(split, 2)
                steps(pe, supertile, tail)

            @block.scalar
            def _(act):
                def supertile(g):
                    for n in range(NH):
                        e, ch = divmod(n, NCH)
                        act.wait_ge(fc_done, lin(g, NH, n + 1))
                        wait_past(act, hl_ready, lin(g, NH, n - 1))
                        for dst in (h[n % 2], hh[n % HBUF]):
                            nc.scalar.activation(dst[:, :], f_ps[n % 3][:, :], ACT.Gelu_apprx_tanh, bias=bfc[:, n:n + 1])\
                                .then_inc(h_ready, 1)
                        if ch == 2 and e:
                            act.wait_ge(gb_done, lin(g, E, e))
                            if e >= 3:
                                act.wait_ge(summed, lin(g, NSUM, READ(e - 2)))
                            elif not first(g):
                                act.wait_ge(summed, lin(before(g), NSUM, READ(e - 2 + E)))
                            nc.scalar.copy(gb[e % 2][:, :], b_ps[:, :]).then_inc(gb_ready, 1)

                act.wait_ge(loaded, 16 * 4)
                steps(act, supertile, lambda g: None)

            @block.vector
            def _(dve):
                dve.wait_ge(loaded, 16 * 4)
                nc.vector.tensor_copy(bph[:, :], bp[:, :]).then_inc(split, 1)
                dve.wait_ge(split, 1)
                nc.vector.tensor_tensor(bpl[:, :], bp[:, :], bph[:, :].bitcast(F32), ALU.subtract).then_inc(split, 1)

                def sum_up(g, e):
                    a = acc[g[1]][:, :]
                    dve.wait_ge(y_done, lin(g, NE, e + 1))
                    if e == 0:
                        wait_past(dve, turned, lin(g, 1, -1))
                        nc.vector.tensor_scalar(a, y_ps[0][:, :], bps[:, 0:1], None, ALU.add).then_inc(summed, 1)
                        return
                    dve.wait_ge(gb_ready, lin(g, E, e))
                    nc.vector.tensor_tensor(prod[e % 2][:, :], y_ps[e % 3][:, :], gb[e % 2][:, :], ALU.mult).then_inc(summed, 1)
                    dve.wait_ge(summed, lin(g, NSUM, 2 * e))
                    nc.vector.tensor_tensor(a, a, prod[e % 2][:, :], ALU.add).then_inc(summed, 1)

                def add(g):
                    dve.wait_ge(turned, lin(g, 1, 1))
                    rows = k.x[:, bass.ds(lin(g, TPS, 0), TPS), :]
                    nc.vector.tensor_tensor(rows, t_ps[:, :].rearrange("p (t d) -> p t d", t=TPS), rows, ALU.add)\
                        .then_inc(added, 1)

                def end(g, n):
                    for e in range(NE):
                        if SUM_AT(e) == NH + n:
                            sum_up(g, e)
                    if n == ADD_AT:
                        add(g)

                def supertile(g):
                    for n in range(NH):
                        dve.wait_ge(h_ready, lin(g, 2 * NH, 2 * (n + 1)))
                        nc.vector.tensor_tensor(hl[n % HBUF][:, :], h[n % 2][:, :], hh[n % HBUF][:, :].bitcast(F32),
                                                ALU.subtract).then_inc(hl_ready, 1)
                        for e in range(NE):
                            if SUM_AT(e) == n:
                                sum_up(g, e)
                        if not first(g):
                            end(before(g), n)

                steps(dve, supertile, lambda g: [end(g, n) for n in range(ADD_AT + 1)])


def absorb(k, w_qT, w_kT, w_vT, w_out, a_q, a_v):
    nc, sem = k.nc, k.sem
    HD, LD = 64, 32
    HPC = P // LD
    with ExitStack() as c:
        sb = lambda n, s: c.enter_context(nc.sbuf_tensor("ab_" + n, s, F32))
        wq, wk = sb("wq", [HD, HEADS, D]), sb("wk", [HD, HEADS, LD])
        wv, wo = sb("wv", [HD, HEADS, LD]), sb("wo", [HD, HEADS, D])
        q_ps = c.enter_context(nc.psum_tensor("ab_q", [P, ST], F32))
        v_ps = c.enter_context(nc.psum_tensor("ab_v", [P, ST], F32))
        loaded, q_done, v_done, kept = (sem("ab_" + n) for n in ("ld", "q", "v", "kept"))
        with nc.Block() as block:
            @block.sync
            def _(sp):
                for dst, src in ((wq, w_qT), (wk, w_kT), (wv, w_vT), (wo, w_out)):
                    sp.dma_start(dst[:, :, :], src).then_inc(loaded, 16)

            @block.tensor
            def _(pe):
                pe.wait_ge(loaded, 64)
                for h in range(HEADS):
                    last = nc.tensor.matmul(q_ps[:, h * LD:(h + 1) * LD], wq[:, h, :], wk[:, h, :], start=True, stop=True)
                last.then_inc(q_done, 1)
                for h in range(HEADS):
                    n, r = divmod(h, HPC)
                    last = nc.tensor.matmul(v_ps[r * LD:(r + 1) * LD, n * D:(n + 1) * D], wv[:, h, :], wo[:, h, :],
                                            start=True, stop=True)
                last.then_inc(v_done, 1)

            @block.vector
            def _(dve):
                dve.wait_ge(q_done, 1)
                nc.vector.tensor_copy(a_q[:, :], q_ps[:, :]).then_inc(kept, 1)
                dve.wait_ge(v_done, 1)
                nc.vector.tensor_copy(a_v[:, :, :], v_ps[:, :].rearrange("p (n o) -> p n o", o=D)).then_inc(kept, 1)


def project_1(k, a_q, w_kv, scr_q, scr_k, scr_v):
    nc, sem = k.nc, k.sem
    LD = 32
    NC = HEADS * LD // P
    NT = NC + 1
    with ExitStack() as c:
        sb = lambda n, s, d: c.enter_context(nc.sbuf_tensor("p1_" + n, s, d))
        pb = lambda n: c.enter_context(nc.psum_tensor("p1_" + n, [P, ST], F32))
        wkv = sb("wkv", [P, LD], F32)
        xn = [sb(f"xn{i}", [P, TPS, D], F32) for i in range(2)]
        xnT = [sb(f"xnT{i}", [P, ST], F32) for i in range(2)]
        hi = [sb(f"hi{i}", [P, NT, ST], F32R) for i in range(2)]
        lo = [sb(f"lo{i}", [P, NT, ST], F32R) for i in range(2)]
        v1 = [sb(f"v{i}", [P, TPS, LD + 1], F32) for i in range(2)]
        xT_ps = [pb(f"xT{i}") for i in range(2)]
        t_ps = [pb(f"t{i}") for i in range(NT)]
        v_ps = pb("v")
        loaded, ones, xn_ready, xT_done, xnT_ready, t_done, v_done, hi_ready, lo_ready, v_ready = (
            sem("p1_" + n) for n in ("ld", "ones", "xn", "xT", "xnT", "t", "v", "hi", "lo", "vr"))
        stored = [sem(f"p1_st{i}") for i in range(2)]
        NSTORE = 2 * NT + 1
        rows = [P] * NC + [LD]
        with nc.Block() as block:
            @block.sync
            def _(sp):
                sp.dma_start(wkv[:, :], w_kv).then_inc(loaded, 16)
                for u in rounds(sp, NST // 2):
                    for par in range(2):
                        g = (u, par)
                        cols = slice(par * ST, (par + 1) * ST)
                        for n in range(NT):
                            dst = scr_q[:, :, n * P:(n + 1) * P, :] if n < NC else scr_k
                            sp.wait_ge(lo_ready, lin(g, NT, n + 1))
                            for part, tile in ((0, hi[par]), (1, lo[par])):
                                sp.dma_start(dst[part, bass.ds(u, 1), :, cols].rearrange("b c n -> (b c) n"),
                                             tile[0:rows[n], n, :].bitcast(F32)).then_inc(stored[par], 16)
                        sp.wait_ge(v_ready, lin(g, 1, 1))
                        sp.dma_start(scr_v[bass.ds(u, 1), :, par * TPS:(par + 1) * TPS, :].rearrange("b p t c -> (b p) t c"),
                                     v1[par][:, :, :]).then_inc(stored[par], 16)
                for par in range(2):
                    sp.wait_ge(stored[par], 16 * NSTORE * (NST // 2))

            @block.gpsimd
            def _(pool):
                for i in range(2):
                    nc.gpsimd.memset(v1[i][:, :, :], 1.0).then_inc(ones, 1)

            @block.vector
            def _(dve):
                for u in rounds(dve, NST // 2):
                    for par in range(2):
                        g = (u, par)
                        wait_past(dve, xT_done, u * 2)
                        normalise(k, dve, xn[par], g, xn_ready)
                        wait_past(dve, stored[par], u * (16 * NSTORE))
                        for n in range(NT):
                            dve.wait_ge(hi_ready, lin(g, NT, n + 1))
                            nc.vector.tensor_tensor(lo[par][0:rows[n], n, :], t_ps[n][0:rows[n], :],
                                                    hi[par][0:rows[n], n, :].bitcast(F32), ALU.subtract).then_inc(lo_ready, 1)

            @block.scalar
            def _(act):
                act.wait_ge(ones, 2)
                for u in rounds(act, NST // 2):
                    for par in range(2):
                        g = (u, par)
                        act.wait_ge(xT_done, lin(g, 1, 1))
                        nc.scalar.copy(xnT[par][:, :], xT_ps[par][:, :]).then_inc(xnT_ready, 1)
                        wait_past(act, stored[par], u * (16 * NSTORE))
                        for n in range(NT):
                            act.wait_ge(t_done, lin(g, NT, n + 1))
                            nc.scalar.copy(hi[par][0:rows[n], n, :], t_ps[n][0:rows[n], :]).then_inc(hi_ready, 1)
                        act.wait_ge(v_done, lin(g, 1, 1))
                        nc.scalar.copy(v1[par][:, :, 0:LD], v_ps[:, 0:TPS * LD].rearrange("p (t c) -> p t c", t=TPS))\
                            .then_inc(v_ready, 1)

            @block.tensor
            def _(pe):
                pe.wait_ge(loaded, 16)
                for u in rounds(pe, NST // 2):
                    for par in range(2):
                        g = (u, par)
                        pe.wait_ge(xn_ready, lin(g, 1, 1))
                        for t in range(TPS):
                            last = nc.tensor.transpose(xT_ps[par][:, t * P:(t + 1) * P], xn[par][:, t, :], k.ident[:, :])
                        last.then_inc(xT_done, 1)
                        pe.wait_ge(xnT_ready, lin(g, 1, 1))
                        for n in range(NT):
                            wait_past(pe, lo_ready, lin(g, NT, 0) if n == NT - 1 else lin(g, NT, 0))
                            w = a_q[:, n * P:(n + 1) * P] if n < NC else wkv[:, :]
                            nc.tensor.matmul(t_ps[n][0:rows[n], :], w, xnT[par][:, :], start=True, stop=True).then_inc(t_done, 1)
                        wait_past(pe, v_ready, lin(g, 1, 0))
                        for t in range(TPS):
                            last = nc.tensor.matmul(v_ps[:, t * LD:(t + 1) * LD], xnT[par][:, t * P:(t + 1) * P], wkv[:, :],
                                                    start=True, stop=True)
                        last.then_inc(v_done, 1)


def moe_1(k, wg, wu, wd, xh, xl, gateT, sel, out):
    nc, sem = k.nc, k.sem
    E = 16
    NE = E + 1
    LAG, HBUF = 2, 4
    with ExitStack() as c:
        sb = lambda n, s, d: c.enter_context(nc.sbuf_tensor("m1_" + n, s, d))
        pb = lambda n: c.enter_context(nc.psum_tensor("m1_" + n, [P, ST], F32))
        act_g = [sb(f"s{i}", [P, ST], F32) for i in range(2)]
        gb = [sb(f"gb{i}", [P, ST], F32) for i in range(2)]
        ones = sb("one", [P, ST], F32)
        prod = [sb(f"pr{i}", [P, ST], F32) for i in range(2)]
        h = [sb(f"h{i}", [P, ST], F32) for i in range(2)]
        hh = [sb(f"hh{i}", [P, ST], F32R) for i in range(HBUF)]
        hl = [sb(f"hl{i}", [P, ST], F32R) for i in range(HBUF)]
        y = [sb(f"y{i}", [P, ST], F32) for i in range(2)]
        g_ps = [pb(f"g{i}") for i in range(2)]
        u_ps = [pb(f"u{i}") for i in range(2)]
        y_ps = [pb(f"yp{i}") for i in range(2)]
        b_ps, t_ps = pb("b"), pb("t")
        g_done, u_done, gb_done, gb_ready, silu_ready, prod_ready, h_ready, hh_ready, hl_ready, one_set = (
            sem("m1_" + n) for n in ("g", "u", "gd", "gb", "si", "pr", "h", "hh", "hl", "one"))
        down_done, y_kept, turned, added, stored = (sem("m1_" + n) for n in ("yd", "yk", "tr", "add", "st"))
        KEEP_AT, TURN_AT, ADD_AT = LAG + 1, LAG + 2, LAG + 3

        def two(g, e):
            return (g[1] * NE + e) % 2

        def ring(g, e):
            n = g[1] * NE + e
            return 3 if n == 2 * NE - 1 else n % 3

        def before(g):
            return (g[0] + (g[1] - 1) // 2, (g[1] - 1) % 2)

        def first(g):
            return isinstance(g[0], int) and g == (0, 0)

        def steps(eng, supertile, tail):
            for u in rounds(eng, NST // 2):
                for par in range(2):
                    supertile((u, par))
            tail((NST // 2 - 1, 1))

        with nc.Block() as block:
            @block.sync
            def _(sp):
                out_t = out.rearrange("(t p) d -> p t d", p=P)
                with sp.Fori(0, NST) as s:
                    sp.wait_ge(added, s + 1)
                    rows = bass.ds(s * TPS, TPS)
                    sp.dma_start(out_t[:, rows, :], k.x[:, rows, :]).then_inc(stored, 16)
                sp.wait_ge(stored, 16 * NST)

            @block.tensor
            def _(pe):
                def product(bank, w, e, hi, lo, start, stop):
                    nc.tensor.matmul(bank, w[0][:, e, :], hi, start=start, stop=False)
                    nc.tensor.matmul(bank, w[0][:, e, :], lo, start=False, stop=False)
                    return nc.tensor.matmul(bank, w[1][:, e, :], hi, start=False, stop=stop)

                def gate_up(g, e):
                    cols = bass.ds(lin(g, ST, 0), ST)
                    hi, lo = xh[:, cols], xl[:, cols]
                    wait_past(pe, silu_ready, lin(g, NE, e - 1))
                    product(g_ps[two(g, e)][:, :], wg, e, hi, lo, True, True).then_inc(g_done, 1)
                    wait_past(pe, prod_ready, lin(g, NE, e - 1))
                    if e < E:
                        wait_past(pe, gb_ready, lin(g, E, e))
                    product(u_ps[two(g, e)][:, :], wu, e, hi, lo, True, True).then_inc(u_done, 1)
                    if e < E:
                        nc.tensor.matmul(b_ps[:, :], sel[:, e:e + 1].broadcast_to([2 * E, P]), gateT[:, cols],
                                         start=True, stop=True).then_inc(gb_done, 1)

                def down(g, e):
                    pe.wait_ge(hl_ready, lin(g, NE, e + 1))
                    if e == 0:
                        wait_past(pe, y_kept, lin(g, 1, -1))
                    product(y_ps[g[1]][:, :], wd, e, hh[ring(g, e)][:, :], hl[ring(g, e)][:, :], e == 0, e == NE - 1)\
                        .then_inc(down_done, 1)

                def turn(g):
                    pe.wait_ge(y_kept, lin(g, 1, 1))
                    wait_past(pe, added, lin(g, 1, 0))
                    for t in range(TPS):
                        last = nc.tensor.transpose(t_ps[:, t * P:(t + 1) * P], y[g[1]][:, t * P:(t + 1) * P], k.ident[:, :])
                    last.then_inc(turned, 1)

                def supertile(g):
                    for e in range(NE):
                        gate_up(g, e)
                        if e >= LAG:
                            down(g, e - LAG)
                        elif not first(g):
                            down(before(g), NE - LAG + e)
                        if e == TURN_AT and not first(g):
                            turn(before(g))

                def tail(g):
                    for e in range(NE - LAG, NE):
                        down(g, e)
                    turn(g)

                steps(pe, supertile, tail)

            @block.scalar
            def _(act):
                def round_h(g, e):
                    act.wait_ge(h_ready, lin(g, NE, e + 1))
                    wait_past(act, down_done, lin(g, NE, e - 2))
                    nc.scalar.copy(hh[ring(g, e)][:, :], h[two(g, e)][:, :]).then_inc(hh_ready, 1)

                def keep(g):
                    act.wait_ge(down_done, lin(g, NE, NE))
                    wait_past(act, turned, lin(g, 1, -1))
                    nc.scalar.copy(y[g[1]][:, :], y_ps[g[1]][:, :]).then_inc(y_kept, 1)

                def supertile(g):
                    for e in range(NE):
                        act.wait_ge(g_done, lin(g, NE, e + 1))
                        wait_past(act, prod_ready, lin(g, NE, e - 1))
                        nc.scalar.activation(act_g[two(g, e)][:, :], g_ps[two(g, e)][:, :], ACT.Silu).then_inc(silu_ready, 1)
                        if e < E:
                            act.wait_ge(gb_done, lin(g, E, e + 1))
                            wait_past(act, h_ready, lin(g, NE, e - 1))
                            nc.scalar.copy(gb[e % 2][:, :], b_ps[:, :]).then_inc(gb_ready, 1)
                        if e:
                            round_h(g, e - 1)
                        elif not first(g):
                            round_h(before(g), NE - 1)
                        if e == KEEP_AT and not first(g):
                            keep(before(g))

                def tail(g):
                    round_h(g, NE - 1)
                    keep(g)

                steps(act, supertile, tail)

            @block.gpsimd
            def _(pool):
                nc.gpsimd.memset(ones[:, :], 1.0).then_inc(one_set, 1)
                pool.wait_ge(one_set, 1)

                def supertile(g):
                    for e in range(NE):
                        pool.wait_ge(prod_ready, lin(g, NE, e + 1))
                        if e < E:
                            pool.wait_ge(gb_ready, lin(g, E, e + 1))
                        wait_past(pool, hl_ready, lin(g, NE, e - 1))
                        gate = gb[e % 2] if e < E else ones
                        nc.gpsimd.tensor_tensor(h[two(g, e)][:, :], prod[two(g, e)][:, :], gate[:, :], ALU.mult).then_inc(h_ready, 1)

                steps(pool, supertile, lambda g: None)

            @block.vector
            def _(dve):
                def rest(g, e):
                    dve.wait_ge(hh_ready, lin(g, NE, e + 1))
                    nc.vector.tensor_tensor(hl[ring(g, e)][:, :], h[two(g, e)][:, :], hh[ring(g, e)][:, :].bitcast(F32),
                                            ALU.subtract).then_inc(hl_ready, 1)

                def add(g):
                    dve.wait_ge(turned, lin(g, 1, 1))
                    rows = k.x[:, bass.ds(lin(g, TPS, 0), TPS), :]
                    nc.vector.tensor_tensor(rows, t_ps[:, :].rearrange("p (t d) -> p t d", t=TPS), rows, ALU.add)\
                        .then_inc(added, 1)

                def supertile(g):
                    for e in range(NE):
                        dve.wait_ge(silu_ready, lin(g, NE, e + 1))
                        dve.wait_ge(u_done, lin(g, NE, e + 1))
                        wait_past(dve, h_ready, lin(g, NE, e - 1))
                        nc.vector.tensor_tensor(prod[two(g, e)][:, :], u_ps[two(g, e)][:, :], act_g[two(g, e)][:, :], ALU.mult)\
                            .then_inc(prod_ready, 1)
                        if e:
                            rest(g, e - 1)
                        elif not first(g):
                            rest(before(g), NE - 1)
                        if e == ADD_AT and not first(g):
                            add(before(g))

                def tail(g):
                    rest(g, NE - 1)
                    add(g)

                steps(dve, supertile, tail)


def constants(k, sel0, sel1):
    nc, sem = k.nc, k.sem
    made, cast = sem("c_made"), sem("c_cast")
    with ExitStack() as c:
        raw = [c.enter_context(nc.sbuf_tensor(f"c_sel{n}", s.shape, F32)) for n, s in enumerate((sel0, sel1))]
        with nc.Block() as block:
            @block.gpsimd
            def _(pool):
                n = 0
                for t in (k.ident, k.ident_bf, k.mask_q):
                    nc.gpsimd.memset(t[:, :], 0.0).then_inc(made, 1)
                for t in raw:
                    nc.gpsimd.memset(t[:, :], 0.0).then_inc(made, 1)
                n = 5
                pool.wait_ge(made, n)
                for t in (k.ident, k.ident_bf):
                    nc.gpsimd.affine_select(out=t[:, :], in_=t[:, :], compare_op=ALU.not_equal, fill=1.0, base=0,
                                            pattern=[[-1, P]], channel_multiplier=1).then_inc(made, 1)
                nc.gpsimd.affine_select(out=k.mask_q[:, :], in_=k.mask_q[:, :], compare_op=ALU.is_ge, fill=MASKED, base=0,
                                        pattern=[[-1, P]], channel_multiplier=1).then_inc(made, 1)
                n += 3
                for t in raw:
                    E = t.shape[1]
                    for part in range(2):
                        pool.wait_ge(made, n)
                        nc.gpsimd.affine_select(out=t[:, :], in_=t[:, :], compare_op=ALU.not_equal, fill=1.0, base=-part * E,
                                                pattern=[[-1, E]], channel_multiplier=1).then_inc(made, 1)
                        n += 1

            @block.vector
            def _(dve):
                dve.wait_ge(made, 12)
                for t, s in zip(raw, (sel0, sel1)):
                    nc.vector.tensor_copy(s[:, :], t[:, :]).then_inc(cast, 1)


def transformer(nc, a, out):
    scr = lambda n, s: nc.dram_tensor(n, s, F32, kind="Internal").ap()
    q0, k0 = (scr(n, [2, BATCH, P, SEQ]) for n in ("scr_q0", "scr_k0"))
    v0 = scr("scr_v0", [BATCH, 4, P, TPB, 36])
    q1, k1 = scr("scr_q1", [2, BATCH, 512, SEQ]), scr("scr_k1", [2, BATCH, 32, SEQ])
    v1 = scr("scr_v1", [BATCH, P, TPB, 33])

    def split_rows(scr, HG, R, parts):
        def load(sp, tile, g, s):
            for n, part in enumerate(parts):
                src = scr[part].rearrange("b c n -> (b c) n")[bass.ds(lin(g, HG * R, 0), HG * R), :]
                sp.dma_start(tile[n * R:(n + 1) * R, :, :].bitcast(F32), src.rearrange("(h r) n -> r h n", h=HG)).then_inc(s, 16)
        return load

    def load_v0(sp, tile, g, s):
        src = v0.rearrange("b g p t c -> (b g) p t c")[bass.ds(lin(g, 1, 0), 1), :, :, :]
        sp.dma_start(tile[:, :, :, :].rearrange("p t h c -> p t (h c)"), src.rearrange("g p t c -> (g p) t c")).then_inc(s, 16)

    def batch_of(g):
        return g[0] // 4

    def load_k1(sp, tile, g, s):
        for n, part in enumerate((0, 1, 0)):
            src = k1[part, bass.ds(batch_of(g), 1), :, :].rearrange("b c n -> (b c) n")
            sp.dma_start(tile[n * 32:(n + 1) * 32, 0, :].bitcast(F32), src).then_inc(s, 16)

    def load_v1(sp, tile, g, s):
        src = v1[bass.ds(batch_of(g), 1), :, :, :].rearrange("b p t c -> (b p) t c")
        sp.dma_start(tile[:, :, 0, :], src).then_inc(s, 16)

    def load_x(sp, loaded):
        xt = a["L0_attn_x"].rearrange("(t p) d -> p t d", p=P)
        for half in range(2):
            rows = slice(half * TILES // 2, (half + 1) * TILES // 2)
            sp.dma_start(k.x[:, rows, :], xt[:, rows, :]).then_inc(loaded, 16)

    with ExitStack() as ctx:
        k = Shared(nc, ctx)
        sb = lambda c, n, s, d=F32: c.enter_context(nc.sbuf_tensor(n, s, d))
        sel0, sel1 = sb(ctx, "sel0", [16, 8], F32R), sb(ctx, "sel1", [32, 16], F32R)
        constants(k, sel0, sel1)

        ln_stats(k, "ln0", load_x)
        project_0(k, a["L0_attn_q_heads"], a["L0_attn_k_heads"], a["L0_attn_v_heads"], q0, k0, v0)
        with ExitStack() as c:
            attn = sb(c, "attn0", [P, 16, TPB, 32])
            attention(k, "a0", 4, 8, 8, 8.0 ** -0.5, split_rows(q0, 4, 8, (0, 0, 1)), split_rows(k0, 4, 8, (0, 1, 0)),
                      load_v0, False, attn)
            w_o = sb(c, "w_o", [P, 1, D])
            load_weights(k, "wo_ld", w_o[:, 0, :], a["L0_attn_output_proj"])
            project_out(k, "o0", attn, w_o, 4)
        with ExitStack() as c:
            xh, xl = sb(c, "xh0", [P, TOK], F32R), sb(c, "xl0", [P, TOK], F32R)
            gateT = sb(c, "gateT0", [16, TOK], F32R)
            wf = [sb(c, f"wf{i}", [P, 9, 512], F32R) for i in range(2)]
            wp = [sb(c, f"wp{i}", [P, 9, 4, D], F32R) for i in range(2)]
            with ExitStack() as c1:
                raw = sb(c1, "wf_raw", [P, 9, 512]), sb(c1, "wp_raw", [P, 9, 4, D])
                parts = [[t[:, e:e + 3] for t in (r, *w)] for r, w in zip(raw, (wf, wp)) for e in range(0, 9, 3)]
                sources = [w[:, e:e + 3] for w in (a["Wfc"], a["Wproj"]) for e in range(0, 9, 3)]
                w_loaded = load_ahead(k, "w0_ld", [x[0] for x in parts], sources)
                ln_stats(k, "ln1")
                route(k, "r0", 8, 2, a["L0_ffn_Wr"], None, xh, xl, gateT, parts, w_loaded)
            moe_0(k, a["bfc"], a["L0_ffn_bproj"], a["L0_ffn_bproj_s"], wf, wp, xh, xl, gateT, sel0)
        ln_stats(k, "ln2")
        with ExitStack() as c:
            a_v = sb(c, "a_v", [P, 4, D])
            with ExitStack() as c1:
                a_q = sb(c1, "a_q", [P, 512])
                absorb(k, a["L1_attn_Wq"], a["L1_attn_Wk_up"], a["L1_attn_Wv_up"], a["L1_attn_Wout"], a_q, a_v)
                project_1(k, a_q, a["L1_attn_Wkv_down"], q1, k1, v1)
            attn = sb(c, "attn1", [P, 32, TPB, 64])
            attention(k, "a1", 2, 32, 32, 64.0 ** -0.5, split_rows(q1, 2, 32, (0, 0, 1)), load_k1, load_v1, True, attn)
            project_out(k, "o1", attn, a_v, 8)
        with ExitStack() as c:
            xh, xl = sb(c, "xh1", [P, TOK], F32R), sb(c, "xl1", [P, TOK], F32R)
            gateT = sb(c, "gateT1", [32, TOK], F32R)
            w = [[sb(c, f"w{n}{i}", [P, 17, P], F32R) for i in range(2)] for n in "gud"]
            with ExitStack() as c1:
                raw = [sb(c1, f"w{n}_raw", [P, 17, P]) for n in "gud"]
                parts = [[t[:, :, :] for t in (r, *x)] for r, x in zip(raw, w)]
                w_loaded = load_ahead(k, "w1_ld", [x[0] for x in parts], [a[n] for n in ("w_gate", "w_up", "w_down")])
                ln_stats(k, "ln3")
                route(k, "r1", 16, 8, a["L1_ffn_gate_w"], a["L1_ffn_expert_bias"], xh, xl, gateT, parts, w_loaded)
            moe_1(k, *w, xh, xl, gateT, sel1, out)


def load_ahead(k, name, tiles, sources):
    loaded = k.sem(name)
    with k.nc.Block() as block:
        @block.sync
        def _(sp):
            for tile, source in zip(tiles, sources):
                sp.dma_start(tile, source).then_inc(loaded, 16)
    return loaded


def load_weights(k, name, dst, src):
    loaded = k.sem(name)
    with k.nc.Block() as block:
        @block.sync
        def _(sp):
            sp.dma_start(dst, src).then_inc(loaded, 16)
            sp.wait_ge(loaded, 16)


def kernel(**inputs):
    import numpy as np
    import concourse.bacc as bacc
    from concourse.bass_utils import run_bass_kernel_spmd

    t = {n: np.asarray(v) for n, v in inputs.items()}
    arrays = {
        "L0_attn_x": t["L0_attn_x"].reshape(TOK, D),
        "L0_attn_q_heads": t["L0_attn_q_heads"].T, "L0_attn_k_heads": t["L0_attn_k_heads"].T,
        "L0_attn_v_heads": t["L0_attn_v_heads"].T, "L0_attn_output_proj": t["L0_attn_output_proj"].T,
        "L0_ffn_Wr": t["L0_ffn_Wr"],
        "Wfc": np.concatenate([t["L0_ffn_Wfc_s"][None], t["L0_ffn_Wfc"]]).transpose(1, 0, 2),
        "bfc": np.concatenate([t["L0_ffn_bfc_s"][None], t["L0_ffn_bfc"]]).reshape(36, P).T,
        "Wproj": np.concatenate([t["L0_ffn_Wproj_s"][None], t["L0_ffn_Wproj"]]).reshape(9, 4, P, D).transpose(2, 0, 1, 3),
        "L0_ffn_bproj": t["L0_ffn_bproj"], "L0_ffn_bproj_s": t["L0_ffn_bproj_s"].reshape(D, 1),
        "L1_attn_Wq": t["L1_attn_Wq"].transpose(2, 1, 0), "L1_attn_Wkv_down": t["L1_attn_Wkv_down"],
        "L1_attn_Wk_up": t["L1_attn_Wk_up"].transpose(2, 1, 0), "L1_attn_Wv_up": t["L1_attn_Wv_up"].transpose(2, 1, 0),
        "L1_attn_Wout": t["L1_attn_Wout"].transpose(1, 0, 2),
        "L1_ffn_gate_w": t["L1_ffn_gate_w"].T, "L1_ffn_expert_bias": t["L1_ffn_expert_bias"],
        "w_gate": np.concatenate([t["L1_ffn_w_gate"], t["L1_ffn_shared_gate_w"][None]]).transpose(2, 0, 1),
        "w_up": np.concatenate([t["L1_ffn_w_up"], t["L1_ffn_shared_up_w"][None]]).transpose(2, 0, 1),
        "w_down": np.concatenate([t["L1_ffn_w_down"], t["L1_ffn_shared_down_w"][None]]).transpose(2, 0, 1),
    }
    arrays = {n: np.ascontiguousarray(v) for n, v in arrays.items()}
    nc = bacc.Bacc("TRN2", target_bir_lowering=False, num_devices=1)
    aps = {n: nc.dram_tensor(n, v.shape, mybir.dt.from_np(v.dtype), kind="ExternalInput").ap() for n, v in arrays.items()}
    out = nc.dram_tensor("out", [TOK, D], F32, kind="ExternalOutput").ap()
    transformer(nc, aps, out)
    r = run_bass_kernel_spmd(nc, [arrays], core_ids=[0])
    return r.results[0]["out"].reshape(BATCH, SEQ, D)
```

```python
from contextlib import ExitStack

import concourse.bass as bass
from concourse import mybir

F32 = mybir.dt.float32
F32R = mybir.dt.float32r
BF16 = mybir.dt.bfloat16
ALU = mybir.AluOpType
ACT = mybir.ActivationFunctionType
AXX = mybir.AxisListType.X

P = 128
D = 128
BATCH, SEQ = 4, 1024
TOK = BATCH * SEQ
TILES = TOK // P
ST = 512
NST = TOK // ST
TPS = ST // P
TPB = SEQ // P
HEADS = 16
EPS = 1e-5
MASKED = -1e30
NEVER = -3e38

ROUTE_SCALE = 2.826


def lin(g, a, c):
    u, par = g
    return u * (2 * a) + (par * a + c)


def rounds(eng, n):
    yield 0
    with eng.Fori(1, n) as u:
        yield u


def wait_past(eng, sem, value):
    if not isinstance(value, int) or value > 0:
        eng.wait_ge(sem, value)


def pipelined(eng, n, front, back):
    def round_(u, more):
        front((u, 1))
        back((u, 0))
        if more:
            front((u + 1, 0))
        back((u, 1))

    front((0, 0))
    round_(0, True)
    with eng.Fori(1, n - 1) as u:
        round_(u, True)
    round_(n - 1, False)


class Shared:

    def __init__(self, nc, ctx):
        self.nc, self.ctx = nc, ctx
        sb = lambda n, s, d: ctx.enter_context(nc.sbuf_tensor(n, s, d))
        self.ident = sb("ident", [P, P], F32)
        self.mask_q = sb("mask_q", [P, SEQ], BF16)
        self.x = sb("x", [P, TILES, D], F32)
        self.stats = sb("stats", [P, TILES, 6], F32)
        self.mean, self.rstd, self.tmp = (sb(n, [P, TILES], F32) for n in ("mean", "rstd", "dev"))

    def sem(self, name):
        return self.ctx.enter_context(self.nc.semaphore(name))


def causal_pieces():
    full, partial = [], []
    for j in range(TPB):
        for half in range(SEQ // ST):
            q0, q1 = max(j * P, half * ST), (half + 1) * ST
            if q0 < q1:
                (full if q1 - q0 == ST else partial).append((j, q0, q1))
    pairs = []
    while partial:
        seg = partial.pop(0)
        mate = next(s for s in partial if s[2] - s[1] + seg[2] - seg[1] == ST)
        partial.remove(mate)
        pairs.append([seg, mate])
    plain = [[seg] for seg in full if seg[0] * P != seg[1]]
    first, last = [[seg] for seg in full if seg[0] * P == seg[1]]
    pieces = [first]
    for pair in pairs:
        pieces += [plain.pop(0), pair]
    return pieces + [last] + plain


PIECES = causal_pieces()
NP = len(PIECES)


def ln_stats(k, name, x_loaded=None):
    nc, sem = k.nc, k.sem
    combined, std_ready = sem(name + "_comb"), sem(name + "_std")
    st = k.stats
    with nc.Block() as block:
        @block.vector
        def _(dve):
            n = [0]
            if x_loaded is not None:
                dve.wait_ge(x_loaded, 16 * 2)
                with dve.Fori(0, TILES // 8) as u:
                    for t in range(8):
                        one = bass.ds(u * 8 + t, 1)
                        nc.vector.bn_stats(st[:, one, :].rearrange("p o s -> p (o s)"),
                                           k.x[:, one, :].rearrange("p o d -> p (o d)")).then_inc(combined, 1)
                n = [TILES]
                dve.wait_ge(combined, TILES)

            def link(ins):
                n[0] += 1
                ins.then_inc(combined, 1)
                dve.wait_ge(combined, n[0])

            mean_e, m2_e, mean_o, m2_o = (st[:, :, i] for i in (1, 2, 4, 5))
            nc.vector.tensor_tensor(k.mean[:, :], mean_e, mean_o, ALU.add).then_inc(combined, 1)
            nc.vector.tensor_tensor(k.tmp[:, :], mean_e, mean_o, ALU.subtract).then_inc(combined, 1)
            nc.vector.tensor_tensor(k.rstd[:, :], m2_e, m2_o, ALU.add).then_inc(combined, 1)
            n[0] += 3
            dve.wait_ge(combined, n[0])
            nc.vector.tensor_scalar(k.mean[:, :], k.mean[:, :], 0.5, None, ALU.mult).then_inc(combined, 1)
            n[0] += 1
            link(nc.vector.tensor_tensor(k.tmp[:, :], k.tmp[:, :], k.tmp[:, :], ALU.mult))
            link(nc.vector.scalar_tensor_tensor(k.rstd[:, :], k.tmp[:, :], D / 4.0, k.rstd[:, :], ALU.mult, ALU.add))
            link(nc.vector.tensor_scalar(k.rstd[:, :], k.rstd[:, :], 1.0 / D, EPS, ALU.mult, ALU.add))
            dve.wait_ge(std_ready, 1)
            link(nc.vector.reciprocal(k.rstd[:, :], k.rstd[:, :]))

        @block.scalar
        def _(act):
            act.wait_ge(combined, (TILES if x_loaded is not None else 0) + 7)
            nc.scalar.activation(k.rstd[:, :], k.rstd[:, :], ACT.Sqrt).then_inc(std_ready, 1)


def normalise(k, dve, xn, g, ready):
    for t in range(TPS):
        tile = lin(g, TPS, t)
        last = normalise_tile(k, xn[:, t, :], tile)
    last.then_inc(ready, 1)


def tile_stats(k, dve, g, added):
    dve.wait_ge(added, lin(g, 1, 1))
    for t in range(TPS):
        one = bass.ds(lin(g, TPS, t), 1)
        k.nc.vector.bn_stats(k.stats[:, one, :].rearrange("p o s -> p (o s)"), k.x[:, one, :].rearrange("p o d -> p (o d)"))


def normalise_tile(k, out, tile):
    one = bass.ds(tile, 1)
    return k.nc.vector.tensor_scalar(out, k.x[:, one, :].rearrange("p o d -> p (o d)"), k.mean[:, one], k.rstd[:, one],
                                     ALU.subtract, ALU.mult)


class Operands:
    MROW = 96

    def __init__(self, nc, c, name, HG, R, shared_k):
        self.nc, self.R, self.KH = nc, R, 1 if shared_k else HG
        tiles = lambda n, heads: [c.enter_context(nc.sbuf_tensor(f"{name}{n}{i}", [P, heads, SEQ], F32R)) for i in range(2)]
        self.qS, self.kS, self.qT, self.kT = tiles("qS", HG), tiles("kS", self.KH), tiles("qT", HG), tiles("kT", self.KH)

    def prepare(self, pool, done):
        zeroed = (*self.kT, *self.kS, *self.qT, *self.qS) if 3 * self.R < self.MROW else ()
        for t in zeroed:
            self.nc.gpsimd.memset(t[:, :, :].bitcast(F32), 0.0).then_inc(done, 1)
        if zeroed:
            pool.wait_ge(done, len(zeroed))
        for t in self.kT:
            self.nc.gpsimd.memset(t[self.MROW:self.MROW + 1, :, :].bitcast(F32), 1.0).then_inc(done, 1)


def project_0(k, w_q, w_k, w_v, scr_q, scr_k, scr_v, operands):
    nc, sem = k.nc, k.sem
    VW = 9
    with ExitStack() as c:
        sb = lambda n, s, d: c.enter_context(nc.sbuf_tensor(n, s, d))
        pb = lambda n: c.enter_context(nc.psum_tensor(n, [P, ST], F32))
        wq, wk, wv = sb("p0_wq", [P, D], F32), sb("p0_wk", [P, D], F32), sb("p0_wv", [P, D], F32)
        xn = [sb(f"p0_xn{i}", [P, TPS, D], F32) for i in range(2)]
        xnT = [sb(f"p0_xnT{i}", [P, ST], F32) for i in range(2)]
        hi = [[sb(f"p0_hi{i}{n}", [P, ST], F32R) for n in "qk"] for i in range(2)]
        lo = [[sb(f"p0_lo{i}{n}", [P, ST], F32R) for n in "qk"] for i in range(2)]
        v1 = [sb(f"p0_v{i}", [P, TPS * HEADS, VW], F32) for i in range(2)]
        xT_ps = [pb(f"p0_xT{i}") for i in range(2)]
        qk_ps = [[pb(f"p0_ps{i}{n}") for n in "qk"] for i in range(2)]
        v_ps = [pb(f"p0_psv{i}") for i in range(2)]
        loaded, ones, prepared, xn_ready, xT_done, xnT_ready = (sem("p0_" + n) for n in ("ld", "ones", "prep", "xn", "xT", "xnT"))
        q_done, k_done, v_done, hi_ready, lo_ready, v_ready = (sem("p0_" + n) for n in ("q", "k", "v", "hi", "lo", "vr"))
        stored = [sem(f"p0_st{i}") for i in range(2)]
        NSTORE = 5
        with nc.Block() as block:
            @block.sync
            def _(sp):
                for dst, src in ((wq, w_q), (wk, w_k), (wv, w_v)):
                    sp.dma_start(dst[:, :], src).then_inc(loaded, 16)
                for u in rounds(sp, NST // 2):
                    for par in range(2):
                        g = (u, par)
                        cols = slice(par * ST, (par + 1) * ST)
                        for n, scr in enumerate((scr_q, scr_k)):
                            sp.wait_ge(hi_ready, lin(g, 2, n + 1))
                            sp.wait_ge(lo_ready, lin(g, 2, n + 1))
                            for part, tile in ((0, hi[par][n]), (1, lo[par][n])):
                                sp.dma_start(scr[part, bass.ds(u, 1), :, cols].rearrange("b c n -> (b c) n"),
                                             tile[:, :].bitcast(F32)).then_inc(stored[par], 16)
                        sp.wait_ge(v_ready, lin(g, 1, 1))
                        sp.dma_start(scr_v[bass.ds(u, 1), :, :, par * TPS:(par + 1) * TPS, :]
                                     .rearrange("b g p t c -> (b p) g (t c)"),
                                     v1[par][:, :, :].rearrange("p (g n) c -> p g (n c)", g=4)).then_inc(stored[par], 16)
                for par in range(2):
                    sp.wait_ge(stored[par], 16 * NSTORE * (NST // 2))

            @block.gpsimd
            def _(pool):
                for i in range(2):
                    nc.gpsimd.memset(v1[i][:, :, :], 1.0).then_inc(ones, 1)
                pool.wait_ge(ones, 2)
                operands.prepare(pool, prepared)

            @block.vector
            def _(dve):
                def front(g):
                    wait_past(dve, xT_done, lin(g, 1, -1))
                    normalise(k, dve, xn[g[1]], g, xn_ready)

                def back(g):
                    u, par = g
                    wait_past(dve, stored[par], u * (16 * NSTORE))
                    for n in range(2):
                        dve.wait_ge(hi_ready, lin(g, 2, n + 1))
                        nc.vector.tensor_tensor(lo[par][n][:, :], qk_ps[par][n][:, :], hi[par][n][:, :].bitcast(F32),
                                                ALU.subtract).then_inc(lo_ready, 1)

                pipelined(dve, NST // 2, front, back)

            @block.scalar
            def _(act):
                def front(g):
                    act.wait_ge(xT_done, lin(g, 1, 1))
                    nc.scalar.copy(xnT[g[1]][:, :], xT_ps[g[1]][:, :]).then_inc(xnT_ready, 1)

                def back(g):
                    u, par = g
                    wait_past(act, stored[par], u * (16 * NSTORE))
                    for n, done in enumerate((q_done, k_done)):
                        act.wait_ge(done, lin(g, 1, 1))
                        nc.scalar.copy(hi[par][n][:, :], qk_ps[par][n][:, :]).then_inc(hi_ready, 1)
                    act.wait_ge(v_done, lin(g, 1, 1))
                    nc.scalar.copy(v1[par][:, :, 0:VW - 1],
                                   v_ps[par][:, :].rearrange("p (n c) -> p n c", c=VW - 1)).then_inc(v_ready, 1)

                act.wait_ge(ones, 2)
                pipelined(act, NST // 2, front, back)

            @block.tensor
            def _(pe):
                def front(g):
                    par = g[1]
                    pe.wait_ge(xn_ready, lin(g, 1, 1))
                    for t in range(TPS):
                        last = nc.tensor.transpose(xT_ps[par][:, t * P:(t + 1) * P], xn[par][:, t, :], k.ident[:, :])
                    last.then_inc(xT_done, 1)

                def back(g):
                    par = g[1]
                    pe.wait_ge(xnT_ready, lin(g, 1, 1))
                    wait_past(pe, lo_ready, lin(g, 2, -2))
                    nc.tensor.matmul(qk_ps[par][0][:, :], wq[:, :], xnT[par][:, :], start=True, stop=True).then_inc(q_done, 1)
                    nc.tensor.matmul(qk_ps[par][1][:, :], wk[:, :], xnT[par][:, :], start=True, stop=True).then_inc(k_done, 1)
                    wait_past(pe, v_ready, lin(g, 1, -1))
                    for t in range(TPS):
                        by_four = v_ps[par][:, :].rearrange("p (g t c) -> p t g c", g=4, t=TPS)[:, t, :, :]
                        last = nc.tensor.matmul(by_four, xnT[par][:, t * P:(t + 1) * P], wv[:, :], start=True, stop=True)
                    last.then_inc(v_done, 1)

                pe.wait_ge(loaded, 48)
                pipelined(pe, NST // 2, front, back)


def attention(k, name, HG, VD, scale, operands, load_q, load_k, load_v, out):
    nc, sem = k.nc, k.sem
    NG = BATCH * HEADS // HG
    CT = P // HG
    VW = VD + 1
    MROW, KH = operands.MROW, operands.KH
    KI = (lambda h: h) if KH == HG else (lambda h: 0)
    qS, kS, qT, kT = operands.qS, operands.kS, operands.qT, operands.kT
    NSLOT = NP * HG
    NLOAD = 6
    LEAD = 4
    BLOCKS = [b for i in reversed(range(TPB // 2)) for b in (TPB // 2 + i, i)]
    PBUF = 3
    assert NP % PBUF == 0
    DIAGONALS = [[(off, seg) for off, seg in zip((0, p[0][2] - p[0][1]), p) if seg[1] == seg[0] * P] for p in PIECES]
    NDIAG = [sum(1 + len(d) for d in DIAGONALS[:p + 1] if d) for p in range(NP)]
    PER_MASK = NDIAG[-1]

    chain = []
    for h in range(HG):
        blocks = [("S", h, i) for i in BLOCKS]
        chain += blocks[:2] + ([("m", h - 1, 0)] if h else []) + blocks[2:]
    chain.append(("m", HG - 1, 0))

    def units_from(items):
        return [(kind, h, i, half, ahead, min(n, NSLOT - 1)) for n, (kind, h, i, ahead) in enumerate(items)
                for half in range(2 if kind == "o" or kind == "S" and i >= TPB // 2 else 1)]

    MAXIMA, NRED = {}, 0
    for kind, h, i, half, _, _ in units_from([(*x, 0) for x in chain]):
        if kind == "S":
            NRED += 3 if i == BLOCKS[-1] else 2
            MAXIMA[h, i, half] = NRED
    lead, own = [(*x, 0) for x in chain[:LEAD]], [(*x, 1) for x in chain[LEAD:]]
    start_units = units_from([(*x, 0) for x in chain] + [(*x, 1) for x in chain[:LEAD]])
    NLEAD = len(units_from(lead))
    NU = len(start_units) - NLEAD
    START_MAXIMA = NRED + MAXIMA[start_units[-1][1:4]]
    BANKS = 4
    assert 2 * (NU + 2) % BANKS == 0
    base_items = own + [(*x, 2) for x in chain[:LEAD]]

    DELAY, PARTS = HG, HG // 2
    VALUES, CARRIED = ({s: [] for s in range(NSLOT)} for _ in range(2))
    for p in range(NP):
        for part in range(PARTS):
            s = p * HG + HG - 1 + DELAY + part * (HG // PARTS)
            (VALUES[s] if s < NSLOT else CARRIED[s - NSLOT]).append((p, part))
    parts = {}
    for p, piece in enumerate(PIECES):
        off = 0
        for seg in piece:
            for part in range(PARTS):
                c0, c1 = max(off, part * (ST // PARTS)), min(off + seg[2] - seg[1], (part + 1) * (ST // PARTS))
                if c0 < c1:
                    parts.setdefault((p, part), []).append((seg, c0, seg[1] + c0 - off, seg[1] + c1 - off))
            off += seg[2] - seg[1]
    LAST_OF_BANK = [max(p for p, piece in enumerate(PIECES) if any(s[1] // ST == b for s in piece)) for b in range(2)]
    COPY_0 = next(s for s in VALUES if (LAST_OF_BANK[0], PARTS - 1) in VALUES[s]) + 1
    COPY_1 = max(s for s in CARRIED if CARRIED[s]) + 1
    OUT_AT = COPY_1 + 2
    out_item = ("o", 0, 0, -1)
    with_out = lambda items: units_from(items[:OUT_AT] + [out_item] + items[OUT_AT:])

    with ExitStack() as c:
        sb = lambda n, s, d: c.enter_context(nc.sbuf_tensor(name + n, s, d))
        vst = [sb(f"v{i}", [P, TPB, KH, VW], F32) for i in range(2)]
        prob = [sb(f"p{i}", [P, HG, ST], F32) for i in range(PBUF)]
        mmax = [sb(f"m{i}", [P, HG, TPB], F32) for i in range(2)]
        mhalf = [sb(f"mh{i}", [P, HG, TPB // 2], F32) for i in range(2)]
        masked_s = [sb(f"ms{i}", [P, ST], BF16) for i in range(BANKS)]
        mrow = [sb(f"mr{i}", [TPB, HG, P], F32R) for i in range(2)]
        osb = sb("o", [P, SEQ], F32)
        rec = [sb(f"rec{i}", [P, TPB, HG], F32) for i in range(2)]
        zero = k.mask_q[:, 0:ST]
        held = sb("held", [P, BANKS + NP], F32)
        s_ps = [c.enter_context(nc.psum_tensor(name + f"S{i}", [P, ST], F32)) for i in range(BANKS)]
        t_ps = [c.enter_context(nc.psum_tensor(name + f"T{i}", [P, ST], F32)) for i in range(2)]
        o_ps = c.enter_context(nc.psum_tensor(name + "O", [P, SEQ], F32))
        unit_ready, red_done, mcopy_done, out_done = (
            sem(name + n) for n in ("unit", "red", "mc", "out"))
        st_ready, exp_done, masked, pv_done, o_copied, rec_done = (
            sem(name + n) for n in ("st", "exp", "mask", "pv", "oc", "rec"))
        ldS = [sem(name + f"ldS{i}") for i in range(2)]
        ldT = [sem(name + f"ldT{i}") for i in range(2)]
        row_set = [[sem(name + f"row{i}{h}") for h in range(HG)] for i in range(2)]

        banks = [*[t[:, :] for t in s_ps], o_ps[:, 0:ST], o_ps[:, ST:SEQ]]
        start_ring = list(range(len(banks)))

        def main_ring(slot):
            return [(slot + n) % BANKS for n in range(BANKS)]

        def after(g, n):
            u, par = g
            return (u + (par + n) // 2, (par + n) % 2)

        def at(g, step):
            return isinstance(g[0], int) and lin(g, 1, 0) == step

        def unit_base(g):
            return NU + NLEAD if at(g, 0) else lin(g, NU + 2, NU - 2 + (0 if at(g, NG - 1) else NLEAD))

        def unit_slot(g):
            return (NU + NLEAD if at(g, 0) else g[1] * (NU + 2) + NU - 2 + (0 if at(g, NG - 1) else NLEAD)) % BANKS

        def units_of(g):
            if at(g, NG - 1):
                return [(*x[:5], OUT_AT) for x in units_from([out_item])]
            if at(g, NG - 2):
                return with_out(own)
            return units_from(base_items) if at(g, 0) else with_out(base_items)

        def before(g):
            if at(g, 0):
                last_of = {n % len(start_ring): x for n, x in enumerate(start_units)}
                return [last_of[bank] for bank in main_ring(unit_slot(g))]
            units = units_from(own if at(g, NG - 1) else base_items)
            return [(*x[:4], x[4] - 1, x[5]) for x in units[-BANKS:]]

        def beside(units, slot):
            return [n for n, x in enumerate(units) if x[5] == slot]

        def main_steps(eng, step):
            step((0, 0))
            step((0, 1))
            with eng.Fori(1, NG // 2 - 1) as u:
                step((u, 0))
                step((u, 1))
            step((NG // 2 - 1, 0))
            step((NG // 2 - 1, 1))

        END = (NG // 2 - 1, 1)

        with nc.Block() as block:
            @block.sync
            def _(sp):
                def load_S(g):
                    load_q(sp, qS[g[1]], g, ldS[g[1]])
                    load_k(sp, kS[g[1]], g, ldS[g[1]])

                def load_T(g):
                    load_q(sp, qT[g[1]], g, ldT[g[1]])
                    load_k(sp, kT[g[1]], g, ldT[g[1]])
                    load_v(sp, vst[g[1]], g, ldT[g[1]])

                def set_row(g, h):
                    sp.wait_ge(mcopy_done, lin(g, HG, h + 1))
                    sp.dma_start(qT[g[1]][MROW:MROW + 1, h, :].bitcast(F32),
                                 mrow[g[1]][:, h, :].bitcast(F32)).then_inc(row_set[g[1]][h], 16)

                def step(g):
                    if not at(g, 0) and not at(g, NG - 1):
                        sp.wait_ge(pv_done, lin(g, NP, 0))
                        load_T(after(g, 1))
                    if not at(g, NG - 2) and not at(g, NG - 1):
                        sp.wait_ge(red_done, lin(g, NRED, NRED))
                        load_S(after(g, 2))
                    if not at(g, NG - 1):
                        for h in range(HG):
                            set_row(after(g, 1), h)

                load_S((0, 0))
                load_S((0, 1))
                load_T((0, 0))
                load_T((0, 1))
                for h in range(HG):
                    set_row((0, 0), h)
                main_steps(sp, step)

            @block.gpsimd
            def _(pool):
                def step(g):
                    for p in range(NP):
                        if not DIAGONALS[p]:
                            continue
                        pool.wait_ge(exp_done, lin(g, NSLOT, (p + 1) * HG))
                        nc.gpsimd.tensor_tensor(held[:, BANKS + p:BANKS + p + 1], k.ident[:, 0:1], k.ident[:, 0:1], ALU.add).then_inc(masked, 1)
                        for off, _ in DIAGONALS[p]:
                            block_ = prob[p % PBUF][:, :, off:off + P]
                            nc.gpsimd.affine_select(out=block_, in_=block_, compare_op=ALU.is_ge, fill=0.0, base=0,
                                                    pattern=[[0, HG], [1, P]], channel_multiplier=-1).then_inc(masked, 1)

                main_steps(pool, step)

            @block.vector
            def _(dve):
                def consume(units, base, ring, g):
                    for n, (kind, h, i, half, ahead, _) in enumerate(units):
                        if kind == "m":
                            continue
                        gU = after(g, ahead)
                        par = gU[1]
                        bank = ring[n % len(ring)]
                        buf = banks[bank]
                        if kind == "S":
                            w, c0 = (i + 1) * P, half * ST
                            c1 = min(w, c0 + ST)
                            wide = w > ST
                            spare = bank % BANKS if ring is not start_ring else n % BANKS
                            earlier = [x for x in units[:n - BANKS + 1] if x[0] == "S"] if n >= BANKS else []
                            if ring is start_ring and earlier:
                                dve.wait_ge(red_done, earlier[-1][4] * NRED + MAXIMA[earlier[-1][1:4]])
                            elif ring is not start_ring and at(g, 0) and n == 0:
                                dve.wait_ge(red_done, START_MAXIMA)
                            dve.wait_ge(unit_ready, base + (n + 1))
                            nc.vector.memset(held[:, spare:spare + 1], 0.0).then_inc(red_done, 1)
                            found = mhalf[par][:, h, i - TPB // 2:i - TPB // 2 + 1] if wide and half == 0 else mmax[par][:, h, i:i + 1]
                            nc.vector.tensor_tensor_reduce(masked_s[spare][:, 0:c1 - c0], buf[:, 0:c1 - c0],
                                                           k.mask_q[:, SEQ - w + c0:SEQ - w + c1], 1.0, NEVER,
                                                           ALU.add, ALU.max, found).then_inc(red_done, 1)
                            if i == BLOCKS[-1]:
                                dve.wait_ge(red_done, lin(gU, NRED, MAXIMA[h, i, half] - 1))
                                upper = mmax[par][:, h, TPB // 2:TPB]
                                nc.vector.tensor_tensor(upper, upper, mhalf[par][:, h, :], ALU.max).then_inc(red_done, 1)
                        else:
                            dve.wait_ge(unit_ready, base + (n + 1))
                            rows = slice(half * TPB // 2, (half + 1) * TPB // 2)
                            o = buf.rearrange("p (i h c) -> p i h c", h=HG, c=CT)
                            nc.vector.reciprocal(rec[par][:, rows, :], o[:, :, :, VD]).then_inc(rec_done, 1)
                            dve.wait_ge(rec_done, lin(gU, 2, half + 1))
                            nc.vector.tensor_tensor(
                                out[:, bass.ds(lin(gU, 1, 0), 1), rows, :].rearrange("p o i (h c) -> p (o i) h c", h=HG),
                                o[:, :, :, 0:VD], rec[par][:, rows, :].unsqueeze(3).broadcast_to([P, TPB // 2, HG, VD]),
                                ALU.mult).then_inc(out_done, 1)

                consume(start_units, 0, start_ring, (0, 0))
                main_steps(dve, lambda g: consume(units_of(g), unit_base(g), main_ring(unit_slot(g)), g))
                consume(units_from([("o", 0, 0, 0)]), unit_base(END) + 2, main_ring(unit_slot(END) + 2), END)

            @block.scalar
            def _(act):
                def copy_out(g, bank):
                    act.wait_ge(pv_done, lin(g, NP, LAST_OF_BANK[bank] + 1))
                    if bank == 0 and not at(g, 0):
                        act.wait_ge(out_done, lin(g, 2, 0))
                    cols = slice(bank * ST, (bank + 1) * ST)
                    nc.scalar.copy(osb[:, cols], o_ps[:, cols]).then_inc(o_copied, 1)

                def copy_max(base, ring, n, g, h):
                    act.wait_ge(unit_ready, base + (n + 1))
                    nc.scalar.mul(mrow[g[1]][:, h, :], banks[ring[n % len(ring)]][0:TPB, 0:P], -1.0).then_inc(mcopy_done, 1)

                for n, (kind, h, _, _, ahead, _) in enumerate(start_units):
                    if kind == "m":
                        copy_max(0, start_ring, n, (0, 0), h)

                def step(g):
                    units = units_of(g)
                    for p in range(NP):
                        for h in range(HG):
                            slot = p * HG + h
                            act.wait_ge(st_ready, lin(g, NSLOT, slot + 1))
                            if h == 0 and not (at(g, 0) and p < PBUF):
                                act.wait_ge(pv_done, lin(g, NP, p - PBUF + 1))
                            nc.scalar.activation(prob[p % PBUF][:, h, :], t_ps[slot % 2][:, :], ACT.Exp, scale=scale)\
                                .then_inc(exp_done, 1)
                            for n in beside(units, slot):
                                kind, hm, _, _, ahead, _ = units[n]
                                if kind == "m":
                                    gm = after(g, ahead)
                                    if not at(gm, 1):
                                        act.wait_ge(row_set[gm[1]][hm], gm[0] * 16)
                                    copy_max(unit_base(g), main_ring(unit_slot(g)), n, gm, hm)
                            if slot == COPY_0:
                                copy_out(g, 0)
                            if slot == COPY_1 and not at(g, 0):
                                copy_out(after(g, -1), 1)

                main_steps(act, step)
                copy_out(END, 1)

            @block.tensor
            def _(pe):
                def unit(units, last_units, ring, n, g):
                    kind, h, i, half, ahead, _ = units[n]
                    gU = after(g, ahead)
                    prev = units[n - len(ring)] if n >= len(ring) else last_units[n] if last_units else None
                    if prev is not None:
                        gP = after(g, prev[4])
                        if prev[0] == "S":
                            pe.wait_ge(red_done, lin(gP, NRED, MAXIMA[prev[1:4]]))
                        elif prev[0] == "m":
                            pe.wait_ge(mcopy_done, lin(gP, HG, prev[1] + 1))
                        else:
                            pe.wait_ge(out_done, lin(gP, 2, prev[3] + 1))
                    buf = banks[ring[n % len(ring)]]
                    if kind == "S":
                        if (h, i, half) == (0, BLOCKS[0], 0):
                            pe.wait_ge(ldS[gU[1]], gU[0] * (16 * NLOAD) + 16 * NLOAD)
                        c0, c1 = half * ST, min((i + 1) * P, (half + 1) * ST)
                        last = nc.tensor.matmul(buf[:, 0:c1 - c0], qS[gU[1]][0:MROW, h, i * P:(i + 1) * P],
                                                kS[gU[1]][0:MROW, KI(h), c0:c1], start=True, stop=True)
                    elif kind == "m":
                        pe.wait_ge(red_done, lin(gU, NRED, MAXIMA[h, BLOCKS[-1], 0]))
                        last = nc.tensor.transpose(buf[0:TPB, 0:P], mmax[gU[1]][:, h, :], k.ident[:, :])
                    else:
                        pe.wait_ge(o_copied, lin(gU, 2, half + 1))
                        for b in range(TPB // 2):
                            rows = slice(half * ST + b * P, half * ST + (b + 1) * P)
                            last = nc.tensor.transpose(buf[:, b * P:(b + 1) * P], osb[:, rows], k.ident[:, :])
                    last.then_inc(unit_ready, 1)

                for n in range(len(start_units)):
                    unit(start_units, None, start_ring, n, (0, 0))

                order = [(p, part, *x) for p in range(NP) for part in range(PARTS) for x in parts[p, part]]
                opens = {b: next(x for x in order if x[2][1] // ST == b) for b in range(SEQ // ST)}
                closes = {b: [x for x in order if x[2][1] // ST == b][-1] for b in range(SEQ // ST)}

                def values(g, p, part):
                    if part == 0 and DIAGONALS[p]:
                        pe.wait_ge(masked, lin(g, PER_MASK, NDIAG[p]))
                    elif part == 0:
                        pe.wait_ge(exp_done, lin(g, NSLOT, (p + 1) * HG))
                    if (p, part) == (0, 0) and at(g, 0):
                        pe.wait_ge(red_done, START_MAXIMA)
                        for b in range(SEQ // ST):
                            nc.tensor.matmul(o_ps[:, b * ST:(b + 1) * ST], zero[:, 0:P], zero, start=True, stop=True)
                    if part == 0 and p < SEQ // ST and not at(g, 0):
                        pe.wait_ge(o_copied, lin(g, 2, p - 1))
                    for x in parts[p, part]:
                        seg, off, q0, q1 = x
                        bank = q0 // ST
                        for h in range(HG):
                            last = nc.tensor.matmul(o_ps[h * CT:h * CT + VW, q0:q1], vst[g[1]][:, seg[0], KI(h), :],
                                                    prob[p % PBUF][:, h, off:off + q1 - q0],
                                                    start=opens[bank] == (p, part, *x), stop=closes[bank] == (p, part, *x))
                    if part == PARTS - 1:
                        last.then_inc(pv_done, 1)

                def step(g):
                    units = units_of(g)
                    pe.wait_ge(ldT[g[1]], g[0] * (16 * (NLOAD + 1)) + 16 * (NLOAD + 1))
                    for p in range(NP):
                        for h in range(HG):
                            slot = p * HG + h
                            if p == 0:
                                pe.wait_ge(row_set[g[1]][h], g[0] * 16 + 16)
                            if not (at(g, 0) and slot < 2):
                                pe.wait_ge(exp_done, lin(g, NSLOT, slot - 1))
                            off = 0
                            for j, q0, q1 in PIECES[p]:
                                last = nc.tensor.matmul(t_ps[slot % 2][:, off:off + q1 - q0],
                                                        kT[g[1]][0:MROW + 1, KI(h), j * P:(j + 1) * P],
                                                        qT[g[1]][0:MROW + 1, h, q0:q1], start=True, stop=True)
                                off += q1 - q0
                            last.then_inc(st_ready, 1)
                            for n in beside(units, slot):
                                unit(units, before(g), main_ring(unit_slot(g)), n, g)
                            if not at(g, 0):
                                for pv, part in CARRIED[slot]:
                                    values(after(g, -1), pv, part)
                            for pv, part in VALUES[slot]:
                                values(g, pv, part)

                main_steps(pe, step)
                for slot in CARRIED:
                    for pv, part in CARRIED[slot]:
                        values(END, pv, part)
                for n in range(2):
                    unit(units_from([("o", 0, 0, 0)]), before(END)[2:], main_ring(unit_slot(END) + 2), n, END)


def project_out(k, name, attn, w_out, NHG, w_loaded=None):
    nc, sem = k.nc, k.sem
    GW = attn.shape[3]
    NC = NHG * GW // P
    with ExitStack() as c:
        sb = lambda n, s, d: c.enter_context(nc.sbuf_tensor(name + n, s, d))
        w = w_out
        stage = [sb(f"st{i}", [P, TPS, NHG * GW], F32) for i in range(2)]
        aT = [sb(f"aT{i}", [P, NC, ST], F32) for i in range(2)]
        aT_ps = [c.enter_context(nc.psum_tensor(name + f"aps{i}", [P, ST], F32)) for i in range(4)]
        y_ps = [c.enter_context(nc.psum_tensor(name + f"y{i}", [P, ST], F32)) for i in range(2)]
        staged, turned, aT_ready, y_ready, added = (sem(name + n) for n in ("sg", "tr", "aT", "y", "add"))
        with nc.Block() as block:
            @block.tensor
            def _(pe):
                def front(g):
                    par = g[1]
                    pe.wait_ge(staged, lin(g, 1, 1))
                    for n in range(NC):
                        wait_past(pe, aT_ready, lin(g, NC, n + 1 - max(NC, 2)))
                        for t in range(TPS):
                            last = nc.tensor.transpose(aT_ps[(par * NC + n) % 4][:, t * P:(t + 1) * P],
                                                       stage[par][:, t, n * P:(n + 1) * P], k.ident[:, :])
                        last.then_inc(turned, 1)

                def back(g):
                    par = g[1]
                    pe.wait_ge(aT_ready, lin(g, NC, NC))
                    wait_past(pe, added, lin(g, 1, -1))
                    for t in range(TPS):
                        for n in range(NC):
                            last = nc.tensor.matmul(y_ps[par][:, t * D:(t + 1) * D], aT[par][:, n, t * P:(t + 1) * P],
                                                    w[:, n, :], start=n == 0, stop=n == NC - 1)
                    last.then_inc(y_ready, 1)

                if w_loaded is not None:
                    pe.wait_ge(w_loaded, 16)
                pipelined(pe, NST // 2, front, back)

            @block.scalar
            def _(act):
                def front(g):
                    u, par = g
                    wait_past(act, turned, lin(g, NC, -NC))
                    for t in range(TPS):
                        last = nc.scalar.copy(stage[par][:, t, :].rearrange("p (g c) -> p g c", g=NHG),
                                              attn[:, bass.ds(u * NHG, NHG), par * TPS + t, :])
                    last.then_inc(staged, 1)

                def back(g):
                    par = g[1]
                    wait_past(act, y_ready, lin(g, 1, -1))
                    for n in range(NC):
                        act.wait_ge(turned, lin(g, NC, n + 1))
                        nc.scalar.copy(aT[par][:, n, :], aT_ps[(par * NC + n) % 4][:, :]).then_inc(aT_ready, 1)

                pipelined(act, NST // 2, front, back)

            @block.vector
            def _(dve):
                for u in rounds(dve, NST // 2):
                    for par in range(2):
                        g = (u, par)
                        dve.wait_ge(y_ready, lin(g, 1, 1))
                        rows = k.x[:, bass.ds(lin(g, TPS, 0), TPS), :]
                        nc.vector.tensor_tensor(rows, y_ps[par][:, :].rearrange("p (t d) -> p t d", t=TPS), rows,
                                                ALU.add).then_inc(added, 1)
                        tile_stats(k, dve, g, added)


def route(k, name, E, K, w_router, bias_row, xh, xl, gateT, weights, weights_loaded):
    nc, sem = k.nc, k.sem
    PAD = 6 if K == 2 else 0
    LOADED = 16 if bias_row is None else 32
    TAKEN, FILL = (-1.0, 3.0) if K == 2 else (-3e38, 0.0)
    with ExitStack() as c:
        sb = lambda n, s, d: c.enter_context(nc.sbuf_tensor(name + n, s, d))
        pb = lambda n: c.enter_context(nc.psum_tensor(name + n, [P, ST], F32))
        wr = sb("wr", [P, E], F32)
        bias = sb("bias", [P, E], F32)
        xn = [sb(f"xn{i}", [P, TPS, D], F32) for i in range(2)]
        xs = [sb(f"xs{i}", [P, ST], F32) for i in range(2)]
        lg = sb("lg", [P, TILES, E], F32)
        pr = sb("pr", [P, TILES, E + PAD], F32)
        sel = sb("sel", [P, TILES, E], F32)
        top = sb("top", [P, TILES, 8], F32)
        srt = sb("srt", [P, TILES, 8], F32)
        rep = sb("rep", [P, TILES, E + PAD], F32)
        sm = sb("sm", [P, TILES], F32)
        gt = sb("gt", [P, TILES, 2, E], F32)
        hi = sb("hi", [P, TILES, E], F32R)
        xT_ps = [pb(f"xT{i}") for i in range(2)]
        l_ps = [pb(f"l{i}") for i in range(2)]
        g_ps = [pb(f"g{i}") for i in range(2)]
        loaded, filled, xn_ready, xT_done, xs_ready, xh_ready, xl_ready = (
            sem(name + n) for n in ("ld", "fl", "xn", "xT", "xs", "xh", "xl"))
        l_done, lg_ready, shifted, pr_ready, chain, g_done, g_kept, gt_ready, w_split = (
            sem(name + n) for n in ("l", "lg", "sh", "pr", "ch", "gd", "gk", "gt", "ws"))
        with nc.Block() as block:
            @block.sync
            def _(sp):
                sp.dma_start(wr[:, :], w_router).then_inc(loaded, 16)
                if bias_row is not None:
                    sp.dma_start(bias[:, :], bias_row.partition_broadcast(P)).then_inc(loaded, 16)

            @block.tensor
            def _(pe):
                pe.wait_ge(loaded, LOADED)

                def turn(g):
                    pe.wait_ge(xn_ready, lin(g, 1, 1))
                    wait_past(pe, xh_ready, lin(g, 1, -1))
                    for t in range(TPS):
                        last = nc.tensor.transpose(xT_ps[g[1]][:, t * P:(t + 1) * P], xn[g[1]][:, t, :], k.ident[:, :])
                    last.then_inc(xT_done, 1)

                def logits(g):
                    pe.wait_ge(xs_ready, lin(g, 1, 1))
                    wait_past(pe, lg_ready, lin(g, 1, -1))
                    for t in range(TPS):
                        last = nc.tensor.matmul(l_ps[g[1]][:, t * E:(t + 1) * E], xs[g[1]][:, t * P:(t + 1) * P], wr[:, :],
                                                start=True, stop=True)
                    last.then_inc(l_done, 1)

                pipelined(pe, NST // 2, turn, logits)
                pe.wait_ge(gt_ready, 1)
                for s in range(NST):
                    if s >= 2:
                        pe.wait_ge(g_kept, s - 1)
                    for t in range(TPS):
                        last = nc.tensor.transpose(g_ps[s % 2][0:2 * E, t * P:(t + 1) * P],
                                                   gt[:, s * TPS + t, :, :].rearrange("p a e -> p (a e)"), k.ident[:, :])
                    last.then_inc(g_done, 1)

            @block.scalar
            def _(act):
                def keep(g):
                    act.wait_ge(xT_done, lin(g, 1, 1))
                    wait_past(act, l_done, lin(g, 1, -1))
                    wait_past(act, xl_ready, lin(g, 1, -1))
                    nc.scalar.copy(xs[g[1]][:, :], xT_ps[g[1]][:, :]).then_inc(xs_ready, 1)
                    nc.scalar.copy(xh[:, bass.ds(lin(g, ST, 0), ST)], xT_ps[g[1]][:, :]).then_inc(xh_ready, 1)

                def keep_logits(g):
                    act.wait_ge(l_done, lin(g, 1, 1))
                    nc.scalar.copy(lg[:, bass.ds(lin(g, TPS, 0), TPS), :],
                                   l_ps[g[1]][:, 0:TPS * E].rearrange("p (t e) -> p t e", t=TPS)).then_inc(lg_ready, 1)

                pipelined(act, NST // 2, keep, keep_logits)
                if K == 2:
                    act.wait_ge(filled, 3)
                    act.wait_ge(shifted, 1)
                else:
                    act.wait_ge(lg_ready, NST)
                nc.scalar.activation(pr[:, :, 0:E], lg[:, :, :], ACT.Exp, scale=1.0 if K == 2 else -1.0).then_inc(pr_ready, 1)
                act.wait_ge(weights_loaded, 16 * len(weights))
                for raw, w_hi, _ in weights:
                    nc.scalar.copy(w_hi, raw).then_inc(w_split, 1)
                for s in range(NST):
                    act.wait_ge(g_done, s + 1)
                    nc.scalar.copy(gateT[:, s * ST:(s + 1) * ST], g_ps[s % 2][0:2 * E, :]).then_inc(g_kept, 1)

            @block.gpsimd
            def _(pool):
                if K == 2:
                    for t in (pr, top, rep):
                        nc.gpsimd.memset(t[:, :, :], FILL).then_inc(filled, 1)
                for u in rounds(pool, NST // 2):
                    for par in range(2):
                        pool.wait_ge(xh_ready, lin((u, par), 1, 1))
                        cols = bass.ds(lin((u, par), ST, 0), ST)
                        nc.gpsimd.tensor_tensor(xl[:, cols], xs[par][:, :], xh[:, cols].bitcast(F32), ALU.subtract)\
                            .then_inc(xl_ready, 1)
                for n, (raw, w_hi, w_lo) in list(enumerate(weights))[:len(weights) // 2]:
                    pool.wait_ge(w_split, n + 1)
                    nc.gpsimd.tensor_tensor(w_lo, raw, w_hi.bitcast(F32), ALU.subtract)

            @block.vector
            def _(dve):
                for u in rounds(dve, NST // 2):
                    for par in range(2):
                        wait_past(dve, xT_done, lin((u, par), 1, -1))
                        normalise(k, dve, xn[par], (u, par), xn_ready)
                dve.wait_ge(loaded, LOADED)
                if K == 2:
                    dve.wait_ge(filled, 3)
                dve.wait_ge(lg_ready, NST)
                count = [0]

                def link(*instructions):
                    for ins in instructions:
                        ins.then_inc(chain, 1)
                    count[0] += len(instructions)
                    dve.wait_ge(chain, count[0])

                wide = lambda a: a.unsqueeze(2).broadcast_to([P, TILES, E])
                s = sm[:, :]
                p = pr[:, :, 0:E]
                if K == 2:
                    link(nc.vector.tensor_reduce(s, lg[:, :, :], AXX, ALU.max))
                    nc.vector.tensor_tensor(lg[:, :, :], lg[:, :, :], wide(s), ALU.subtract).then_inc(shifted, 1)
                    dve.wait_ge(pr_ready, 1)
                    link(*[nc.vector.max(srt[:, t, :], pr[:, t, 0:E]) for t in range(TILES)])
                    link(nc.vector.tensor_copy(top[:, :, 0:K], srt[:, :, 0:K]))
                    values, chosen = pr, p
                else:
                    dve.wait_ge(pr_ready, 1)
                    link(nc.vector.tensor_scalar(p, p, 1.0, None, ALU.add))
                    link(nc.vector.reciprocal(p, p))
                    link(nc.vector.tensor_tensor(sel[:, :, :], p, bias[:, :].unsqueeze(1).broadcast_to([P, TILES, E]), ALU.add))
                    link(*[nc.vector.max(top[:, t, :], sel[:, t, :]) for t in range(TILES)])
                    values, chosen = sel, sel[:, :, :]
                link(*[nc.vector.match_replace(rep[:, t, :], top[:, t, :], values[:, t, :], TAKEN) for t in range(TILES)])
                r = rep[:, :, 0:E]
                link(nc.vector.tensor_tensor(r, r, chosen, ALU.not_equal))
                link(nc.vector.tensor_tensor(r, r, p, ALU.mult))
                link(nc.vector.tensor_reduce(s, r, AXX, ALU.add))
                link(nc.vector.reciprocal(s, s))
                if K != 2:
                    link(nc.vector.tensor_scalar(s, s, ROUTE_SCALE, None, ALU.mult))
                link(nc.vector.tensor_tensor(r, r, wide(s), ALU.mult))
                link(nc.vector.tensor_copy(hi[:, :, :], r))
                link(nc.vector.tensor_copy(gt[:, :, 0, :], hi[:, :, :].bitcast(F32)))
                nc.vector.tensor_tensor(gt[:, :, 1, :], r, hi[:, :, :].bitcast(F32), ALU.subtract).then_inc(gt_ready, 1)
                for n, (raw, w_hi, w_lo) in list(enumerate(weights))[len(weights) // 2:]:
                    dve.wait_ge(w_split, n + 1)
                    nc.vector.tensor_tensor(w_lo, raw, w_hi.bitcast(F32), ALU.subtract)


def moe_0(k, b_fc, b_proj, b_proj_s, wf, wp, xh, xl, gateT, sel):
    nc, sem = k.nc, k.sem
    E, NCH = 8, 4
    NE = E + 1
    NH = NE * NCH
    LAG, HBUF = 3, 4
    with ExitStack() as c:
        sb = lambda n, s, d: c.enter_context(nc.sbuf_tensor("m0_" + n, s, d))
        pb = lambda n: c.enter_context(nc.psum_tensor("m0_" + n, [P, ST], F32))
        bfc, bps = sb("bfc", [P, NH], F32), sb("bps", [P, 1], F32)
        bp = sb("bp", [2 * E, D], F32)
        bph, bpl = sb("bph", [2 * E, D], F32R), sb("bpl", [2 * E, D], F32R)
        h = [sb(f"h{i}", [P, ST], F32) for i in range(2)]
        hh = [sb(f"hh{i}", [P, ST], F32R) for i in range(HBUF)]
        hl = [sb(f"hl{i}", [P, ST], F32R) for i in range(HBUF)]
        gb = [sb(f"gb{i}", [P, ST], F32) for i in range(2)]
        prod = [sb(f"pr{i}", [P, ST], F32) for i in range(2)]
        acc = [sb(f"acc{i}", [P, ST], F32) for i in range(2)]
        f_ps = [pb(f"f{i}") for i in range(3)]
        y_ps = [pb(f"y{i}") for i in range(3)]
        b_ps, t_ps = pb("b"), pb("t")
        loaded, split, fc_done, h_ready, hl_ready, y_done = (sem("m0_" + n) for n in ("ld", "sp", "fc", "h", "hl", "y"))
        gb_done, gb_ready, summed, turned, added = (sem("m0_" + n) for n in ("gd", "gb", "sum", "tr", "add"))
        NSUM = 1 + 2 * E
        READ = lambda e: max(2 * e, 1)
        SUM_AT = lambda e: e * NCH + NCH + LAG
        TURN_AT, ADD_AT = LAG + 3, LAG + 5

        def before(g):
            return (g[0] + (g[1] - 1) // 2, (g[1] - 1) % 2)

        def first(g):
            return isinstance(g[0], int) and g == (0, 0)

        def steps(eng, supertile, tail):
            for u in rounds(eng, NST // 2):
                for par in range(2):
                    supertile((u, par))
            tail((NST // 2 - 1, 1))

        with nc.Block() as block:
            @block.sync
            def _(sp):
                for dst, src in ((bfc[:, :], b_fc), (bps[:, :], b_proj_s), (bp[0:E, :], b_proj), (bp[E:2 * E, :], b_proj)):
                    sp.dma_start(dst, src).then_inc(loaded, 16)

            @block.tensor
            def _(pe):
                def fc(g, n):
                    e, ch = divmod(n, NCH)
                    cols = bass.ds(lin(g, ST, 0), ST)
                    wait_past(pe, h_ready, lin(g, 2 * NH, 2 * (n - 2)))
                    if ch == 2 and e:
                        wait_past(pe, gb_ready, lin(g, E, e - 1))
                    part = slice(ch * P, (ch + 1) * P)
                    nc.tensor.matmul(f_ps[n % 3][:, :], wf[0][:, e, part], xh[:, cols], start=True, stop=False)
                    nc.tensor.matmul(f_ps[n % 3][:, :], wf[0][:, e, part], xl[:, cols], start=False, stop=False)
                    nc.tensor.matmul(f_ps[n % 3][:, :], wf[1][:, e, part], xh[:, cols], start=False, stop=True)\
                        .then_inc(fc_done, 1)
                    if ch == 2 and e:
                        nc.tensor.matmul(b_ps[:, :], sel[:, e - 1:e].broadcast_to([2 * E, P]), gateT[:, cols],
                                         start=True, stop=True).then_inc(gb_done, 1)

                def project(g, n):
                    e, ch = divmod(n, NCH)
                    cols = bass.ds(lin(g, ST, 0), ST)
                    if ch == 0:
                        if e >= 3:
                            pe.wait_ge(summed, lin(g, NSUM, READ(e - 3)))
                        elif not first(g):
                            pe.wait_ge(summed, lin(before(g), NSUM, READ(e - 3 + NE)))
                    pe.wait_ge(hl_ready, lin(g, NH, n + 1))
                    y = y_ps[e % 3][:, :]
                    nc.tensor.matmul(y, wp[0][:, e, ch, :], hh[n % HBUF][:, :], start=ch == 0, stop=False)
                    nc.tensor.matmul(y, wp[0][:, e, ch, :], hl[n % HBUF][:, :], start=False, stop=False)
                    last = nc.tensor.matmul(y, wp[1][:, e, ch, :], hh[n % HBUF][:, :], start=False,
                                            stop=ch == NCH - 1 and e > 0)
                    if ch == NCH - 1:
                        if e == 0:
                            nc.tensor.matmul(y, bph[:, :], gateT[:, cols], start=False, stop=False)
                            last = nc.tensor.matmul(y, bpl[:, :], gateT[:, cols], start=False, stop=True)
                        last.then_inc(y_done, 1)

                def turn(g):
                    pe.wait_ge(summed, lin(g, NSUM, NSUM))
                    wait_past(pe, added, lin(g, 1, 0))
                    for t in range(TPS):
                        last = nc.tensor.transpose(t_ps[:, t * P:(t + 1) * P], acc[g[1]][:, t * P:(t + 1) * P], k.ident[:, :])
                    last.then_inc(turned, 1)

                def supertile(g):
                    for n in range(NH):
                        fc(g, n)
                        if n >= LAG:
                            project(g, n - LAG)
                        elif not first(g):
                            project(before(g), NH - LAG + n)
                        if n == TURN_AT and not first(g):
                            turn(before(g))

                def tail(g):
                    for n in range(NH - LAG, NH):
                        project(g, n)
                    turn(g)

                pe.wait_ge(split, 2)
                steps(pe, supertile, tail)

            @block.scalar
            def _(act):
                def supertile(g):
                    for n in range(NH):
                        e, ch = divmod(n, NCH)
                        act.wait_ge(fc_done, lin(g, NH, n + 1))
                        wait_past(act, hl_ready, lin(g, NH, n - 1))
                        for dst in (h[n % 2], hh[n % HBUF]):
                            nc.scalar.activation(dst[:, :], f_ps[n % 3][:, :], ACT.Gelu_apprx_tanh, bias=bfc[:, n:n + 1])\
                                .then_inc(h_ready, 1)
                        if ch == 2 and e:
                            act.wait_ge(gb_done, lin(g, E, e))
                            if e >= 3:
                                act.wait_ge(summed, lin(g, NSUM, READ(e - 2)))
                            elif not first(g):
                                act.wait_ge(summed, lin(before(g), NSUM, READ(e - 2 + E)))
                            nc.scalar.copy(gb[e % 2][:, :], b_ps[:, :]).then_inc(gb_ready, 1)

                act.wait_ge(loaded, 16 * 4)
                steps(act, supertile, lambda g: None)

            @block.vector
            def _(dve):
                dve.wait_ge(loaded, 16 * 4)
                nc.vector.tensor_copy(bph[:, :], bp[:, :]).then_inc(split, 1)
                dve.wait_ge(split, 1)
                nc.vector.tensor_tensor(bpl[:, :], bp[:, :], bph[:, :].bitcast(F32), ALU.subtract).then_inc(split, 1)

                def sum_up(g, e):
                    a = acc[g[1]][:, :]
                    dve.wait_ge(y_done, lin(g, NE, e + 1))
                    if e == 0:
                        wait_past(dve, turned, lin(g, 1, -1))
                        nc.vector.tensor_scalar(a, y_ps[0][:, :], bps[:, 0:1], None, ALU.add).then_inc(summed, 1)
                        return
                    dve.wait_ge(gb_ready, lin(g, E, e))
                    nc.vector.tensor_tensor(prod[e % 2][:, :], y_ps[e % 3][:, :], gb[e % 2][:, :], ALU.mult).then_inc(summed, 1)
                    dve.wait_ge(summed, lin(g, NSUM, 2 * e))
                    nc.vector.tensor_tensor(a, a, prod[e % 2][:, :], ALU.add).then_inc(summed, 1)

                def add(g):
                    dve.wait_ge(turned, lin(g, 1, 1))
                    rows = k.x[:, bass.ds(lin(g, TPS, 0), TPS), :]
                    nc.vector.tensor_tensor(rows, t_ps[:, :].rearrange("p (t d) -> p t d", t=TPS), rows, ALU.add)\
                        .then_inc(added, 1)
                    tile_stats(k, dve, g, added)

                def end(g, n):
                    for e in range(NE):
                        if SUM_AT(e) == NH + n:
                            sum_up(g, e)
                    if n == ADD_AT:
                        add(g)

                def supertile(g):
                    for n in range(NH):
                        dve.wait_ge(h_ready, lin(g, 2 * NH, 2 * (n + 1)))
                        nc.vector.tensor_tensor(hl[n % HBUF][:, :], h[n % 2][:, :], hh[n % HBUF][:, :].bitcast(F32),
                                                ALU.subtract).then_inc(hl_ready, 1)
                        for e in range(NE):
                            if SUM_AT(e) == n:
                                sum_up(g, e)
                        if not first(g):
                            end(before(g), n)

                steps(dve, supertile, lambda g: [end(g, n) for n in range(ADD_AT + 1)])


def absorb(k, w_qT, w_kT, w_vT, w_out, a_q, a_v, then_load):
    nc, sem = k.nc, k.sem
    HD, LD = 64, 32
    HPC = P // LD
    with ExitStack() as c:
        sb = lambda n, s: c.enter_context(nc.sbuf_tensor("ab_" + n, s, F32))
        wq, wk = sb("wq", [HD, HEADS, D]), sb("wk", [HD, HEADS, LD])
        wv, wo = sb("wv", [HD, HEADS, LD]), sb("wo", [HD, HEADS, D])
        q_ps = c.enter_context(nc.psum_tensor("ab_q", [P, ST], F32))
        v_ps = c.enter_context(nc.psum_tensor("ab_v", [P, ST], F32))
        loaded, q_done, v_done, kept = (sem("ab_" + n) for n in ("ld", "q", "v", "kept"))
        with nc.Block() as block:
            @block.sync
            def _(sp):
                for dst, src in ((wq, w_qT), (wk, w_kT), (wv, w_vT), (wo, w_out)):
                    sp.dma_start(dst[:, :, :], src).then_inc(loaded, 16)
                then_load(sp)

            @block.tensor
            def _(pe):
                pe.wait_ge(loaded, 64)
                for h in range(HEADS):
                    last = nc.tensor.matmul(q_ps[:, h * LD:(h + 1) * LD], wq[:, h, :], wk[:, h, :], start=True, stop=True)
                last.then_inc(q_done, 1)
                for h in range(HEADS):
                    n, r = divmod(h, HPC)
                    last = nc.tensor.matmul(v_ps[r * LD:(r + 1) * LD, n * D:(n + 1) * D], wv[:, h, :], wo[:, h, :],
                                            start=True, stop=True)
                last.then_inc(v_done, 1)

            @block.vector
            def _(dve):
                dve.wait_ge(q_done, 1)
                nc.vector.tensor_copy(a_q[:, :], q_ps[:, :]).then_inc(kept, 1)
                dve.wait_ge(v_done, 1)
                nc.vector.tensor_copy(a_v[:, :, :], v_ps[:, :].rearrange("p (n o) -> p n o", o=D)).then_inc(kept, 1)


def project_1(k, a_q, w_kv, scr_q, scr_k, scr_v, operands):
    nc, sem = k.nc, k.sem
    LD = 32
    NC = HEADS * LD // P
    NT = NC + 1
    with ExitStack() as c:
        sb = lambda n, s, d: c.enter_context(nc.sbuf_tensor("p1_" + n, s, d))
        pb = lambda n: c.enter_context(nc.psum_tensor("p1_" + n, [P, ST], F32))
        wkv = sb("wkv", [P, LD], F32)
        xn = [sb(f"xn{i}", [P, TPS, D], F32) for i in range(2)]
        xnT = [sb(f"xnT{i}", [P, ST], F32) for i in range(2)]
        hi = [sb(f"hi{i}", [P, NT, ST], F32R) for i in range(2)]
        lo = [sb(f"lo{i}", [P, NT, ST], F32R) for i in range(2)]
        v1 = [sb(f"v{i}", [P, TPS, LD + 1], F32) for i in range(2)]
        xT_ps = [pb(f"xT{i}") for i in range(2)]
        t_ps = [pb(f"t{i}") for i in range(NT)]
        v_ps = pb("v")
        loaded, ones, prepared, xn_ready, xT_done, xnT_ready, t_done, v_done, hi_ready, lo_ready, v_ready = (
            sem("p1_" + n) for n in ("ld", "ones", "prep", "xn", "xT", "xnT", "t", "v", "hi", "lo", "vr"))
        stored = [sem(f"p1_st{i}") for i in range(2)]
        NSTORE = 2 * NT + 1
        rows = [P] * NC + [LD]
        with nc.Block() as block:
            @block.sync
            def _(sp):
                sp.dma_start(wkv[:, :], w_kv).then_inc(loaded, 16)
                for u in rounds(sp, NST // 2):
                    for par in range(2):
                        g = (u, par)
                        cols = slice(par * ST, (par + 1) * ST)
                        for n in range(NT):
                            dst = scr_q[:, :, n * P:(n + 1) * P, :] if n < NC else scr_k
                            sp.wait_ge(lo_ready, lin(g, NT, n + 1))
                            for part, tile in ((0, hi[par]), (1, lo[par])):
                                sp.dma_start(dst[part, bass.ds(u, 1), :, cols].rearrange("b c n -> (b c) n"),
                                             tile[0:rows[n], n, :].bitcast(F32)).then_inc(stored[par], 16)
                        sp.wait_ge(v_ready, lin(g, 1, 1))
                        sp.dma_start(scr_v[bass.ds(u, 1), :, par * TPS:(par + 1) * TPS, :].rearrange("b p t c -> (b p) t c"),
                                     v1[par][:, :, :]).then_inc(stored[par], 16)
                for par in range(2):
                    sp.wait_ge(stored[par], 16 * NSTORE * (NST // 2))

            @block.gpsimd
            def _(pool):
                for i in range(2):
                    nc.gpsimd.memset(v1[i][:, :, :], 1.0).then_inc(ones, 1)
                pool.wait_ge(ones, 2)
                operands.prepare(pool, prepared)

            @block.vector
            def _(dve):
                def front(g):
                    wait_past(dve, xT_done, lin(g, 1, -1))
                    normalise(k, dve, xn[g[1]], g, xn_ready)

                def back(g):
                    u, par = g
                    wait_past(dve, stored[par], u * (16 * NSTORE))
                    for n in range(NT):
                        dve.wait_ge(hi_ready, lin(g, NT, n + 1))
                        nc.vector.tensor_tensor(lo[par][0:rows[n], n, :], t_ps[n][0:rows[n], :],
                                                hi[par][0:rows[n], n, :].bitcast(F32), ALU.subtract).then_inc(lo_ready, 1)

                pipelined(dve, NST // 2, front, back)

            @block.scalar
            def _(act):
                def front(g):
                    act.wait_ge(xT_done, lin(g, 1, 1))
                    nc.scalar.copy(xnT[g[1]][:, :], xT_ps[g[1]][:, :]).then_inc(xnT_ready, 1)

                def back(g):
                    u, par = g
                    wait_past(act, stored[par], u * (16 * NSTORE))
                    for n in range(NT):
                        act.wait_ge(t_done, lin(g, NT, n + 1))
                        nc.scalar.copy(hi[par][0:rows[n], n, :], t_ps[n][0:rows[n], :]).then_inc(hi_ready, 1)
                    act.wait_ge(v_done, lin(g, 1, 1))
                    nc.scalar.copy(v1[par][:, :, 0:LD], v_ps[:, 0:TPS * LD].rearrange("p (t c) -> p t c", t=TPS))\
                        .then_inc(v_ready, 1)

                act.wait_ge(ones, 2)
                pipelined(act, NST // 2, front, back)

            @block.tensor
            def _(pe):
                def front(g):
                    par = g[1]
                    pe.wait_ge(xn_ready, lin(g, 1, 1))
                    for t in range(TPS):
                        last = nc.tensor.transpose(xT_ps[par][:, t * P:(t + 1) * P], xn[par][:, t, :], k.ident[:, :])
                    last.then_inc(xT_done, 1)

                def back(g):
                    par = g[1]
                    pe.wait_ge(xnT_ready, lin(g, 1, 1))
                    for n in range(NT):
                        wait_past(pe, lo_ready, lin(g, NT, n + 1 - NT))
                        w = a_q[:, n * P:(n + 1) * P] if n < NC else wkv[:, :]
                        nc.tensor.matmul(t_ps[n][0:rows[n], :], w, xnT[par][:, :], start=True, stop=True).then_inc(t_done, 1)
                    wait_past(pe, v_ready, lin(g, 1, 0))
                    for t in range(TPS):
                        last = nc.tensor.matmul(v_ps[:, t * LD:(t + 1) * LD], xnT[par][:, t * P:(t + 1) * P], wkv[:, :],
                                                start=True, stop=True)
                    last.then_inc(v_done, 1)

                pe.wait_ge(loaded, 16)
                pipelined(pe, NST // 2, front, back)


def moe_1(k, wg, wu, wd, xh, xl, gateT, sel, out):
    nc, sem = k.nc, k.sem
    E = 16
    NE = E + 1
    LAG, HBUF = 2, 4
    with ExitStack() as c:
        sb = lambda n, s, d: c.enter_context(nc.sbuf_tensor("m1_" + n, s, d))
        pb = lambda n: c.enter_context(nc.psum_tensor("m1_" + n, [P, ST], F32))
        act_g = [sb(f"s{i}", [P, ST], F32) for i in range(2)]
        gb = [sb(f"gb{i}", [P, ST], F32) for i in range(2)]
        ones = sb("one", [P, ST], F32)
        prod = [sb(f"pr{i}", [P, ST], F32) for i in range(2)]
        h = [sb(f"h{i}", [P, ST], F32) for i in range(2)]
        hh = [sb(f"hh{i}", [P, ST], F32R) for i in range(HBUF)]
        hl = [sb(f"hl{i}", [P, ST], F32R) for i in range(HBUF)]
        y = [sb(f"y{i}", [P, ST], F32) for i in range(2)]
        g_ps = [pb(f"g{i}") for i in range(2)]
        u_ps = [pb(f"u{i}") for i in range(2)]
        y_ps = [pb(f"yp{i}") for i in range(2)]
        b_ps, t_ps = pb("b"), pb("t")
        g_done, u_done, gb_done, gb_ready, silu_ready, prod_ready, h_ready, hh_ready, hl_ready, one_set = (
            sem("m1_" + n) for n in ("g", "u", "gd", "gb", "si", "pr", "h", "hh", "hl", "one"))
        down_done, y_kept, turned, added, stored = (sem("m1_" + n) for n in ("yd", "yk", "tr", "add", "st"))
        KEEP_AT, TURN_AT, ADD_AT = LAG + 1, LAG + 2, LAG + 3

        def two(g, e):
            return (g[1] * NE + e) % 2

        def ring(g, e):
            n = g[1] * NE + e
            return 3 if n == 2 * NE - 1 else n % 3

        def before(g):
            return (g[0] + (g[1] - 1) // 2, (g[1] - 1) % 2)

        def first(g):
            return isinstance(g[0], int) and g == (0, 0)

        def steps(eng, supertile, tail):
            for u in rounds(eng, NST // 2):
                for par in range(2):
                    supertile((u, par))
            tail((NST // 2 - 1, 1))

        with nc.Block() as block:
            @block.sync
            def _(sp):
                out_t = out.rearrange("(t p) d -> p t d", p=P)
                with sp.Fori(0, NST) as s:
                    sp.wait_ge(added, s + 1)
                    rows = bass.ds(s * TPS, TPS)
                    sp.dma_start(out_t[:, rows, :], k.x[:, rows, :]).then_inc(stored, 16)
                sp.wait_ge(stored, 16 * NST)

            @block.tensor
            def _(pe):
                def product(bank, w, e, hi, lo, start, stop):
                    nc.tensor.matmul(bank, w[0][:, e, :], hi, start=start, stop=False)
                    nc.tensor.matmul(bank, w[0][:, e, :], lo, start=False, stop=False)
                    return nc.tensor.matmul(bank, w[1][:, e, :], hi, start=False, stop=stop)

                def gate_up(g, e):
                    cols = bass.ds(lin(g, ST, 0), ST)
                    hi, lo = xh[:, cols], xl[:, cols]
                    wait_past(pe, silu_ready, lin(g, NE, e - 1))
                    product(g_ps[two(g, e)][:, :], wg, e, hi, lo, True, True).then_inc(g_done, 1)
                    wait_past(pe, prod_ready, lin(g, NE, e - 1))
                    if e < E:
                        wait_past(pe, gb_ready, lin(g, E, e))
                    product(u_ps[two(g, e)][:, :], wu, e, hi, lo, True, True).then_inc(u_done, 1)
                    if e < E:
                        nc.tensor.matmul(b_ps[:, :], sel[:, e:e + 1].broadcast_to([2 * E, P]), gateT[:, cols],
                                         start=True, stop=True).then_inc(gb_done, 1)

                def down(g, e):
                    pe.wait_ge(hl_ready, lin(g, NE, e + 1))
                    if e == 0:
                        wait_past(pe, y_kept, lin(g, 1, -1))
                    product(y_ps[g[1]][:, :], wd, e, hh[ring(g, e)][:, :], hl[ring(g, e)][:, :], e == 0, e == NE - 1)\
                        .then_inc(down_done, 1)

                def turn(g):
                    pe.wait_ge(y_kept, lin(g, 1, 1))
                    wait_past(pe, added, lin(g, 1, 0))
                    for t in range(TPS):
                        last = nc.tensor.transpose(t_ps[:, t * P:(t + 1) * P], y[g[1]][:, t * P:(t + 1) * P], k.ident[:, :])
                    last.then_inc(turned, 1)

                def supertile(g):
                    for e in range(NE):
                        gate_up(g, e)
                        if e >= LAG:
                            down(g, e - LAG)
                        elif not first(g):
                            down(before(g), NE - LAG + e)
                        if e == TURN_AT and not first(g):
                            turn(before(g))

                def tail(g):
                    for e in range(NE - LAG, NE):
                        down(g, e)
                    turn(g)

                steps(pe, supertile, tail)

            @block.scalar
            def _(act):
                def round_h(g, e):
                    act.wait_ge(h_ready, lin(g, NE, e + 1))
                    wait_past(act, down_done, lin(g, NE, e - 2))
                    nc.scalar.copy(hh[ring(g, e)][:, :], h[two(g, e)][:, :]).then_inc(hh_ready, 1)

                def keep(g):
                    act.wait_ge(down_done, lin(g, NE, NE))
                    wait_past(act, turned, lin(g, 1, -1))
                    nc.scalar.copy(y[g[1]][:, :], y_ps[g[1]][:, :]).then_inc(y_kept, 1)

                def supertile(g):
                    for e in range(NE):
                        act.wait_ge(g_done, lin(g, NE, e + 1))
                        wait_past(act, prod_ready, lin(g, NE, e - 1))
                        nc.scalar.activation(act_g[two(g, e)][:, :], g_ps[two(g, e)][:, :], ACT.Silu).then_inc(silu_ready, 1)
                        if e < E:
                            act.wait_ge(gb_done, lin(g, E, e + 1))
                            wait_past(act, h_ready, lin(g, NE, e - 1))
                            nc.scalar.copy(gb[e % 2][:, :], b_ps[:, :]).then_inc(gb_ready, 1)
                        if e:
                            round_h(g, e - 1)
                        elif not first(g):
                            round_h(before(g), NE - 1)
                        if e == KEEP_AT and not first(g):
                            keep(before(g))

                def tail(g):
                    round_h(g, NE - 1)
                    keep(g)

                steps(act, supertile, tail)

            @block.gpsimd
            def _(pool):
                nc.gpsimd.memset(ones[:, :], 1.0).then_inc(one_set, 1)
                pool.wait_ge(one_set, 1)

                def supertile(g):
                    for e in range(NE):
                        pool.wait_ge(prod_ready, lin(g, NE, e + 1))
                        if e < E:
                            pool.wait_ge(gb_ready, lin(g, E, e + 1))
                        wait_past(pool, hl_ready, lin(g, NE, e - 1))
                        gate = gb[e % 2] if e < E else ones
                        nc.gpsimd.tensor_tensor(h[two(g, e)][:, :], prod[two(g, e)][:, :], gate[:, :], ALU.mult).then_inc(h_ready, 1)

                steps(pool, supertile, lambda g: None)

            @block.vector
            def _(dve):
                def rest(g, e):
                    dve.wait_ge(hh_ready, lin(g, NE, e + 1))
                    nc.vector.tensor_tensor(hl[ring(g, e)][:, :], h[two(g, e)][:, :], hh[ring(g, e)][:, :].bitcast(F32),
                                            ALU.subtract).then_inc(hl_ready, 1)

                def add(g):
                    dve.wait_ge(turned, lin(g, 1, 1))
                    rows = k.x[:, bass.ds(lin(g, TPS, 0), TPS), :]
                    nc.vector.tensor_tensor(rows, t_ps[:, :].rearrange("p (t d) -> p t d", t=TPS), rows, ALU.add)\
                        .then_inc(added, 1)

                def supertile(g):
                    for e in range(NE):
                        dve.wait_ge(silu_ready, lin(g, NE, e + 1))
                        dve.wait_ge(u_done, lin(g, NE, e + 1))
                        wait_past(dve, h_ready, lin(g, NE, e - 1))
                        nc.vector.tensor_tensor(prod[two(g, e)][:, :], u_ps[two(g, e)][:, :], act_g[two(g, e)][:, :], ALU.mult)\
                            .then_inc(prod_ready, 1)
                        if e:
                            rest(g, e - 1)
                        elif not first(g):
                            rest(before(g), NE - 1)
                        if e == ADD_AT and not first(g):
                            add(before(g))

                def tail(g):
                    rest(g, NE - 1)
                    add(g)

                steps(dve, supertile, tail)


def constants(k, sel0, sel1):
    nc, sem = k.nc, k.sem
    made, cast = sem("c_made"), sem("c_cast")
    with ExitStack() as c:
        raw = [c.enter_context(nc.sbuf_tensor(f"c_sel{n}", s.shape, F32)) for n, s in enumerate((sel0, sel1))]
        with nc.Block() as block:
            @block.gpsimd
            def _(pool):
                n = 0
                for t in (k.ident, k.mask_q):
                    nc.gpsimd.memset(t[:, :], 0.0).then_inc(made, 1)
                for t in raw:
                    nc.gpsimd.memset(t[:, :], 0.0).then_inc(made, 1)
                n = 4
                pool.wait_ge(made, n)
                nc.gpsimd.affine_select(out=k.ident[:, :], in_=k.ident[:, :], compare_op=ALU.not_equal, fill=1.0, base=0,
                                        pattern=[[-1, P]], channel_multiplier=1).then_inc(made, 1)
                nc.gpsimd.affine_select(out=k.mask_q[:, SEQ - P:SEQ], in_=k.mask_q[:, SEQ - P:SEQ], compare_op=ALU.is_ge, fill=MASKED, base=0,
                                        pattern=[[-1, P]], channel_multiplier=1).then_inc(made, 1)
                n += 2
                for t in raw:
                    E = t.shape[1]
                    for part in range(2):
                        pool.wait_ge(made, n)
                        nc.gpsimd.affine_select(out=t[:, :], in_=t[:, :], compare_op=ALU.not_equal, fill=1.0, base=-part * E,
                                                pattern=[[-1, E]], channel_multiplier=1).then_inc(made, 1)
                        n += 1

            @block.vector
            def _(dve):
                dve.wait_ge(made, 10)
                for t, s in zip(raw, (sel0, sel1)):
                    nc.vector.tensor_copy(s[:, :], t[:, :]).then_inc(cast, 1)


def transformer(nc, a, out):
    scr = lambda n, s: nc.dram_tensor(n, s, F32, kind="Internal").ap()
    q0, k0 = (scr(n, [2, BATCH, P, SEQ]) for n in ("scr_q0", "scr_k0"))
    v0 = scr("scr_v0", [BATCH, 4, P, TPB, 36])
    q1, k1 = scr("scr_q1", [2, BATCH, 512, SEQ]), scr("scr_k1", [2, BATCH, 32, SEQ])
    v1 = scr("scr_v1", [BATCH, P, TPB, 33])

    def split_rows(scr, HG, R, parts):
        def load(sp, tile, g, s):
            for n, part in enumerate(parts):
                src = scr[part].rearrange("b c n -> (b c) n")[bass.ds(lin(g, HG * R, 0), HG * R), :]
                sp.dma_start(tile[n * R:(n + 1) * R, :, :].bitcast(F32), src.rearrange("(h r) n -> r h n", h=HG)).then_inc(s, 16)
        return load

    def load_v0(sp, tile, g, s):
        src = v0.rearrange("b g p t c -> (b g) p t c")[bass.ds(lin(g, 1, 0), 1), :, :, :]
        sp.dma_start(tile[:, :, :, :].rearrange("p t h c -> p t (h c)"), src.rearrange("g p t c -> (g p) t c")).then_inc(s, 16)

    def batch_of(g):
        return g[0] // 4

    def load_k1(sp, tile, g, s):
        for n, part in enumerate((0, 1, 0)):
            src = k1[part, bass.ds(batch_of(g), 1), :, :].rearrange("b c n -> (b c) n")
            sp.dma_start(tile[n * 32:(n + 1) * 32, 0, :].bitcast(F32), src).then_inc(s, 16)

    def load_v1(sp, tile, g, s):
        src = v1[bass.ds(batch_of(g), 1), :, :, :].rearrange("b p t c -> (b p) t c")
        sp.dma_start(tile[:, :, 0, :], src).then_inc(s, 16)

    with ExitStack() as ctx:
        k = Shared(nc, ctx)
        sb = lambda c, n, s, d=F32: c.enter_context(nc.sbuf_tensor(n, s, d))
        sel0, sel1 = sb(ctx, "sel0", [16, 8], F32R), sb(ctx, "sel1", [32, 16], F32R)
        constants(k, sel0, sel1)

        a_q, a_v, w_o = sb(ctx, "a_q", [P, 512]), sb(ctx, "a_v", [P, 4, D]), sb(ctx, "w_o", [P, 1, D])
        x_loaded, w_o_loaded = k.sem("x_ld"), k.sem("w_o_ld")

        def load_x(sp):
            xt = a["L0_attn_x"].rearrange("(t p) d -> p t d", p=P)
            for half in range(2):
                rows = slice(half * TILES // 2, (half + 1) * TILES // 2)
                sp.dma_start(k.x[:, rows, :], xt[:, rows, :]).then_inc(x_loaded, 16)
            sp.dma_start(w_o[:, 0, :], a["L0_attn_output_proj"]).then_inc(w_o_loaded, 16)

        absorb(k, a["L1_attn_Wq"], a["L1_attn_Wk_up"], a["L1_attn_Wv_up"], a["L1_attn_Wout"], a_q, a_v, load_x)

        ln_stats(k, "ln0", x_loaded)
        with ExitStack() as c:
            attn = sb(c, "attn0", [P, 16, TPB, 32])
            with ExitStack() as c1:
                rows = Operands(nc, c1, "a0", 4, 8, False)
                project_0(k, a["L0_attn_q_heads"], a["L0_attn_k_heads"], a["L0_attn_v_heads"], q0, k0, v0, rows)
                attention(k, "a0", 4, 8, 8.0 ** -0.5, rows, split_rows(q0, 4, 8, (0, 0, 1)), split_rows(k0, 4, 8, (0, 1, 0)),
                          load_v0, attn)
            project_out(k, "o0", attn, w_o, 4, w_o_loaded)
        with ExitStack() as c:
            xh, xl = sb(c, "xh0", [P, TOK], F32R), sb(c, "xl0", [P, TOK], F32R)
            gateT = sb(c, "gateT0", [16, TOK], F32R)
            wf = [sb(c, f"wf{i}", [P, 9, 512], F32R) for i in range(2)]
            wp = [sb(c, f"wp{i}", [P, 9, 4, D], F32R) for i in range(2)]
            with ExitStack() as c1:
                raw = sb(c1, "wf_raw", [P, 9, 512]), sb(c1, "wp_raw", [P, 9, 4, D])
                parts = [[t[:, e:e + 3] for t in (r, *w)] for r, w in zip(raw, (wf, wp)) for e in range(0, 9, 3)]
                sources = [w[:, e:e + 3] for w in (a["Wfc"], a["Wproj"]) for e in range(0, 9, 3)]
                w_loaded = load_ahead(k, "w0_ld", [x[0] for x in parts], sources)
                ln_stats(k, "ln1")
                route(k, "r0", 8, 2, a["L0_ffn_Wr"], None, xh, xl, gateT, parts, w_loaded)
            moe_0(k, a["bfc"], a["L0_ffn_bproj"], a["L0_ffn_bproj_s"], wf, wp, xh, xl, gateT, sel0)
        ln_stats(k, "ln2")
        with ExitStack() as c:
            attn = sb(c, "attn1", [P, 32, TPB, 64])
            with ExitStack() as c1:
                rows = Operands(nc, c1, "a1", 2, 32, True)
                project_1(k, a_q, a["L1_attn_Wkv_down"], q1, k1, v1, rows)
                attention(k, "a1", 2, 32, 64.0 ** -0.5, rows, split_rows(q1, 2, 32, (0, 0, 1)), load_k1, load_v1, attn)
            project_out(k, "o1", attn, a_v, 8)
        with ExitStack() as c:
            xh, xl = sb(c, "xh1", [P, TOK], F32R), sb(c, "xl1", [P, TOK], F32R)
            gateT = sb(c, "gateT1", [32, TOK], F32R)
            w = [[sb(c, f"w{n}{i}", [P, 17, P], F32R) for i in range(2)] for n in "gud"]
            with ExitStack() as c1:
                raw = [sb(c1, f"w{n}_raw", [P, 17, P]) for n in "gud"]
                parts = [[t[:, :, :] for t in (r, *x)] for r, x in zip(raw, w)]
                w_loaded = load_ahead(k, "w1_ld", [x[0] for x in parts], [a[n] for n in ("w_gate", "w_up", "w_down")])
                ln_stats(k, "ln3")
                route(k, "r1", 16, 8, a["L1_ffn_gate_w"], a["L1_ffn_expert_bias"], xh, xl, gateT, parts, w_loaded)
            moe_1(k, *w, xh, xl, gateT, sel1, out)


def load_ahead(k, name, tiles, sources):
    loaded = k.sem(name)
    with k.nc.Block() as block:
        @block.sync
        def _(sp):
            for tile, source in zip(tiles, sources):
                sp.dma_start(tile, source).then_inc(loaded, 16)
    return loaded


def kernel(**inputs):
    import numpy as np
    import concourse.bacc as bacc
    from concourse.bass_utils import run_bass_kernel_spmd

    t = {n: np.asarray(v) for n, v in inputs.items()}
    arrays = {
        "L0_attn_x": t["L0_attn_x"].reshape(TOK, D),
        "L0_attn_q_heads": t["L0_attn_q_heads"].T, "L0_attn_k_heads": t["L0_attn_k_heads"].T,
        "L0_attn_v_heads": t["L0_attn_v_heads"].T, "L0_attn_output_proj": t["L0_attn_output_proj"].T,
        "L0_ffn_Wr": t["L0_ffn_Wr"],
        "Wfc": np.concatenate([t["L0_ffn_Wfc_s"][None], t["L0_ffn_Wfc"]]).transpose(1, 0, 2),
        "bfc": np.concatenate([t["L0_ffn_bfc_s"][None], t["L0_ffn_bfc"]]).reshape(36, P).T,
        "Wproj": np.concatenate([t["L0_ffn_Wproj_s"][None], t["L0_ffn_Wproj"]]).reshape(9, 4, P, D).transpose(2, 0, 1, 3),
        "L0_ffn_bproj": t["L0_ffn_bproj"], "L0_ffn_bproj_s": t["L0_ffn_bproj_s"].reshape(D, 1),
        "L1_attn_Wq": t["L1_attn_Wq"].transpose(2, 1, 0), "L1_attn_Wkv_down": t["L1_attn_Wkv_down"],
        "L1_attn_Wk_up": t["L1_attn_Wk_up"].transpose(2, 1, 0), "L1_attn_Wv_up": t["L1_attn_Wv_up"].transpose(2, 1, 0),
        "L1_attn_Wout": t["L1_attn_Wout"].transpose(1, 0, 2),
        "L1_ffn_gate_w": t["L1_ffn_gate_w"].T, "L1_ffn_expert_bias": t["L1_ffn_expert_bias"],
        "w_gate": np.concatenate([t["L1_ffn_w_gate"], t["L1_ffn_shared_gate_w"][None]]).transpose(2, 0, 1),
        "w_up": np.concatenate([t["L1_ffn_w_up"], t["L1_ffn_shared_up_w"][None]]).transpose(2, 0, 1),
        "w_down": np.concatenate([t["L1_ffn_w_down"], t["L1_ffn_shared_down_w"][None]]).transpose(2, 0, 1),
    }
    arrays = {n: np.ascontiguousarray(v) for n, v in arrays.items()}
    nc = bacc.Bacc("TRN2", target_bir_lowering=False, num_devices=1)
    aps = {n: nc.dram_tensor(n, v.shape, mybir.dt.from_np(v.dtype), kind="ExternalInput").ap() for n, v in arrays.items()}
    out = nc.dram_tensor("out", [TOK, D], F32, kind="ExternalOutput").ap()
    transformer(nc, aps, out)
    r = run_bass_kernel_spmd(nc, [arrays], core_ids=[0])
    return r.results[0]["out"].reshape(BATCH, SEQ, D)
```
